# Optimizing a Trainium2 kernel written in Bass

```python
import numpy as np
import jax
import jax.numpy as jnp

def _softmax(x, axis=-1):
    return jax.nn.softmax(x, axis=axis)

def _gelu(x):
    return jax.nn.gelu(x, approximate=True)

def _silu(x):
    return jax.nn.silu(x)

def _sigmoid(x):
    return jax.nn.sigmoid(x)

def _layernorm(x, axis=-1, eps=1e-05):
    m = jnp.mean(x, axis=axis, keepdims=True)
    v = jnp.var(x, axis=axis, keepdims=True)
    return (x - m) / jnp.sqrt(v + eps)

def _scatter_add(tgt, idx, src, axis=0):
    return tgt.at[idx].add(src)

def _segment_sum(src, seg, n):
    return jax.ops.segment_sum(src, seg, n)
kernel_name = 'mk_gnn_resnorm_d4_gnn_r32_f7d85e'

def setup_inputs(seed: int=0):
    np.random.seed(seed)
    _w = jnp.asarray

    def _rec_inputs():
        import jax
        import jax.numpy as jnp
        _gk = jax.random.key(seed)
        x = -0.000202 + 1 * jax.random.normal(jax.random.fold_in(_gk, 1), (3125, 64), jnp.float32)
        _s = jax.random.randint(jax.random.fold_in(_gk, 2), (50000,), 0, 3125, jnp.int32)
        _d = jax.random.randint(jax.random.fold_in(_gk, 3), (50000,), 0, 3125, jnp.int32)
        _loop = jnp.arange(3125, dtype=jnp.int32)
        src = jnp.concatenate([_s, _d, _loop])
        dst = jnp.concatenate([_d, _s, _loop])
        _o = jnp.argsort(dst, stable=True)
        src = src[_o]
        dst = dst[_o]
        edge_attr_32 = 0.000189758 + 1.00013 * jax.random.normal(jax.random.fold_in(_gk, 12), (103125, 32), jnp.float32)
        edge_weight = jax.random.uniform(jax.random.fold_in(_gk, 14), (103125,), jnp.float32, 0.0, 0.999998)
        return (x, src, dst, edge_attr_32, edge_weight)
    x, src, dst, edge_attr_32, edge_weight = _rec_inputs()

    def _L0_gnn_setup():
        import jax, jax.numpy as jnp
        import numpy as np
        N_NODES = 3125
        N_EDGES = 50000
        DIM = 64
        key = jax.random.key(seed)
        k1, k2, k3, k4 = jax.random.split(key, 4)
        x = jax.random.normal(k1, (N_NODES, DIM), dtype=jnp.float32)
        edge_index = jax.random.randint(k2, (2, N_EDGES), 0, N_NODES, dtype=jnp.int64)
        W1 = jax.random.normal(k3, (DIM, DIM), dtype=jnp.float32) * 0.05
        b1 = jnp.zeros((DIM,), dtype=jnp.float32)
        W2 = jax.random.normal(k4, (DIM, DIM), dtype=jnp.float32) * 0.05
        b2 = jnp.zeros((DIM,), dtype=jnp.float32)
        return {'x': x, 'edge_index': edge_index, 'W1': W1, 'b1': b1, 'W2': W2, 'b2': b2}
    _L0_gnn_all = _L0_gnn_setup()
    _L0_gnn_in = {k: v for k, v in _L0_gnn_all.items() if k in ('W1', 'b1', 'W2', 'b2')}
    del _L0_gnn_all

    def _L1_gnn_setup():
        import jax, jax.numpy as jnp
        import numpy as np
        N = 3125
        D = 64
        E = 1250000
        H = D * D

        def _gru_cell(x, h, w_ih, w_hh, b_ih, b_hh):
            gi = w_ih @ x + b_ih
            gh = w_hh @ h + b_hh
            i_r, i_z, i_n = jnp.split(gi, 3)
            h_r, h_z, h_n = jnp.split(gh, 3)
            r = jax.nn.sigmoid(i_r + h_r)
            z = jax.nn.sigmoid(i_z + h_z)
            n = jnp.tanh(i_n + r * h_n)
            return (1.0 - z) * n + z * h
        key = jax.random.key(seed)
        ks = jax.random.split(key, 9)
        return {'node_embeddings': jax.random.normal(ks[0], (N, D), jnp.float32), 'gc_weights': jax.random.normal(ks[1], (D, D), jnp.float32) * 0.1, 'prev_weights': jax.random.normal(ks[2], (D, D), jnp.float32) * 0.1, 'w_ih': jax.random.normal(ks[3], (3 * H, H), jnp.float32) * 0.01, 'w_hh': jax.random.normal(ks[4], (3 * H, H), jnp.float32) * 0.01, 'b_ih': jnp.zeros((3 * H,), jnp.float32), 'b_hh': jnp.zeros((3 * H,), jnp.float32), 'src': jax.random.randint(ks[5], (E,), 0, N), 'dst': jax.random.randint(ks[6], (E,), 0, N)}
    _L1_gnn_all = _L1_gnn_setup()
    _L1_gnn_in = {k: v for k, v in _L1_gnn_all.items() if k in ('gc_weights', 'prev_weights', 'w_ih', 'w_hh', 'b_ih', 'b_hh')}
    del _L1_gnn_all

    def _L2_gnn_setup():
        import jax, jax.numpy as jnp
        import numpy as np
        N_NODES = 50000
        N_EDGES = 31250
        C_FEAT = 64
        key = jax.random.key(seed)
        k1, k2, k3 = jax.random.split(key, 3)
        x = jax.random.normal(k1, (N_NODES, C_FEAT), dtype=jnp.float32)
        g = jax.random.randint(k2, (2, N_EDGES), 0, N_NODES, dtype=jnp.int64)
        ew = jax.random.uniform(k3, (N_EDGES,), dtype=jnp.float32)
        return {'x': x, 'g': g, 'ew': ew}
    _L2_gnn_all = _L2_gnn_setup()
    _L2_gnn_in = {k: v for k, v in _L2_gnn_all.items() if k in ()}
    del _L2_gnn_all

    def _L3_gnn_setup():
        import jax, jax.numpy as jnp
        import numpy as np
        N, E, D, ED = (3125, 50000, 64, 32)
        LN_EPS = 1e-05
        NEG_SLOPE = 0.2
        key = jax.random.key(seed)
        ks = jax.random.split(key, 12)
        return {'x': jax.random.normal(ks[0], (N, D), jnp.float32), 'edge_index': jax.random.randint(ks[1], (2, E), 0, N, dtype=jnp.int64), 'edge_attr': jax.random.normal(ks[2], (E, ED), jnp.float32), 'We': jax.random.normal(ks[3], (ED, D), jnp.float32) / np.sqrt(ED), 'be': jnp.zeros((D,), jnp.float32), 'W1': jax.random.normal(ks[4], (D, D), jnp.float32) / np.sqrt(D), 'b1': jnp.zeros((D,), jnp.float32), 'W2': jax.random.normal(ks[5], (D, D), jnp.float32) / np.sqrt(D), 'b2': jnp.zeros((D,), jnp.float32), 'eps_gin': jnp.zeros((), jnp.float32), 'gamma': jnp.ones((D,), jnp.float32), 'beta': jnp.zeros((D,), jnp.float32)}
    _L3_gnn_all = _L3_gnn_setup()
    _L3_gnn_in = {k: v for k, v in _L3_gnn_all.items() if k in ('We', 'be', 'W1', 'b1', 'W2', 'b2', 'eps_gin', 'gamma', 'beta')}
    del _L3_gnn_all
    return {'x': x, 'src': src, 'dst': dst, 'edge_attr_32': edge_attr_32, 'edge_weight': edge_weight, 'L0_gnn_W1': _L0_gnn_in['W1'], 'L0_gnn_b1': _L0_gnn_in['b1'], 'L0_gnn_W2': _L0_gnn_in['W2'], 'L0_gnn_b2': _L0_gnn_in['b2'], 'L1_gnn_gc_weights': _L1_gnn_in['gc_weights'], 'L1_gnn_prev_weights': _L1_gnn_in['prev_weights'], 'L1_gnn_w_ih': _L1_gnn_in['w_ih'], 'L1_gnn_w_hh': _L1_gnn_in['w_hh'], 'L1_gnn_b_ih': _L1_gnn_in['b_ih'], 'L1_gnn_b_hh': _L1_gnn_in['b_hh'], 'L3_gnn_We': _L3_gnn_in['We'], 'L3_gnn_be': _L3_gnn_in['be'], 'L3_gnn_W1': _L3_gnn_in['W1'], 'L3_gnn_b1': _L3_gnn_in['b1'], 'L3_gnn_W2': _L3_gnn_in['W2'], 'L3_gnn_b2': _L3_gnn_in['b2'], 'L3_gnn_eps_gin': _L3_gnn_in['eps_gin'], 'L3_gnn_gamma': _L3_gnn_in['gamma'], 'L3_gnn_beta': _L3_gnn_in['beta']}

def reference(x, src, dst, edge_attr_32, edge_weight, L0_gnn_W1, L0_gnn_b1, L0_gnn_W2, L0_gnn_b2, L1_gnn_gc_weights, L1_gnn_prev_weights, L1_gnn_w_ih, L1_gnn_w_hh, L1_gnn_b_ih, L1_gnn_b_hh, L3_gnn_We, L3_gnn_be, L3_gnn_W1, L3_gnn_b1, L3_gnn_W2, L3_gnn_b2, L3_gnn_eps_gin, L3_gnn_gamma, L3_gnn_beta):
    import jax
    import jax.numpy as jnp

    def _L0_gnn_ref(x, edge_index, W1, b1, W2, b2):
        import jax, jax.numpy as jnp
        import numpy as np
        N_NODES = 3125
        N_EDGES = 50000
        DIM = 64
        src = edge_index[0]
        dst = edge_index[1]
        agg = jax.ops.segment_sum(x[src], dst, num_segments=x.shape[0])
        h = x + agg
        h = jax.nn.relu(h @ W1.T + b1)
        out = h @ W2.T + b2
        return out

    def _L1_gnn_ref(node_embeddings, gc_weights, prev_weights, w_ih, w_hh, b_ih, b_hh, src, dst):
        import jax, jax.numpy as jnp
        import numpy as np
        N = 3125
        D = 64
        E = 1250000
        H = D * D

        def _gru_cell(x, h, w_ih, w_hh, b_ih, b_hh):
            gi = w_ih @ x + b_ih
            gh = w_hh @ h + b_hh
            i_r, i_z, i_n = jnp.split(gi, 3)
            h_r, h_z, h_n = jnp.split(gh, 3)
            r = jax.nn.sigmoid(i_r + h_r)
            z = jax.nn.sigmoid(i_z + h_z)
            n = jnp.tanh(i_n + r * h_n)
            return (1.0 - z) * n + z * h
        d = gc_weights.shape[0]
        n_nodes = node_embeddings.shape[0]
        new_w = _gru_cell(prev_weights.reshape(-1), gc_weights.reshape(-1), w_ih, w_hh, b_ih, b_hh).reshape(d, d)
        h = node_embeddings @ new_w
        msg_sum = jax.ops.segment_sum(h[src], dst, num_segments=n_nodes)
        deg = jax.ops.segment_sum(jnp.ones((src.shape[0],), h.dtype), dst, num_segments=n_nodes)
        return msg_sum / jnp.maximum(deg, 1.0)[:, None]

    def _L2_gnn_ref(x, g, ew):
        import jax, jax.numpy as jnp
        import numpy as np
        N_NODES = 50000
        N_EDGES = 31250
        C_FEAT = 64
        i, j = (g[0], g[1])
        weighted_info = x[i] * ew[:, None]
        aggr_out = jax.ops.segment_sum(weighted_info, j, num_segments=x.shape[0])
        return aggr_out

    def _L3_gnn_ref(x, edge_index, edge_attr, We, be, W1, b1, W2, b2, eps_gin, gamma, beta):
        import jax, jax.numpy as jnp
        import numpy as np
        N, E, D, ED = (3125, 50000, 64, 32)
        LN_EPS = 1e-05
        NEG_SLOPE = 0.2
        src, dst = (edge_index[0], edge_index[1])
        msg = jax.nn.relu(x[src] + edge_attr @ We + be)
        aggr = jax.ops.segment_sum(msg, dst, num_segments=x.shape[0])
        h = (1.0 + eps_gin) * x + aggr
        h = jax.nn.relu(h @ W1 + b1) @ W2 + b2
        h = jnp.where(h >= 0, h, NEG_SLOPE * h)
        mu = jnp.mean(h, axis=-1, keepdims=True)
        var = jnp.mean((h - mu) ** 2, axis=-1, keepdims=True)
        return (h - mu) / jnp.sqrt(var + LN_EPS) * gamma + beta
    edge_index = jnp.stack([src, dst])
    x = _layernorm(x + _L0_gnn_ref(x, edge_index, L0_gnn_W1, L0_gnn_b1, L0_gnn_W2, L0_gnn_b2), axis=-1)
    x = _layernorm(x + _L1_gnn_ref(x, L1_gnn_gc_weights, L1_gnn_prev_weights, L1_gnn_w_ih, L1_gnn_w_hh, L1_gnn_b_ih, L1_gnn_b_hh, src, dst), axis=-1)
    x = _layernorm(x + _L2_gnn_ref(x, edge_index, edge_weight), axis=-1)
    x = _layernorm(x + _L3_gnn_ref(x, edge_index, edge_attr_32, L3_gnn_We, L3_gnn_be, L3_gnn_W1, L3_gnn_b1, L3_gnn_W2, L3_gnn_b2, L3_gnn_eps_gin, L3_gnn_gamma, L3_gnn_beta), axis=-1)
    return x

_drawn_inputs = setup_inputs


def setup_inputs(seed=0):
    import zlib

    import numpy as np

    out = dict(_drawn_inputs(seed))
    spreads = {'L0_gnn_b1': (0.0, 0.1),
     'L0_gnn_b2': (0.0, 0.1),
     'L1_gnn_b_ih': (0.0, 0.1),
     'L1_gnn_b_hh': (0.0, 0.1),
     'L3_gnn_be': (0.0, 0.1),
     'L3_gnn_b1': (0.0, 2.0),
     'L3_gnn_b2': (0.0, 0.8),
     'L3_gnn_gamma': (1.0, 0.2),
     'L3_gnn_beta': (0.0, 0.1)}
    factors = {}
    for name, (base, spread) in spreads.items():
        noise = np.random.default_rng([zlib.crc32(name.encode()), seed]).standard_normal(out[name].shape)
        drawn = base * np.exp(spread * noise) if base else spread * noise
        out[name] = jnp.asarray(drawn.astype(out[name].dtype))
    for name, factor in factors.items():
        out[name] = (out[name] * factor).astype(out[name].dtype)
    return out
```

```python
import numpy as np
import concourse.bass as bass
from concourse import mybir
from contextlib import ExitStack

fp32 = mybir.dt.float32
bf16 = mybir.dt.bfloat16
fp16 = mybir.dt.float16
i32 = mybir.dt.int32
ALU = mybir.AluOpType
ACT = mybir.ActivationFunctionType
AX = mybir.AxisListType

P = 128
N = 3125
D = 64
ED = 32
E = 103125
NB = 25
BN = N // NB
G = 24
NG = -(-E // (P * G))
COLS = NG * G
TAIL = E - (NG - 1) * P * G
TP, TR = TAIL // G, TAIL % G
H = D * D
TILES = 3 * H // P
GT = H // P
RING = 4
MID = (N - 1) // 2
LN_EPS = 1e-5
SLOPE = 0.2
HALVES = ((0, 4), (4, G // 4))
NT = 500


class Step:

    def __init__(self, engine, sem):
        self.engine, self.sem, self.n = engine, sem, 0

    def link(self, ins):
        self.n += 1
        ins.then_inc(self.sem, 1)
        self.engine.wait_ge(self.sem, self.n)


def gnn_kernel(nc, x, src, dst, edge_attr_32, edge_weight, L0_gnn_W1, L0_gnn_b1, L0_gnn_W2, L0_gnn_b2,
               L1_gnn_gc_weights, L1_gnn_prev_weights, L1_gnn_w_ih, L1_gnn_w_hh, L1_gnn_b_ih, L1_gnn_b_hh,
               L3_gnn_We, L3_gnn_be, L3_gnn_W1, L3_gnn_b1, L3_gnn_W2, L3_gnn_b2, L3_gnn_eps_gin,
               L3_gnn_gamma, L3_gnn_beta, out):
    ctx = ExitStack()
    with ctx:
        def sb(name, shape, dt=fp32):
            return ctx.enter_context(nc.sbuf_tensor(name, shape, dt))

        def sem(name):
            return ctx.enter_context(nc.semaphore(name))

        def row(v):
            return v.rearrange("(a n) -> a n", a=1)

        tables = [nc.dram_tensor(f"node_table{k}", (N, D), fp32).ap() for k in range(3)]

        w_tile = [sb(f"w_tile{k}", [P, H]) for k in range(RING)]
        vec = [sb(f"cell_vec{k}", [P, H]) for k in range(2)]
        junk = [sb(f"junk{k}", [P, H], bf16) for k in range(2)]
        acc = sb("acc", [P, RING])
        gates = sb("gates", [P, 2 * TILES])
        src_i = sb("src_i", [P, NG, G], i32)
        dst_i = sb("dst_i", [P, NG, G], i32)
        dst_f = sb("dst_f", [P, COLS])
        wgt = sb("wgt", [P, NG, G])
        node_no = sb("node_no", [P, N], fp16)
        ident = sb("ident", [P, P])
        idx = [sb(f"idx{k}", [P, G], i32) for k in range(2)]
        gat = [sb(f"gat{k}", [P, G, D]) for k in range(2)]
        part = sb("part", [P, 2 * G, 3, D], bf16)
        hot = [sb(f"hot{k}", [P, N], bf16) for k in range(2)]
        ones = sb("ones", [P, 1], bf16)
        zeros = sb("zeros", [P, 512], bf16)
        ea = [sb(f"ea{k}", [P, G * ED]) for k in range(2)]
        eaT = sb("eaT", [P, G // 4, P])
        we4 = sb("we4", [P, 4, D])
        X = sb("X", [BN, NB, D])
        stat = sb("stat", [BN, 4, NB])
        rdeg = sb("rdeg", [BN, NB])
        hT = w_tile[0][0:D, 0:N]
        rT = w_tile[1][0:D + 1, 0:N]
        hb = w_tile[2][0:BN, 0:NB * D].rearrange("p (b f) -> p b f", f=D)
        sq = w_tile[3][0:BN, 0:NB * D].rearrange("p (b f) -> p b f", f=D)
        w_in = sb("w_in", [D, 2, D])
        w1T = sb("w1T", [D, D])
        w2T = sb("w2T", [D + 1, D])
        w1c = sb("w1c", [D, D])
        w2c = sb("w2c", [D + 1, D])
        b1 = sb("b1", [D, 2])
        be_b = sb("be_b", [P, D])
        gam_b = sb("gam_b", [P, D])
        bet_b = sb("bet_b", [P, D])
        eps_b = sb("eps_b", [P, 1])
        bias_g = sb("bias_g", [GT, 2, 3, P])
        gc_g = sb("gc_g", [GT, P])
        cell = sb("cell", [GT, 6, P])
        newRT = sb("newRT", [GT, P])
        spread = sb("spread", [GT, 2, GT, 2])
        new_w = sb("new_w", [D, D])

        agg_ps = ctx.enter_context(nc.psum_tensor("agg_ps", [P, 2048], fp32))
        work_ps = ctx.enter_context(nc.psum_tensor("work_ps", [P, 2048], fp32))
        agg = agg_ps[0:BN, 0:NB * D].rearrange("p (b f) -> p b f", f=D)
        deg = agg_ps[0:BN, NB * D:NB * D + NB]

        s_edges = sem("edges_loaded")
        s_pads = sem("pads_set")
        s_small = sem("weights_loaded")
        s_x = sem("x_loaded")
        s_vec = sem("cell_vectors_loaded")
        s_w = [sem(f"w_tile_loaded{k}") for k in range(RING)]
        s_wused = sem("w_tile_used")
        s_acc = sem("acc_copied")
        s_iota = sem("pool_constants")
        s_dve = sem("dve_steps")
        s_act = sem("act_steps")
        s_const = sem("dve_constants")
        s_idx = sem("idx_ready")
        s_gat = [sem(f"gathered{k}") for k in range(2)]
        s_gfree = sem("gat_free")
        s_part = sem("part_ready")
        s_pfree = sem("part_free")
        s_hot = sem("hot_ready")
        s_hfree = sem("hot_free")
        s_ea = [sem(f"ea_loaded{k}") for k in range(2)]
        s_eafree = sem("ea_free")
        s_tail = sem("ea_tail_row_loaded")
        s_tp = sem("eaT_transposed")
        s_eaT = sem("eaT_ready")
        s_eaW = sem("eaW_ready")
        s_eaWfree = sem("eaW_free")
        s_agg = sem("agg_done")
        s_pe = sem("pe_node_steps")
        s_ev = sem("act_node_steps")
        s_h = sem("h_ready")
        s_aggfree = sem("agg_free")
        s_var = sem("variance_ready")
        s_std = sem("std_ready")
        s_xnew = sem("x_new")
        s_tab = sem("table_stored")
        s_res = sem("out_stored")
        s_cell = sem("cell_gates_ready")
        s_cellT = sem("cell_gates_transposed")
        s_ca = sem("cell_act")
        s_cd = sem("cell_dve")
        s_nw = sem("new_w_ready")

        w_rows = [w.rearrange("(t p) k -> t p k", p=P) for w in (L1_gnn_w_ih, L1_gnn_w_hh)]
        ea_rows = edge_attr_32[0:(NG - 1) * P * G, :].rearrange("(g p j) c -> g p (j c)", p=P, j=G)
        N_SMALL = 21

        block = ctx.enter_context(nc.Block())

        @block.sync
        def _(sp):
            for k, v in enumerate((L1_gnn_prev_weights, L1_gnn_gc_weights)):
                sp.dma_start(vec[k][:, :], v.rearrange("a c -> (a c)").partition_broadcast(P)).then_inc(s_vec, 16)
            for k in range(RING):
                sp.dma_start(w_tile[k][:, :], w_rows[0][k]).then_inc(s_w[k], 16)
            sp.dma_start(X[:, :, :], x.rearrange("(b p) f -> p b f", p=BN)).then_inc(s_x, 16)
            sp.wait_ge(s_pads, 3)
            full = (NG - 1) * P * G
            for v, t in ((src, src_i), (dst, dst_i), (edge_weight, wgt)):
                sp.dma_start(t[:, 0:NG - 1, :], v[0:full].rearrange("(g p j) -> p g j", p=P, j=G)).then_inc(s_edges, 16)
                sp.dma_start(t[0:TP, NG - 1, :], v[full:full + TP * G].rearrange("(p j) -> p j", j=G)).then_inc(s_edges, 16)
                sp.dma_start(t[TP:TP + 1, NG - 1, 0:TR], row(v[full + TP * G:E])).then_inc(s_edges, 16)
            n = 0
            small = [
                (w_in[:, 0, :], L0_gnn_W1), (w_in[:, 1, :], L0_gnn_W2), (w2T[D:D + 1, :], row(L0_gnn_b2)),
                (b1[:, 0:1], L0_gnn_b1.rearrange("(n a) -> n a", a=1)),
                (w1c[:, :], L3_gnn_W1), (w2c[0:D, :], L3_gnn_W2), (w2c[D:D + 1, :], row(L3_gnn_b2)),
                (b1[:, 1:2], L3_gnn_b1.rearrange("(n a) -> n a", a=1)),
                (be_b[:, :], L3_gnn_be.partition_broadcast(P)),
                (gam_b[:, :], L3_gnn_gamma.partition_broadcast(P)),
                (bet_b[:, :], L3_gnn_beta.partition_broadcast(P)),
                (eps_b[:, :], L3_gnn_eps_gin.partition_broadcast(P)),
                (bias_g[:, 0, :, :], L1_gnn_b_ih.rearrange("(g t p) -> t g p", t=GT, p=P)),
                (bias_g[:, 1, :, :], L1_gnn_b_hh.rearrange("(g t p) -> t g p", t=GT, p=P)),
                (gc_g[:, :], L1_gnn_gc_weights.rearrange("(t a) c -> t (a c)", a=2)),
            ]
            sp.wait_ge(s_const, 3)
            for k in range(4):
                small.append((we4[ED * k:ED * (k + 1), k, :], L3_gnn_We))
            for to, of in small:
                n += 1
                sp.dma_start(to, of).then_inc(s_small, 16)
            assert n == N_SMALL - 2
            with sp.Fori(0, TILES // RING - 1) as i:
                for k in range(RING):
                    sp.wait_ge(s_wused, RING * i + k + 3)
                    sp.dma_start(w_tile[k][:, :], w_rows[0][RING * i + RING + k]).then_inc(s_w[k], 16)
            with sp.Fori(0, TILES // RING) as i:
                for k in range(RING):
                    sp.wait_ge(s_wused, RING * i + (TILES - RING + k + 3))
                    sp.dma_start(w_tile[k][:, :], w_rows[1][RING * i + k]).then_inc(s_w[k], 16)
            for layer in range(3):
                sp.wait_ge(s_xnew, layer + 1)
                made = hb if layer == 2 else X
                sp.dma_start(tables[layer].rearrange("(b p) f -> p b f", p=BN), made[:, :, :]).then_inc(s_tab, 16)
            with sp.Fori(0, NG // 2 - 1) as i:
                for q in range(2):
                    sp.wait_ge(s_eafree, 2 * i + q + 1)
                    sp.dma_start(ea[q][:, :], ea_rows[2 * i + q]).then_inc(s_ea[q], 16)
            sp.wait_ge(s_eafree, NG - 1)
            sp.dma_start(ea[0][:, :], ea_rows[NG - 2]).then_inc(s_ea[0], 16)
            sp.wait_ge(s_eafree, NG)
            sp.dma_start(ea[1][TP:TP + 1, 0:TR * ED], row(edge_attr_32[full + TP * G:E, :].rearrange("e c -> (e c)"))).then_inc(s_tail, 16)
            sp.wait_ge(s_tail, 16)
            sp.dma_start(ea[1][0:TP, :], edge_attr_32[full:full + TP * G, :].rearrange("(p j) c -> p (j c)", j=G)).then_inc(s_ea[1], 16)
            sp.wait_ge(s_xnew, 4)
            sp.dma_start(out.rearrange("(b p) f -> p b f", p=BN), X[:, :, :]).then_inc(s_res, 16)
            sp.wait_ge(s_res, 16)
            sp.wait_ge(s_tab, 48)

        @block.gpsimd
        def _(pool):
            pool.memset(src_i[:, :, :], 0).then_inc(s_pads, 1)
            pool.memset(dst_i[:, :, :], -N).then_inc(s_pads, 1)
            pool.memset(wgt[:, :, :], 0.0).then_inc(s_pads, 1)
            pool.iota(node_no[:, :], pattern=[[1, N]], base=-MID, channel_multiplier=0, allow_small_or_imprecise_dtypes=True).then_inc(s_iota, 1)
            pool.memset(ident[:, :], 0.0).then_inc(s_iota, 1)
            pool.wait_ge(s_iota, 2)
            pool.affine_select(out=ident[:, :], in_=ident[:, :], compare_op=ALU.not_equal, fill=1.0,
                               base=0, pattern=[[-1, P]], channel_multiplier=1).then_inc(s_iota, 1)
            pool.wait_ge(s_edges, 16 * 9)
            for layer in range(4):
                table = x if layer == 0 else tables[layer - 1]
                if layer:
                    pool.wait_ge(s_tab, 16 * layer)
                first = layer * NG
                with pool.Fori(0, NG // 2) as i:
                    for q in range(2):
                        pool.wait_ge(s_gfree, 2 * i + (first + q + 1))
                        pool.tensor_copy(idx[q][:, :], src_i[:, 2 * i + q, :]).then_inc(s_idx, 1)
                        pool.wait_ge(s_pads, 3)
                        pool.wait_ge(s_idx, 2 * i + (first + q + 1))
                        for j in range(G):
                            pool.indirect_dma_start(
                                out=gat[q][:, j, :], out_offset=None, in_=table,
                                in_offset=bass.IndirectOffsetOnAxis(ap=idx[q][:, j:j + 1], axis=0)).then_inc(s_gat[q], 16)

        @block.vector
        def _(dve):
            st = Step(dve, s_dve)
            dve.memset(ones[:, :], 1.0).then_inc(s_const, 1)
            dve.memset(zeros[:, :], 0.0).then_inc(s_const, 1)
            dve.memset(eaT[:, :, :], 0.0).then_inc(s_eaT, 1)
            dve.sem_inc(s_eaW, 1)
            dve.sem_inc(s_eaWfree, 1)
            dve.memset(we4[:, :, :], 0.0).then_inc(s_const, 1)
            st.link(dve.memset(spread[:, :, :, :], 0.0))
            for q in range(2):
                dve.memset(ea[q][:, :], 0.0).then_inc(s_eafree, 1)
                dve.memset(gat[q][:, :, :], 0.0).then_inc(s_gfree, 1)
                dve.memset(part[:, q * G:(q + 1) * G, :, :], 0.0).then_inc(s_pfree, 1)
                dve.memset(hot[q][:, :], 0.0).then_inc(s_hfree, 1)
            dve.memset(gates[:, :], 0.0).then_inc(s_acc, 1)
            dve.wait_ge(s_iota, 3)
            for k in range(2):
                dve.tensor_copy(spread[:, k, :, k], ident[0:GT, 0:GT]).then_inc(s_const, 1)
            dve.wait_ge(s_edges, 16 * 9)
            st.link(dve.tensor_scalar(dst_f[:, :], dst_i[:, :, :].rearrange("p g j -> p (g j)"), float(MID), None, ALU.subtract))
            dve.wait_ge(s_const, 5)
            for q in range(2):
                dve.memset(junk[q][:, :], 0.0).then_inc(s_wused, 1)

            dve.wait_ge(s_vec, 32)
            for m in range(2):
                with dve.Fori(0, TILES // RING) as i:
                    dve.wait_ge(s_acc, i + (m * (TILES // RING) + 1))
                    for k in range(RING):
                        dve.wait_ge(s_w[k], 16 * i + 16 * (m * (TILES // RING) + 1))
                        dve.wait_ge(s_wused, RING * i + (m * TILES + k + 1))
                        dve.tensor_tensor_reduce(out=junk[k % 2][:, 0:H], in0=w_tile[k][:, :], in1=vec[m][:, :],
                                                 scale=1.0, scalar=0.0, op0=ALU.mult, op1=ALU.add,
                                                 accum_out=acc[:, k:k + 1]).then_inc(s_wused, 1)
                    dve.wait_ge(s_wused, RING * i + (m * TILES + RING + 2))
                    dve.tensor_copy(gates[:, bass.ds(RING * i + m * TILES, RING)], acc[:, :]).then_inc(s_acc, 1)
            dve.wait_ge(s_acc, 2 * TILES // RING + 1)
            dve.memset(rT[D:D + 1, :], 1.0).then_inc(s_const, 1)
            dve.sem_inc(s_cell, 1)
            tg = work_ps[0:GT, 0:6 * P].rearrange("t (m g p) -> t m g p", m=2, g=3)
            dve.wait_ge(s_cellT, 1)
            dve.wait_ge(s_small, 16 * (N_SMALL - 2))
            gi = cell[:, 0:3, :]
            gh = cell[:, 3:6, :]
            st.link(dve.tensor_tensor(gi, tg[:, 0, :, :], bias_g[:, 0, :, :], ALU.add))
            st.link(dve.tensor_tensor(gh, tg[:, 1, :, :], bias_g[:, 1, :, :], ALU.add))
            dve.tensor_tensor(cell[:, 0:2, :], cell[:, 0:2, :], cell[:, 3:5, :], ALU.add).then_inc(s_cd, 1)
            dve.wait_ge(s_ca, 1)
            st.link(dve.tensor_tensor(cell[:, 5, :], cell[:, 0, :], cell[:, 5, :], ALU.mult))
            dve.tensor_tensor(cell[:, 2, :], cell[:, 2, :], cell[:, 5, :], ALU.add).then_inc(s_cd, 1)
            dve.wait_ge(s_ca, 2)
            st.link(dve.tensor_scalar(cell[:, 3, :], cell[:, 1, :], -1.0, 1.0, ALU.mult, ALU.add))
            st.link(dve.tensor_tensor(cell[:, 3, :], cell[:, 3, :], cell[:, 2, :], ALU.mult))
            st.link(dve.tensor_tensor(cell[:, 4, :], cell[:, 1, :], gc_g[:, :], ALU.mult))
            dve.tensor_tensor(newRT[:, :], cell[:, 3, :], cell[:, 4, :], ALU.add).then_inc(s_cd, 1)
            dve.wait_ge(s_nw, 1)
            dve.tensor_copy(new_w[:, :], work_ps[0:D, 0:D]).then_inc(s_cd, 1)
            dve.wait_ge(s_nw, 2)
            dve.tensor_copy(w1T[:, :], work_ps[0:D, D:2 * D]).then_inc(s_cd, 1)
            dve.tensor_copy(w2T[0:D, :], work_ps[0:D, 2 * D:3 * D]).then_inc(s_cd, 1)
            dve.wait_ge(s_x, 16)

            def aggregate(layer):
                first = layer * NG
                with dve.Fori(0, NG // 2) as i:
                    for q in range(2):
                        n0 = st.n
                        dve.wait_ge(s_gat[q], 16 * G * i + 16 * G * (layer * NG // 2 + 1))
                        dve.wait_ge(s_pfree, 2 * i + (first + q + 1))
                        m = gat[q][:, :, :]
                        per = 4 + (layer == 2) + 2 * (layer == 3)

                        def dep(ins, k):
                            ins.then_inc(s_dve, 1)
                            dve.wait_ge(s_dve, 2 * per * i + (n0 + q * per + k))

                        k = 1
                        if layer == 2:
                            wg = wgt[:, 2 * i + q, :].unsqueeze(2).to_broadcast([P, G, D])
                            dep(dve.tensor_tensor(m, m, wg, ALU.mult), k)
                            k += 1
                        if layer == 3:
                            dve.wait_ge(s_eaW, 2 * i + (q + 2))
                            dep(dve.tensor_tensor(m, m, work_ps[:, 0:G * D].rearrange("p (j f) -> p j f", f=D), ALU.add), k)
                            k += 1
                            ins = dve.tensor_scalar(m, m, 0.0, None, ALU.max)
                            dep(ins, k)
                            dve.sem_inc(s_eaWfree, 1)
                            k += 1
                        pt = part[:, q * G:(q + 1) * G, :, :]
                        dep(dve.tensor_copy(pt[:, :, 0, :], m), k)
                        dep(dve.tensor_tensor(m, m, pt[:, :, 0, :], ALU.subtract), k + 1)
                        dep(dve.tensor_copy(pt[:, :, 1, :], m), k + 2)
                        dep(dve.tensor_tensor(m, m, pt[:, :, 1, :], ALU.subtract), k + 3)
                        dve.tensor_copy(pt[:, :, 2, :], m).then_inc(s_part, 1)
                        dve.wait_ge(s_part, 2 * i + (first + q + 1))
                        dve.sem_inc(s_gfree, 1)
                        for j in range(G):
                            dve.wait_ge(s_hfree, 2 * G * i + ((first + q) * G + j + 1))
                            dve.tensor_scalar(hot[j % 2][:, :], node_no[:, :], dst_f[:, bass.ds(2 * G * i + (q * G + j), 1)],
                                              None, ALU.is_equal).then_inc(s_hot, 1)
                st.n += (NG // 2) * 2 * per

            def normalise(y, z):
                normalise.count += 1
                st.link(dve.tensor_reduce(stat[:, 0, :], y, AX.X, ALU.add))
                st.link(dve.tensor_scalar(stat[:, 1, :], stat[:, 0, :], 1.0 / D, None, ALU.mult))
                st.link(dve.tensor_tensor(y, y, stat[:, 1, :].unsqueeze(2).to_broadcast([BN, NB, D]), ALU.subtract))
                st.link(dve.tensor_tensor(sq[:, :, :], y, y, ALU.mult))
                st.link(dve.tensor_reduce(stat[:, 0, :], sq[:, :, :], AX.X, ALU.add))
                dve.tensor_scalar(stat[:, 2, :], stat[:, 0, :], 1.0 / D, LN_EPS, ALU.mult, ALU.add).then_inc(s_var, 1)
                dve.wait_ge(s_std, normalise.count)
                st.link(dve.reciprocal(stat[:, 1, :], stat[:, 3, :]))
                return dve.tensor_tensor(z, y, stat[:, 1, :].unsqueeze(2).to_broadcast([BN, NB, D]), ALU.mult)

            normalise.count = 0
            Xv, hv, sv = X[:, :, :], hb[:, :, :], sq[:, :, :]
            out2 = agg

            aggregate(0)
            dve.wait_ge(s_agg, 1)
            st.link(dve.tensor_scalar(rdeg[:, :], deg, 1.0, None, ALU.max))
            st.link(dve.reciprocal(rdeg[:, :], rdeg[:, :]))
            dve.tensor_tensor(hv, Xv, agg, ALU.add).then_inc(s_h, 1)
            dve.wait_ge(s_pe, 1)
            st.link(dve.tensor_tensor(hv, Xv, out2, ALU.add))
            dve.sem_inc(s_aggfree, 1)
            normalise(hv, Xv).then_inc(s_xnew, 1)
            dve.wait_ge(s_xnew, 1)
            aggregate(1)
            dve.wait_ge(s_agg, 2)
            dve.tensor_copy(hv, agg).then_inc(s_h, 1)
            dve.wait_ge(s_pe, 2)
            st.link(dve.tensor_tensor(hv, out2, rdeg[:, :].unsqueeze(2).to_broadcast([BN, NB, D]), ALU.mult))
            dve.sem_inc(s_aggfree, 1)
            st.link(dve.tensor_tensor(hv, hv, Xv, ALU.add))
            dve.wait_ge(s_tab, 16)
            normalise(hv, Xv).then_inc(s_xnew, 1)
            dve.wait_ge(s_xnew, 2)
            aggregate(2)
            dve.wait_ge(s_agg, 3)
            st.link(dve.tensor_tensor(hv, Xv, agg, ALU.add))
            dve.sem_inc(s_aggfree, 1)
            dve.wait_ge(s_tab, 32)
            st.link(normalise(hv, Xv))
            dve.tensor_tensor(hv, Xv, be_b[0:BN, :].unsqueeze(1).to_broadcast([BN, NB, D]), ALU.add).then_inc(s_xnew, 1)
            aggregate(3)
            dve.wait_ge(s_agg, 4)
            dve.wait_ge(s_tab, 48)
            st.link(dve.tensor_scalar(stat[:, 0, 0:1], eps_b[0:BN, :], 1.0, None, ALU.add))
            dve.scalar_tensor_tensor(hv, Xv, stat[:, 0, 0:1], agg, ALU.mult, ALU.add).then_inc(s_h, 1)
            dve.wait_ge(s_pe, 3)
            st.link(dve.tensor_scalar(sv, out2, SLOPE, None, ALU.mult))
            st.link(dve.tensor_tensor(hv, out2, sv, ALU.max))
            st.link(normalise(hv, hv))
            st.link(dve.tensor_tensor(hv, hv, gam_b[0:BN, :].unsqueeze(1).to_broadcast([BN, NB, D]), ALU.mult))
            st.link(dve.tensor_tensor(hv, hv, bet_b[0:BN, :].unsqueeze(1).to_broadcast([BN, NB, D]), ALU.add))
            st.link(dve.tensor_tensor(hv, hv, Xv, ALU.add))
            normalise(hv, Xv).then_inc(s_xnew, 1)

        @block.scalar
        def _(act):
            act.wait_ge(s_cd, 1)
            act.activation(cell[:, 0:2, :], cell[:, 0:2, :], ACT.Sigmoid).then_inc(s_ca, 1)
            act.wait_ge(s_cd, 2)
            act.activation(cell[:, 2, :], cell[:, 2, :], ACT.Tanh).then_inc(s_ca, 1)

            def copy_hT(layer_no):
                for c in range(N // NT + 1):
                    w = min(NT, N - c * NT)
                    act.wait_ge(s_tp, layer_no * 14 + c + 1)
                    act.activation(hT[:, c * NT:c * NT + w], work_ps[0:D, 512 * (c % 2):512 * (c % 2) + w], ACT.Copy).then_inc(s_ev, 1)

            def relu_rT(layer_no, col):
                for c in range(N // NT + 1):
                    w = min(NT, N - c * NT)
                    act.wait_ge(s_tp, layer_no * 14 + 7 + c + 1)
                    act.activation(rT[0:D, c * NT:c * NT + w], work_ps[0:D, 1024 + 512 * (c % 2):1024 + 512 * (c % 2) + w],
                                   ACT.Relu, bias=b1[:, col:col + 1]).then_inc(s_ev, 1)

            def std(n):
                act.wait_ge(s_var, n)
                act.activation(stat[:, 3, :], stat[:, 2, :], ACT.Sqrt).then_inc(s_std, 1)

            copy_hT(0)
            relu_rT(0, 0)
            std(1)
            copy_hT(1)
            std(2)
            std(3)
            with act.Fori(0, NG) as g:
                act.wait_ge(s_eaW, g + 1)
                for h, (k0, k1) in enumerate(HALVES):
                    act.wait_ge(s_tp, 2 * g + (21 + h + 1))
                    act.activation(eaT[:, k0:k1, :], work_ps[:, 1536:1536 + P * (k1 - k0)].rearrange("p (k e) -> p k e", e=P),
                                   ACT.Copy).then_inc(s_eaT, 1)
            base = 21 + NG * 2
            for c in range(7):
                w = min(NT, N - c * NT)
                act.wait_ge(s_tp, base + c + 1)
                act.activation(hT[:, c * NT:c * NT + w], work_ps[0:D, 512 * (c % 2):512 * (c % 2) + w], ACT.Copy).then_inc(s_ev, 1)
            for c in range(7):
                w = min(NT, N - c * NT)
                act.wait_ge(s_tp, base + 7 + c + 1)
                act.activation(rT[0:D, c * NT:c * NT + w], work_ps[0:D, 1024 + 512 * (c % 2):1024 + 512 * (c % 2) + w],
                               ACT.Relu, bias=b1[:, 1:2]).then_inc(s_ev, 1)
            std(4)
            std(5)

        @block.tensor
        def _(pe):
            pe.wait_ge(s_iota, 3)
            pe.wait_ge(s_const, 5)
            pe.wait_ge(s_cell, 1)
            for k in range(6):
                last = pe.transpose(work_ps[0:GT, k * P:(k + 1) * P], gates[:, k * GT:(k + 1) * GT], ident[:, :])
            last.then_inc(s_cellT, 1)
            pe.wait_ge(s_cd, 3)
            for k in range(2):
                last = pe.matmul(work_ps[0:D, 0:D], spread[:, k, :, :].rearrange("t a k -> t (a k)"),
                                 newRT[:, k * D:(k + 1) * D], start=(k == 0), stop=(k == 1))
            last.then_inc(s_nw, 1)
            pe.wait_ge(s_cd, 4)
            pe.wait_ge(s_small, 16 * (N_SMALL - 2))
            for k in range(2):
                last = pe.transpose(work_ps[0:D, (k + 1) * D:(k + 2) * D], w_in[:, k, :], ident[0:D, 0:D])
            last.then_inc(s_nw, 1)
            pe.wait_ge(s_cd, 6)

            def aggregate(layer):
                if layer:
                    pe.wait_ge(s_aggfree, layer)
                for k in range(4):
                    pe.matmul(agg_ps[:, 512 * k:512 * (k + 1)], zeros[:, 0:P], zeros[:, :], start=True, stop=False, skip_group_check=True)
                first = layer * NG

                def edge_products(g, q):
                    pe.wait_ge(s_ea[q], 16 * g[0] + 16)
                    for h, (k0, k1) in enumerate(HALVES):
                        pe.wait_ge(s_eaT, 2 * g[1] + (h + 1))
                        for k in range(k0, k1):
                            last = pe.transpose(work_ps[:, 1536 + P * (k - k0):1536 + P * (k - k0 + 1)], ea[q][:, k * P:(k + 1) * P], ident[:, :])
                        last.then_inc(s_tp, 1)

                with pe.Fori(0, NG // 2) as i:
                    for q in range(2):
                        if layer == 3:
                            edge_products((i, 2 * i + q), q)
                            pe.wait_ge(s_eaWfree, 2 * i + (q + 1))
                            pe.wait_ge(s_eaT, 4 * i + (2 * q + 3))
                            for k in range(G // 4):
                                last = pe.matmul(work_ps[:, 256 * k:256 * (k + 1)], eaT[:, k, :],
                                                 we4[:, :, :].rearrange("p a f -> p (a f)"), start=True, stop=True)
                            last.then_inc(s_eaW, 1)
                            pe.wait_ge(s_eaW, 2 * i + (q + 2))
                            pe.sem_inc(s_eafree, 1)
                        with pe.Fori(0, G // 2) as c:
                            for u in range(2):
                                pe.wait_ge(s_hot, 2 * G * i + 2 * c + ((first + q) * G + u + 1))
                                for b in range(NB):
                                    mark = hot[u][:, b * BN:(b + 1) * BN]
                                    for k in range(3):
                                        last = pe.matmul(agg_ps[0:BN, b * D:(b + 1) * D], mark, part[:, 2 * c + (q * G + u), k, :],
                                                         start=False, stop=False, skip_group_check=True)
                                    if layer == 0:
                                        last = pe.matmul(agg_ps[0:BN, NB * D + b:NB * D + b + 1], mark, ones[:, :],
                                                         start=False, stop=False, skip_group_check=True)
                                last.then_inc(s_hfree, 1)
                        pe.wait_ge(s_hfree, 2 * G * i + ((first + q + 1) * G + 2))
                        pe.sem_inc(s_pfree, 1)
                pe.wait_ge(s_hfree, (layer + 1) * NG * G + 2)
                pe.sem_inc(s_agg, 1)

            def transposed(evs):
                for c in range(7):
                    if c >= 2:
                        pe.wait_ge(s_ev, evs + c - 1)
                    for b in range(4 * c, min(4 * c + 4, NB)):
                        last = pe.transpose(work_ps[0:D, 512 * (c % 2) + BN * (b % 4):512 * (c % 2) + BN * (b % 4 + 1)],
                                            hb[:, b, :], ident[0:BN, 0:BN])
                    last.then_inc(s_tp, 1)

            def two_products(evs, w_first, w_second):
                for c in range(7):
                    w = min(NT, N - c * NT)
                    pe.wait_ge(s_ev, evs + max(c + 1, 7 + c - 1 if c >= 2 else 0))
                    pe.matmul(work_ps[0:D, 1024 + 512 * (c % 2):1024 + 512 * (c % 2) + w], w_first, hT[:, c * NT:c * NT + w],
                              start=True, stop=True).then_inc(s_tp, 1)
                pe.wait_ge(s_ev, evs + 14)
                for b in range(NB):
                    last = pe.matmul(agg_ps[0:BN, b * D:(b + 1) * D], rT[:, b * BN:(b + 1) * BN], w_second, start=True, stop=True)
                last.then_inc(s_pe, 1)

            aggregate(0)
            pe.wait_ge(s_h, 1)
            pe.wait_ge(s_const, 6)
            transposed(0)
            two_products(0, w1T[:, :], w2T[:, :])
            aggregate(1)
            pe.wait_ge(s_h, 2)
            transposed(14)
            pe.wait_ge(s_ev, 21)
            for b in range(NB):
                last = pe.matmul(agg_ps[0:BN, b * D:(b + 1) * D], hT[:, b * BN:(b + 1) * BN], new_w[:, :], start=True, stop=True)
            last.then_inc(s_pe, 1)
            aggregate(2)
            aggregate(3)
            pe.wait_ge(s_h, 3)
            transposed(21)
            two_products(21, w1c[:, :], w2c[:, :])


_INS = ['x', 'src', 'dst', 'edge_attr_32', 'edge_weight', 'L0_gnn_W1', 'L0_gnn_b1', 'L0_gnn_W2', 'L0_gnn_b2',
        'L1_gnn_gc_weights', 'L1_gnn_prev_weights', 'L1_gnn_w_ih', 'L1_gnn_w_hh', 'L1_gnn_b_ih', 'L1_gnn_b_hh',
        'L3_gnn_We', 'L3_gnn_be', 'L3_gnn_W1', 'L3_gnn_b1', 'L3_gnn_W2', 'L3_gnn_b2', 'L3_gnn_eps_gin',
        'L3_gnn_gamma', 'L3_gnn_beta']


def kernel(**inputs):
    import numpy as _np
    import concourse.bacc as _bacc
    from concourse import mybir as _mybir
    from concourse.bass_utils import run_bass_kernel_spmd as _run

    nc = _bacc.Bacc("TRN2", target_bir_lowering=False, num_devices=1)
    arrays, args = {}, []
    for name in _INS:
        a = _np.ascontiguousarray(inputs[name])
        if a.ndim == 0:
            a = a.reshape(1)
        arrays[f"in_{name}_dram"] = a
        args.append(nc.dram_tensor(f"in_{name}_dram", a.shape, _mybir.dt.from_np(a.dtype), kind="ExternalInput").ap())
    res = nc.dram_tensor("out_0_dram", (N, D), fp32, kind="ExternalOutput").ap()
    gnn_kernel(nc, *args, res)
    r = _run(nc, [arrays], core_ids=[0])
    return r.results[0]["out_0_dram"]
```

```python
import numpy as np
import concourse.bass as bass
from concourse import mybir
from contextlib import ExitStack

fp32 = mybir.dt.float32
bf16 = mybir.dt.bfloat16
fp16 = mybir.dt.float16
i32 = mybir.dt.int32
ALU = mybir.AluOpType
ACT = mybir.ActivationFunctionType
AX = mybir.AxisListType

P = 128
N = 3125
D = 64
ED = 32
E = 103125
NB = 25
BN = N // NB
G = 24
NG = -(-E // (P * G))
COLS = NG * G
TAIL = E - (NG - 1) * P * G
TP, TR = TAIL // G, TAIL % G
H = D * D
TILES = 3 * H // P
GT = H // P
RING = 6
STEPS = TILES // RING
MID = (N - 1) // 2
LN_EPS = 1e-5
SLOPE = 0.2
HALVES = ((0, 4), (4, G // 4))
NT = 500
NC7 = -(-N // NT)

CH = 2 * NB + 1
SLOTS = CH * P
DUMP = NB * SLOTS
ROW = ED + 4
MAGIC = 1.5 * 2.0 ** 23
SECTIONS = ((0, 15), (15, 33), (33, CH))


W = 3
MS = 3 * D + 2


def groups_of(k):
    c0, c1 = SECTIONS[k]
    return [(c, c + W) for c in range(c0, c1, W)]


GROUPS = [(k, *cc) for k in range(3) for cc in groups_of(k)]
NGR = len(GROUPS)
ENDS = [sum(len(groups_of(i)) for i in range(k + 1)) for k in range(3)]


def source_of(c):
    return 0 if c < 3 else (c - 1) // 2


class Step:

    def __init__(self, engine, sem):
        self.engine, self.sem, self.n = engine, sem, 0

    def link(self, ins):
        self.n += 1
        ins.then_inc(self.sem, 1)
        self.engine.wait_ge(self.sem, self.n)


def gnn_kernel(nc, x, src, dst, edge_attr_32, edge_weight, L0_gnn_W1, L0_gnn_b1, L0_gnn_W2, L0_gnn_b2,
               L1_gnn_gc_weights, L1_gnn_prev_weights, L1_gnn_w_ih, L1_gnn_w_hh, L1_gnn_b_ih, L1_gnn_b_hh,
               L3_gnn_We, L3_gnn_be, L3_gnn_W1, L3_gnn_b1, L3_gnn_W2, L3_gnn_b2, L3_gnn_eps_gin,
               L3_gnn_gamma, L3_gnn_beta, out):
    ctx = ExitStack()
    with ctx:
        def sb(name, shape, dt=fp32):
            return ctx.enter_context(nc.sbuf_tensor(name, shape, dt))

        def sem(name):
            return ctx.enter_context(nc.semaphore(name))

        def row(v):
            return v.rearrange("(a n) -> a n", a=1)

        tables = [nc.dram_tensor(f"node_table{k}", (N, D), fp32).ap() for k in range(3)]

        slots = nc.dram_tensor("edge_slots", (DUMP + P * COLS, ROW), fp32).ap()
        slot_src = nc.dram_tensor("slot_src", (NB, SLOTS), fp16).ap()

        arena = sb("arena", [P, (RING + 3) * H])
        taken = [0]

        def carve(rows, words):
            at = taken[0]
            taken[0] += words
            assert taken[0] <= (RING + 3) * H, taken
            return arena[0:rows, at:at + words]

        w_tile = [carve(P, H) for k in range(RING)]
        vec = [carve(P, H) for k in range(2)]
        junk = [carve(P, H // 2).bitcast(bf16) for k in range(2)]
        taken[0] = 0
        hT = carve(D, N)
        bias_g, cell, gc_g, newRT = (arena[0:GT, at:at + n] for at, n in ((0, 6 * P), (6 * P, 6 * P), (12 * P, P), (13 * P, P)))
        bias_g = bias_g.rearrange("t (m g p) -> t m g p", m=2, g=3)
        cell = cell.rearrange("t (m p) -> t m p", p=P)
        spread = arena[0:GT, 14 * P:15 * P].rearrange("t (k a m) -> t k a m", k=2, m=2)
        w_in = arena[0:D, 15 * P:16 * P].rearrange("n (k m) -> n k m", k=2)
        rT = carve(D + 1, N)
        hb = carve(BN, NB * D).rearrange("p (b f) -> p b f", f=D)
        sq = carve(BN, NB * D).rearrange("p (b f) -> p b f", f=D)
        X = carve(BN, NB * D).rearrange("p (b f) -> p b f", f=D)
        layers_at = taken[0]
        gat = [carve(P, G * D).rearrange("p (j f) -> p j f", f=D) for k in range(2)]
        part = carve(P, 2 * G * 3 * D // 2).bitcast(bf16).rearrange("p (c k f) -> p c k f", k=3, f=D)
        hot = [carve(P, (N + 1) // 2).bitcast(bf16)[:, 0:N] for k in range(2)]
        node_no = carve(P, (N + 1) // 2).bitcast(fp16)[:, 0:N]
        ea = [carve(P, G * ED) for k in range(2)]
        zeros = carve(P, 256).bitcast(bf16)
        eaT = carve(P, G // 4 * P).rearrange("p (k e) -> p k e", e=P)
        taken[0] = layers_at
        x_part = carve(BN, 2 * NB * 3 * D // 2).bitcast(bf16).rearrange("p (b c) -> p b c", c=3 * D)
        src_mark = carve(P, SLOTS // 2).bitcast(bf16)
        src_row = carve(P, SLOTS // 2).bitcast(fp16)
        dst_mark32 = carve(P, CH * BN + 1)[:, 0:CH * BN].rearrange("p (c n) -> p c n", n=BN)
        dst_mark = arena[:, taken[0] - CH * BN - 1:taken[0]].bitcast(bf16)[:, 0:CH * BN].rearrange("p (c n) -> p c n", n=BN)
        curT = arena[0:CH, taken[0] - CH * BN - 1:taken[0]].bitcast(fp16)[:, 0:NB * P].rearrange("c (b p) -> c b p", p=P)
        msg = [carve(P, W * MS // 2).bitcast(bf16).rearrange("p (j c) -> p j c", c=MS) for k in range(2)]
        msg32 = [carve(P, W * D) for k in range(2)]
        slot_row = carve(P, CH * ROW).rearrange("p (c w) -> p c w", w=ROW)
        slotT = [carve(P, P) for k in range(2)]
        slot_rowB = carve(P, CH * ROW).rearrange("p (c w) -> p c w", w=ROW)
        slot_dst = carve(P, NB * CH)
        slot_w = carve(P, NB * CH)

        acc = sb("acc", [P, RING])
        gates = sb("gates", [P, 2 * TILES])
        src_i = sb("src_i", [P, NG, G], i32)
        dst_i = sb("dst_i", [P, NG, G], i32)
        dst_f = dst_i[:, :, :].rearrange("p g j -> p (g j)").bitcast(fp32)
        wgt = sb("wgt", [P, NG, G])
        ident = sb("ident", [P, P])
        ident16 = sb("ident16", [P, P], fp16)
        before = sb("before", [P, P], fp16)
        idx = [sb(f"idx{k}", [P, G], i32) for k in range(2)]
        ones = sb("ones", [P, 1], bf16)
        ones32 = sb("ones32", [P, 1])
        we4 = sb("we4", [P, 4, D])
        we3 = sb("we3", [W * ROW, W, D])
        no25 = sb("no25", [P, NB], fp16)
        dblk = sb("dblk", [P, COLS], fp16)
        sblk = sb("sblk", [P, COLS], fp16)
        slo = sb("slo", [P, COLS], fp16)
        dlo1 = sb("dlo1", [P, COLS], fp16)
        cap = sb("cap", [P, COLS], fp16)
        base = sb("base", [P, COLS])
        efeat = [sb(f"efeat{k}", [P, G, ED]) for k in range(2)]
        pay = [sb(f"pay{k}", [P, G, ROW]) for k in range(2)]
        mark25 = sb("mark25", [P, G, 2 * NB], fp16)
        markT = sb("markT", [2 * NB, G, P], fp16)
        hist = sb("hist", [NB, NB, G + 1])
        keep = sb("keep", [NB, NB, G + 1])
        upto = sb("upto", [NB, NB, G + 1])
        upto16 = sb("upto16", [NB, G, NB], fp16)
        rjunk = sb("rjunk", [P, 4, P], bf16)
        dump = sb("dump", [P, G])
        minus2 = sb("minus2", [P, 1])
        rank_in = sb("rank_in", [P, G])
        rsel = sb("rsel", [P, G, NB])
        rank = sb("rank", [P, 5, G])
        pos = [sb(f"pos{k}", [P, G], i32) for k in range(2)]
        placed = sb("placed", [P, G])
        count = sb("count", [P, 1])
        flag = sb("flag", [1, 1], i32)
        node_f = sb("node_f", [P, 1])
        no125 = sb("no125", [P, BN])
        no125h = sb("no125h", [P, BN], fp16)
        cur = sb("cur", [P, 3, CH])
        blank = sb("blank", [P, CH * ROW // 9])

        stat = sb("stat", [BN, 4, NB])
        rdeg = sb("rdeg", [BN, NB])
        w1T = sb("w1T", [D, D])
        w2T = sb("w2T", [D + 1, D])
        w1c = sb("w1c", [D, D])
        w2c = sb("w2c", [D + 1, D])
        b1 = sb("b1", [D, 2])
        be_b = sb("be_b", [P, D])
        gam_b = sb("gam_b", [P, D])
        bet_b = sb("bet_b", [P, D])
        eps_b = sb("eps_b", [P, 1])
        new_w = sb("new_w", [D, D])

        agg_ps = ctx.enter_context(nc.psum_tensor("agg_ps", [P, 2048], fp32))
        work_ps = ctx.enter_context(nc.psum_tensor("work_ps", [P, 2048], fp32))
        agg = agg_ps[0:BN, 0:NB * D].rearrange("p (b f) -> p b f", f=D)
        deg = agg_ps[0:BN, NB * D:NB * D + NB]

        s_edges = sem("edges_loaded")
        s_pads = sem("pads_set")
        s_small = sem("weights_loaded")
        s_x = sem("x_loaded")
        s_vec = sem("cell_vectors_loaded")
        s_w = [sem(f"w_tile_loaded{k}") for k in range(RING)]
        s_wused = sem("w_tile_used")
        s_acc = sem("acc_copied")
        s_iota = sem("pool_constants")
        s_dve = sem("dve_steps")
        s_act = sem("act_steps")
        s_const = sem("dve_constants")
        s_idx = sem("idx_ready")
        s_gat = [sem(f"gathered{k}") for k in range(2)]
        s_gfree = sem("gat_free")
        s_part = sem("part_ready")
        s_pfree = sem("part_free")
        s_hot = sem("hot_ready")
        s_hfree = sem("hot_free")
        s_ea = [sem(f"ea_loaded{k}") for k in range(2)]
        s_eafree = sem("ea_free")
        s_tail = sem("ea_tail_row_loaded")
        s_tp = sem("eaT_transposed")
        s_eaT = sem("eaT_ready")
        s_eaW = sem("eaW_ready")
        s_eaWfree = sem("eaW_free")
        s_agg = sem("agg_done")
        s_pe = sem("pe_node_steps")
        s_ev = sem("act_node_steps")
        s_h = sem("h_ready")
        s_aggfree = sem("agg_free")
        s_var = sem("variance_ready")
        s_std = sem("std_ready")
        s_xnew = sem("x_new")
        s_tab = sem("table_stored")
        s_res = sem("out_stored")
        s_cell = sem("cell_gates_ready")
        s_cellT = sem("cell_gates_transposed")
        s_ca = sem("cell_act")
        s_cd = sem("cell_dve")
        s_nw = sem("new_w_ready")

        s_pool_pass = sem("pool_wait_passed")
        s_pe_pass = sem("pe_wait_passed")
        s_gtp = sem("ea_transposed")
        s_blank = sem("blank_set")
        s_init = sem("slots_blanked")
        s_ef = [sem(f"efeat_loaded{k}") for k in range(2)]
        s_eftail = sem("efeat_tail_row_loaded")
        s_efused = sem("efeat_used")
        s_mark = sem("mark25_ready")
        s_mtp = sem("mark25_transposed")
        s_mT = sem("markT_ready")
        s_hps = sem("histogram_in_psum")
        s_hist = sem("histogram_ready")
        s_upto = sem("upto_ready")
        s_same = sem("same_key_in_psum")
        s_rin = sem("rank_in_column_ready")
        s_sel = sem("upto_of_block_in_psum")
        s_pos = sem("pos_ready")
        s_placed = [sem(f"edges_placed{k}") for k in range(2)]
        s_cnt = sem("count_ready")
        s_tot = sem("total_in_psum")
        s_flag = sem("flag_ready")
        s_srow = [sem(f"slot_row_loaded{k}") for k in range(2)]
        s_cur = sem("cur_ready")
        s_curtp = sem("cur_transposed")
        s_curT = sem("curT_ready")
        s_ssrc = sem("slot_src_stored")
        s_row = [sem(f"src_row_loaded{k}") for k in range(3)]
        s_slot = [sem(f"slot_section_loaded{k}") for k in range(3)]
        s_sec = sem("section_marked")
        s_xp = sem("x_parts_ready")
        s_gps = sem("messages_in_psum")
        s_hi = sem("high_part_ready")
        s_msg = sem("messages_ready")
        s_sct = sem("group_scattered")
        s_blk = sem("block_taken")
        s_stp = sem("slots_transposed")
        s_sT = sem("slotT_ready")
        s_back = sem("agg_transposed_back")

        w_rows = [w.rearrange("(t p) k -> t p k", p=P) for w in (L1_gnn_w_ih, L1_gnn_w_hh)]
        ea_rows = edge_attr_32[0:(NG - 1) * P * G, :].rearrange("(g p j) c -> g p (j c)", p=P, j=G)
        N_SMALL = 19 + W
        block_slots = slots[0:DUMP, :].rearrange("(b p c) w -> b p (c w)", p=P, c=CH)

        def same_ps(j):
            return work_ps[:, 1024 + P * (j % 8):1024 + P * (j % 8 + 1)]

        s_scan, s_carry, s_place, s_curw, s_split = (sem(k) for k in ("scan_done", "carry_set", "place_steps", "cur_weights", "split_steps"))

        block = ctx.enter_context(nc.Block())

        def fast_sp(sp):
            rows = [slot_row, slot_rowB]

            def load_block(d, q):
                sp.dma_start(rows[q][:, :, :].rearrange("p c w -> p (c w)"), block_slots[d]).then_inc(s_srow[q], 16)

            for q in range(2):
                sp.wait_ge(s_placed[q], 16 * G * (NG // 2))
            for q in range(2):
                load_block(q, q)
            with sp.Fori(0, NB // 2 - 1) as i:
                for q in range(2):
                    sp.wait_ge(s_cur, 2 * i + q + 1)
                    load_block(2 * i + q + 2, q)
            sp.wait_ge(s_cur, NB - 2)
            load_block(NB - 1, 0)
            sp.wait_ge(s_curT, NB + 1)
            sp.dma_start(slot_src.rearrange("b (c p) -> c b p", p=P), curT[:, :, :]).then_inc(s_ssrc, 16)
            sp.wait_ge(s_ssrc, 16)

            def load_sections(layer, d, waits):
                for k, (c0, c1) in enumerate(SECTIONS):
                    if waits:
                        sp.wait_ge(s_sec, 6 * d + (6 * (NB * layer - 1) + 2 * k + 1))
                    sp.dma_start(src_row[:, c0 * P:c1 * P],
                                 slot_src[d, c0 * P:c1 * P].partition_broadcast(P)).then_inc(s_row[k], 16)
                    if layer == 3:
                        if waits != 2:
                            sp.wait_ge(s_stp, NGR * d + (ENDS[k] - NGR))
                        sp.dma_start(slot_row[:, c0:c1, :].rearrange("p c w -> p (c w)"),
                                     block_slots[d][:, c0 * ROW:c1 * ROW]).then_inc(s_slot[k], 16)

            for layer in range(4):
                if layer in (0, 3):
                    load_sections(layer, 0, 2 if layer else 0)
                with sp.Fori(1 if layer in (0, 3) else 0, NB) as d:
                    load_sections(layer, d, 1)
            sp.wait_ge(s_xnew, 4)

        def general_sp(sp):
            full = (NG - 1) * P * G
            for layer in range(3):
                sp.wait_ge(s_xnew, layer + 1)
                made = hb if layer == 2 else X
                sp.dma_start(tables[layer].rearrange("(b p) f -> p b f", p=BN), made[:, :, :]).then_inc(s_tab, 16)
            with sp.Fori(0, NG // 2 - 1) as i:
                for q in range(2):
                    sp.wait_ge(s_eafree, 2 * i + q + 1)
                    sp.dma_start(ea[q][:, :], ea_rows[2 * i + q]).then_inc(s_ea[q], 16)
            sp.wait_ge(s_eafree, NG - 1)
            sp.dma_start(ea[0][:, :], ea_rows[NG - 2]).then_inc(s_ea[0], 16)
            sp.wait_ge(s_eafree, NG)
            sp.dma_start(ea[1][TP:TP + 1, 0:TR * ED], row(edge_attr_32[full + TP * G:E, :].rearrange("e c -> (e c)"))).then_inc(s_tail, 16)
            sp.wait_ge(s_tail, 16)
            sp.dma_start(ea[1][0:TP, :], edge_attr_32[full:full + TP * G, :].rearrange("(p j) c -> p (j c)", j=G)).then_inc(s_ea[1], 16)
            sp.wait_ge(s_xnew, 4)
            sp.wait_ge(s_tab, 48)

        @block.sync
        def _(sp):
            for k, v in enumerate((L1_gnn_prev_weights, L1_gnn_gc_weights)):
                sp.dma_start(vec[k][:, :], v.rearrange("a c -> (a c)").partition_broadcast(P)).then_inc(s_vec, 16)
            sp.wait_ge(s_pads, 3)
            full = (NG - 1) * P * G
            for v, t in ((src, src_i), (dst, dst_i), (edge_weight, wgt)):
                sp.dma_start(t[:, 0:NG - 1, :], v[0:full].rearrange("(g p j) -> p g j", p=P, j=G)).then_inc(s_edges, 16)
                sp.dma_start(t[0:TP, NG - 1, :], v[full:full + TP * G].rearrange("(p j) -> p j", j=G)).then_inc(s_edges, 16)
                sp.dma_start(t[TP:TP + 1, NG - 1, 0:TR], row(v[full + TP * G:E])).then_inc(s_edges, 16)
            for k in range(RING):
                sp.dma_start(w_tile[k][:, :], w_rows[0][k]).then_inc(s_w[k], 16)
            n = 0
            small = [
                (w2T[D:D + 1, :], row(L0_gnn_b2)),
                (b1[:, 0:1], L0_gnn_b1.rearrange("(n a) -> n a", a=1)),
                (w1c[:, :], L3_gnn_W1), (w2c[0:D, :], L3_gnn_W2), (w2c[D:D + 1, :], row(L3_gnn_b2)),
                (b1[:, 1:2], L3_gnn_b1.rearrange("(n a) -> n a", a=1)),
                (be_b[:, :], L3_gnn_be.partition_broadcast(P)),
                (gam_b[:, :], L3_gnn_gamma.partition_broadcast(P)),
                (bet_b[:, :], L3_gnn_beta.partition_broadcast(P)),
                (eps_b[:, :], L3_gnn_eps_gin.partition_broadcast(P)),
            ]
            sp.wait_ge(s_const, 3)
            for k in range(4):
                small.append((we4[ED * k:ED * (k + 1), k, :], L3_gnn_We))
            for k in range(W):
                small.append((we3[ROW * k:ROW * k + ED, k, :], L3_gnn_We))
            for to, of in small:
                n += 1
                sp.dma_start(to, of).then_inc(s_small, 16)
            assert n == N_SMALL - 5
            with sp.Fori(0, STEPS - 1) as i:
                for k in range(RING):
                    sp.wait_ge(s_wused, RING * i + k + 3)
                    sp.dma_start(w_tile[k][:, :], w_rows[0][RING * i + RING + k]).then_inc(s_w[k], 16)
            with sp.Fori(0, STEPS) as i:
                for k in range(RING):
                    sp.wait_ge(s_wused, RING * i + (TILES - RING + k + 3))
                    sp.dma_start(w_tile[k][:, :], w_rows[1][RING * i + k]).then_inc(s_w[k], 16)
            sp.wait_ge(s_cell, 1)
            sp.dma_start(bias_g[:, 0, :, :], L1_gnn_b_ih.rearrange("(g t p) -> t g p", t=GT, p=P)).then_inc(s_small, 16)
            sp.dma_start(bias_g[:, 1, :, :], L1_gnn_b_hh.rearrange("(g t p) -> t g p", t=GT, p=P)).then_inc(s_small, 16)
            sp.dma_start(w_in[:, 0, :], L0_gnn_W1).then_inc(s_small, 16)
            sp.dma_start(w_in[:, 1, :], L0_gnn_W2).then_inc(s_small, 16)
            sp.dma_start(gc_g[:, :], L1_gnn_gc_weights.rearrange("(t a) c -> t (a c)", a=2)).then_inc(s_small, 16)
            sp.dma_start(X[:, :, :], x.rearrange("(b p) f -> p b f", p=BN)).then_inc(s_x, 16)
            sp.wait_ge(s_flag, 1)
            fits = sp.value_load(flag[0:1, 0:1], min_val=0, max_val=1)
            with sp.If(fits == 1):
                fast_sp(sp)
            with sp.Else():
                general_sp(sp)
            sp.dma_start(out.rearrange("(b p) f -> p b f", p=BN), X[:, :, :]).then_inc(s_res, 16)
            sp.wait_ge(s_res, 16)

        def general_pool(pool):
            pool.wait_ge(s_cell, 1)
            pool.iota(node_no[:, :], pattern=[[1, N]], base=-MID, channel_multiplier=0, allow_small_or_imprecise_dtypes=True).then_inc(s_iota, 1)
            for layer in range(4):
                table = x if layer == 0 else tables[layer - 1]
                if layer:
                    pool.wait_ge(s_tab, 16 * layer)
                first = layer * NG
                with pool.Fori(0, NG // 2) as i:
                    for q in range(2):
                        pool.wait_ge(s_gfree, 2 * i + (first + q + 1))
                        pool.tensor_copy(idx[q][:, :], src_i[:, 2 * i + q, :]).then_inc(s_idx, 1)
                        pool.wait_ge(s_pads, 3)
                        pool.wait_ge(s_idx, 2 * i + (first + q + 1))
                        for j in range(G):
                            pool.indirect_dma_start(
                                out=gat[q][:, j, :], out_offset=None, in_=table,
                                in_offset=bass.IndirectOffsetOnAxis(ap=idx[q][:, j:j + 1], axis=0)).then_inc(s_gat[q], 16)

        @block.gpsimd
        def _(pool):
            pool.memset(src_i[:, :, :], 0).then_inc(s_pads, 1)
            pool.memset(dst_i[:, :, :], -N).then_inc(s_pads, 1)
            pool.memset(wgt[:, :, :], 0.0).then_inc(s_pads, 1)
            pool.memset(ident[:, :], 0.0).then_inc(s_iota, 1)
            pool.memset(before[:, :], 1.0).then_inc(s_iota, 1)
            pool.iota(no25[:, :], pattern=[[1, NB]], base=0, channel_multiplier=0, allow_small_or_imprecise_dtypes=True).then_inc(s_iota, 1)
            pool.iota(no125[:, :], pattern=[[1, BN]], base=1, channel_multiplier=0, allow_small_or_imprecise_dtypes=True).then_inc(s_iota, 1)
            pool.iota(no125h[:, :], pattern=[[1, BN]], base=1, channel_multiplier=0, allow_small_or_imprecise_dtypes=True).then_inc(s_iota, 1)
            pool.iota(node_f[:, :], pattern=[[0, 1]], base=0, channel_multiplier=1, allow_small_or_imprecise_dtypes=True).then_inc(s_iota, 1)
            pool.iota(dump[:, :], pattern=[[1, G]], base=DUMP, channel_multiplier=COLS, allow_small_or_imprecise_dtypes=True).then_inc(s_iota, 1)
            pool.wait_ge(s_iota, 7)
            pool.affine_select(out=ident[:, :], in_=ident[:, :], compare_op=ALU.not_equal, fill=1.0,
                               base=0, pattern=[[-1, P]], channel_multiplier=1).then_inc(s_iota, 1)
            pool.affine_select(out=before[:, :], in_=before[:, :], compare_op=ALU.is_gt, fill=0.0,
                               base=0, pattern=[[-1, P]], channel_multiplier=1).then_inc(s_iota, 1)
            pool.wait_ge(s_init, 16 * NB)
            with pool.Fori(0, NG // 2) as i:
                for q in range(2):
                    pool.wait_ge(s_pos, 2 * i + (q + 2))
                    pool.sem_inc(s_pool_pass, 1)
                    for j in range(G):
                        pool.indirect_dma_start(
                            out=slots, out_offset=bass.IndirectOffsetOnAxis(ap=pos[q][:, j:j + 1], axis=0),
                            in_=pay[q][:, j, :], in_offset=None).then_inc(s_placed[q], 16)
            for q in range(2):
                pool.wait_ge(s_placed[q], 16 * G * (NG // 2))
            pool.wait_ge(s_flag, 1)
            fits = pool.value_load(flag[0:1, 0:1], min_val=0, max_val=1)
            with pool.If(fits == 1):
                pool.sem_inc(s_idx, 1)
            with pool.Else():
                general_pool(pool)

        def normaliser(dve, st):
            done = [0]

            def normalise(y, z):
                done[0] += 1
                st.link(dve.tensor_reduce(stat[:, 0, :], y, AX.X, ALU.add))
                st.link(dve.tensor_scalar(stat[:, 1, :], stat[:, 0, :], 1.0 / D, None, ALU.mult))
                st.link(dve.tensor_tensor(y, y, stat[:, 1, :].unsqueeze(2).to_broadcast([BN, NB, D]), ALU.subtract))
                st.link(dve.tensor_tensor(sq[:, :, :], y, y, ALU.mult))
                st.link(dve.tensor_reduce(stat[:, 0, :], sq[:, :, :], AX.X, ALU.add))
                dve.tensor_scalar(stat[:, 2, :], stat[:, 0, :], 1.0 / D, LN_EPS, ALU.mult, ALU.add).then_inc(s_var, 1)
                dve.wait_ge(s_std, done[0])
                st.link(dve.reciprocal(stat[:, 1, :], stat[:, 3, :]))
                return dve.tensor_tensor(z, y, stat[:, 1, :].unsqueeze(2).to_broadcast([BN, NB, D]), ALU.mult)

            return normalise

        Xv, hv, sv = X[:, :, :], hb[:, :, :], sq[:, :, :]
        out2 = agg

        def last_stage(dve, st, normalise):
            dve.wait_ge(s_pe, 3)
            st.link(dve.tensor_scalar(sv, out2, SLOPE, None, ALU.mult))
            st.link(dve.tensor_tensor(hv, out2, sv, ALU.max))
            st.link(normalise(hv, hv))
            st.link(dve.tensor_tensor(hv, hv, gam_b[0:BN, :].unsqueeze(1).to_broadcast([BN, NB, D]), ALU.mult))
            st.link(dve.tensor_tensor(hv, hv, bet_b[0:BN, :].unsqueeze(1).to_broadcast([BN, NB, D]), ALU.add))
            st.link(dve.tensor_tensor(hv, hv, Xv, ALU.add))
            normalise(hv, Xv).then_inc(s_xnew, 1)

        def fast_dve(dve, st):
            normalise = normaliser(dve, st)
            rows = [slot_row, slot_rowB]
            for q in range(2):
                dve.memset(msg[q][:, :, 3 * D:MS], 1.0).then_inc(s_msg, 1)
            dve.wait_ge(s_msg, 2)
            dve.sem_inc(s_sct, NGR)
            dve.sem_inc(s_blk, 1)

            def take_block(d, q, loads):
                dve.wait_ge(s_srow[q], loads)
                at = bass.ds(CH * d, CH)
                dve.tensor_copy(slot_dst[:, at], rows[q][:, :, ED + 1])
                dve.tensor_copy(slot_w[:, at], rows[q][:, :, ED + 2])
                if loads is not None:
                    dve.wait_ge(s_curtp, d + 1)
                dve.tensor_copy(cur[:, 0, :], rows[q][:, :, ED]).then_inc(s_cur, 1)

            dve.sem_inc(s_curtp, 1)
            with dve.Fori(0, NB // 2) as i:
                for q in range(2):
                    take_block(2 * i + q, q, 16 * i + 16)
            take_block(NB - 1, 0, 16 * (NB // 2 + 1))
            dve.wait_ge(s_cur, NB)

            def parts_of(y):
                pt = [x_part[:, 0:NB, k * D:(k + 1) * D] for k in range(3)]
                st.link(dve.tensor_copy(pt[0], y))
                st.link(dve.tensor_tensor(sv, y, pt[0], ALU.subtract))
                st.link(dve.tensor_copy(pt[1], sv))
                st.link(dve.tensor_tensor(sv, sv, pt[1], ALU.subtract))
                st.link(dve.tensor_copy(pt[2], sv))
                dve.tensor_copy(x_part[:, NB:2 * NB, :], x_part[:, 0:NB, :]).then_inc(s_xp, 1)

            def mark_section(layer, k, d):
                c0, c1 = SECTIONS[k]
                dve.wait_ge(s_row[k], 16 * d + 16 * (NB * layer + 1))
                dve.wait_ge(s_sct, NGR * d + (NGR * NB * layer + ENDS[k]))
                dve.tensor_scalar(src_mark[:, c0 * P:c1 * P], src_row[:, c0 * P:c1 * P], node_f[:, :], None, ALU.is_equal).then_inc(s_sec, 1)
                if layer == 2:
                    if k == 0:
                        dve.wait_ge(s_sec, 6 * d + (6 * NB * layer + 1))
                        at = bass.ds(CH * d, CH)
                        dve.tensor_copy(cur[:, 1, :], slot_dst[:, at])
                        dve.tensor_copy(cur[:, 2, :], slot_w[:, at]).then_inc(s_curw, 1)
                        dve.wait_ge(s_curw, d + 1)
                    for c in range(c0, c1):
                        last = dve.tensor_scalar(dst_mark32[:, c, :], no125[:, :], cur[:, 1, c:c + 1], cur[:, 2, c:c + 1], ALU.is_equal, ALU.mult)
                    last.then_inc(s_sec, 1)
                else:
                    n = c1 - c0
                    dve.tensor_tensor(dst_mark[:, c0:c1, :], no125h[:, :].unsqueeze(1).to_broadcast([P, n, BN]),
                                      slot_dst[:, bass.ds(CH * d + c0, n)].unsqueeze(2).to_broadcast([P, n, BN]), ALU.is_equal).then_inc(s_sec, 1)

            def split_groups(k, d):
                for n, (kk, c0, c1) in enumerate(GROUPS):
                    if kk != k:
                        continue
                    w = (c1 - c0)
                    ps = agg_ps[:, 1024 * (n % 2):1024 * (n % 2) + w * D].rearrange("p (j f) -> p j f", f=D)
                    m32 = msg32[n % 2][:, 0:w * D].rearrange("p (j f) -> p j f", f=D)
                    mm = msg[n % 2]
                    dve.wait_ge(s_hi, NGR * d + (n + 1))
                    dve.wait_ge(s_msg, NGR * d + (3 * NGR * NB + n + 2))
                    dve.scalar_tensor_tensor(m32, ps, 0.0, mm[:, 0:w, 0:D], ALU.max, ALU.subtract).then_inc(s_split, 1)
                    dve.wait_ge(s_split, 2 * NGR * d + (2 * n + 1))
                    dve.tensor_copy(mm[:, 0:w, D:2 * D], m32).then_inc(s_split, 1)
                    dve.wait_ge(s_split, 2 * NGR * d + (2 * n + 2))
                    dve.tensor_tensor(mm[:, 0:w, 2 * D:3 * D], m32, mm[:, 0:w, D:2 * D], ALU.subtract).then_inc(s_msg, 1)

            def take_sum(layer, d):
                dve.wait_ge(s_sct, NGR * d + NGR * (NB * layer + 2))
                if layer == 2:
                    dve.tensor_copy(hT[:, bass.ds(BN * d, BN)], work_ps[0:D, 0:BN]).then_inc(s_blk, 1)
                    return
                if layer == 0:
                    dve.tensor_copy(rdeg[:, bass.ds(d, 1)], work_ps[0:BN, 3 * D:3 * D + 1])
                dve.tensor_reduce(hb[:, d, :], work_ps[0:BN, 0:3 * D].rearrange("p (k f) -> p f k", f=D), AX.X, ALU.add).then_inc(s_blk, 1)

            def block_of(layer, d, last):
                mark_section(layer, 1, d)
                if layer == 3:
                    split_groups(0, d)
                mark_section(layer, 2, d)
                if layer == 3:
                    split_groups(1, d)
                if not last:
                    mark_section(layer, 0, d + 1)
                if layer == 3:
                    split_groups(2, d)
                take_sum(layer, d)

            def aggregate(layer):
                mark_section(layer, 0, 0)
                with dve.Fori(0, NB - 1) as d:
                    block_of(layer, d, False)
                block_of(layer, NB - 1, True)
                dve.wait_ge(s_blk, NB * (layer + 1) + 1)

            parts_of(Xv)
            aggregate(0)
            st.link(dve.tensor_scalar(rdeg[:, :], rdeg[:, :], 1.0, None, ALU.max))
            st.link(dve.reciprocal(rdeg[:, :], rdeg[:, :]))
            dve.tensor_tensor(hv, Xv, hv, ALU.add).then_inc(s_h, 1)
            dve.wait_ge(s_pe, 1)
            st.link(dve.tensor_tensor(hv, Xv, out2, ALU.add))
            normalise(hv, Xv).then_inc(s_xnew, 1)
            dve.wait_ge(s_xnew, 1)
            parts_of(Xv)
            aggregate(1)
            dve.sem_inc(s_h, 1)
            dve.wait_ge(s_pe, 2)
            st.link(dve.tensor_tensor(hv, out2, rdeg[:, :].unsqueeze(2).to_broadcast([BN, NB, D]), ALU.mult))
            st.link(dve.tensor_tensor(hv, hv, Xv, ALU.add))
            normalise(hv, Xv).then_inc(s_xnew, 1)
            dve.wait_ge(s_xnew, 2)
            parts_of(Xv)
            aggregate(2)
            dve.sem_inc(s_h, 1)
            dve.wait_ge(s_back, 1)
            st.link(dve.tensor_tensor(hv, Xv, agg, ALU.add))
            st.link(normalise(hv, Xv))
            dve.tensor_tensor(hv, Xv, be_b[0:BN, :].unsqueeze(1).to_broadcast([BN, NB, D]), ALU.add).then_inc(s_xnew, 1)
            dve.wait_ge(s_xnew, 3)
            parts_of(hv)
            dve.wait_ge(s_xp, 4)
            aggregate(3)
            st.link(dve.tensor_scalar(stat[:, 0, 0:1], eps_b[0:BN, :], 1.0, None, ALU.add))
            dve.scalar_tensor_tensor(hv, Xv, stat[:, 0, 0:1], hv, ALU.mult, ALU.add).then_inc(s_h, 1)
            last_stage(dve, st, normalise)

        def general_dve(dve, st):
            normalise = normaliser(dve, st)
            dve.memset(eaT[:, :, :], 0.0).then_inc(s_eaT, 1)
            dve.memset(zeros[:, :], 0.0).then_inc(s_const, 1)
            dve.sem_inc(s_eaW, 1)
            dve.sem_inc(s_eaWfree, 1)
            for q in range(2):
                dve.memset(ea[q][:, :], 0.0).then_inc(s_eafree, 1)
                dve.memset(gat[q][:, :, :], 0.0).then_inc(s_gfree, 1)
                dve.memset(part[:, q * G:(q + 1) * G, :, :], 0.0).then_inc(s_pfree, 1)
                dve.memset(hot[q][:, :], 0.0).then_inc(s_hfree, 1)
            dve.wait_ge(s_iota, 10)
            dve.wait_ge(s_eafree, 2)

            def aggregate(layer):
                first = layer * NG
                with dve.Fori(0, NG // 2) as i:
                    for q in range(2):
                        n0 = st.n
                        dve.wait_ge(s_gat[q], 16 * G * i + 16 * G * (layer * NG // 2 + 1))
                        dve.wait_ge(s_pfree, 2 * i + (first + q + 1))
                        m = gat[q][:, :, :]
                        per = 4 + (layer == 2) + 2 * (layer == 3)

                        def dep(ins, k):
                            ins.then_inc(s_dve, 1)
                            dve.wait_ge(s_dve, 2 * per * i + (n0 + q * per + k))

                        k = 1
                        if layer == 2:
                            wg = wgt[:, 2 * i + q, :].unsqueeze(2).to_broadcast([P, G, D])
                            dep(dve.tensor_tensor(m, m, wg, ALU.mult), k)
                            k += 1
                        if layer == 3:
                            dve.wait_ge(s_eaW, 2 * i + (q + 2))
                            dep(dve.tensor_tensor(m, m, work_ps[:, 0:G * D].rearrange("p (j f) -> p j f", f=D), ALU.add), k)
                            k += 1
                            ins = dve.tensor_scalar(m, m, 0.0, None, ALU.max)
                            dep(ins, k)
                            dve.sem_inc(s_eaWfree, 1)
                            k += 1
                        pt = part[:, q * G:(q + 1) * G, :, :]
                        dep(dve.tensor_copy(pt[:, :, 0, :], m), k)
                        dep(dve.tensor_tensor(m, m, pt[:, :, 0, :], ALU.subtract), k + 1)
                        dep(dve.tensor_copy(pt[:, :, 1, :], m), k + 2)
                        dep(dve.tensor_tensor(m, m, pt[:, :, 1, :], ALU.subtract), k + 3)
                        dve.tensor_copy(pt[:, :, 2, :], m).then_inc(s_part, 1)
                        dve.wait_ge(s_part, 2 * i + (first + q + 1))
                        dve.sem_inc(s_gfree, 1)
                        for j in range(G):
                            dve.wait_ge(s_hfree, 2 * G * i + ((first + q) * G + j + 1))
                            dve.tensor_scalar(hot[j % 2][:, :], node_no[:, :], dst_f[:, bass.ds(2 * G * i + (q * G + j), 1)],
                                              None, ALU.is_equal).then_inc(s_hot, 1)
                st.n += (NG // 2) * 2 * per

            aggregate(0)
            dve.wait_ge(s_agg, 1)
            st.link(dve.tensor_scalar(rdeg[:, :], deg, 1.0, None, ALU.max))
            st.link(dve.reciprocal(rdeg[:, :], rdeg[:, :]))
            dve.tensor_tensor(hv, Xv, agg, ALU.add).then_inc(s_h, 1)
            dve.wait_ge(s_pe, 1)
            st.link(dve.tensor_tensor(hv, Xv, out2, ALU.add))
            dve.sem_inc(s_aggfree, 1)
            normalise(hv, Xv).then_inc(s_xnew, 1)
            dve.wait_ge(s_xnew, 1)
            aggregate(1)
            dve.wait_ge(s_agg, 2)
            dve.tensor_copy(hv, agg).then_inc(s_h, 1)
            dve.wait_ge(s_pe, 2)
            st.link(dve.tensor_tensor(hv, out2, rdeg[:, :].unsqueeze(2).to_broadcast([BN, NB, D]), ALU.mult))
            dve.sem_inc(s_aggfree, 1)
            st.link(dve.tensor_tensor(hv, hv, Xv, ALU.add))
            dve.wait_ge(s_tab, 16)
            normalise(hv, Xv).then_inc(s_xnew, 1)
            dve.wait_ge(s_xnew, 2)
            aggregate(2)
            dve.wait_ge(s_agg, 3)
            st.link(dve.tensor_tensor(hv, Xv, agg, ALU.add))
            dve.sem_inc(s_aggfree, 1)
            dve.wait_ge(s_tab, 32)
            st.link(normalise(hv, Xv))
            dve.tensor_tensor(hv, Xv, be_b[0:BN, :].unsqueeze(1).to_broadcast([BN, NB, D]), ALU.add).then_inc(s_xnew, 1)
            aggregate(3)
            dve.wait_ge(s_agg, 4)
            dve.wait_ge(s_tab, 48)
            dve.sem_inc(s_h, 1)
            st.link(dve.tensor_scalar(stat[:, 0, 0:1], eps_b[0:BN, :], 1.0, None, ALU.add))
            dve.scalar_tensor_tensor(hv, Xv, stat[:, 0, 0:1], agg, ALU.mult, ALU.add).then_inc(s_h, 1)
            last_stage(dve, st, normalise)

        @block.vector
        def _(dve):
            st = Step(dve, s_dve)
            dve.memset(blank[:, :], 0.0).then_inc(s_blank, 1)
            dve.memset(ones[:, :], 1.0).then_inc(s_const, 1)
            dve.memset(we4[:, :, :], 0.0).then_inc(s_const, 1)
            dve.memset(we3[:, :, :], 0.0).then_inc(s_const, 1)
            dve.memset(minus2[:, :], -2.0).then_inc(s_const, 1)
            dve.memset(ones32[:, :], 1.0).then_inc(s_const, 1)
            for q in range(2):
                dve.memset(efeat[q][:, :, :], 0.0).then_inc(s_efused, 1)
                dve.memset(junk[q][:, :], 0.0).then_inc(s_wused, 1)
            dve.memset(gates[:, :], 0.0).then_inc(s_acc, 1)
            dve.memset(rjunk[:, :, :], 0.0)
            dve.sem_inc(s_rin, 4)
            st.link(dve.memset(placed[:, :], 0.0))
            st.link(dve.memset(keep[:, :, :], 1.0))
            st.link(dve.memset(keep[:, :, 0:1], 0.0))
            st.link(dve.memset(hist[:, :, :], 0.0))
            dve.wait_ge(s_iota, 9)
            dve.tensor_copy(ident16[:, :], ident[:, :]).then_inc(s_const, 1)
            dve.wait_ge(s_const, 6)

            dve.wait_ge(s_edges, 16 * 9)
            flat_src = src_i[:, :, :].rearrange("p g j -> p (g j)")
            flat_dst = dst_i[:, :, :].rearrange("p g j -> p (g j)")
            t0, t1 = base[:, :], pay[0][:, :, :].rearrange("p j w -> p (j w)")[:, 0:COLS]
            for flat, blk, low, plus in ((flat_src, sblk, slo, 0.0), (flat_dst, dblk, dlo1, 1.0)):
                st.link(dve.tensor_scalar(t0, flat, 1.0 / BN, 0.5 / BN - 0.5, ALU.mult, ALU.add))
                st.link(dve.tensor_scalar(t0, t0, MAGIC, MAGIC, ALU.add, ALU.subtract))
                st.link(dve.tensor_copy(blk[:, :], t0))
                st.link(dve.tensor_scalar(t0, t0, -float(BN), plus, ALU.mult, ALU.add))
                st.link(dve.tensor_copy(t1, flat))
                st.link(dve.tensor_tensor(low[:, :], t0, t1, ALU.add))
            st.link(dve.tensor_scalar(cap[:, :], t1, 0.0, None, ALU.is_ge))
            st.link(dve.tensor_tensor(t1, sblk[:, :], dblk[:, :], ALU.subtract))
            st.link(dve.tensor_scalar(t0, t1, 0.0, None, ALU.is_lt))
            st.link(dve.scalar_tensor_tensor(t1, t0, float(NB), t1, ALU.mult, ALU.add))
            st.link(dve.tensor_scalar(t0, t1, 0.0, None, ALU.is_gt))
            st.link(dve.scalar_tensor_tensor(t1, t1, 2.0, t0, ALU.mult, ALU.add))
            st.link(dve.tensor_scalar(t0, t0, -float(P), 3.0 * P, ALU.mult, ALU.add))
            st.link(dve.tensor_tensor(cap[:, :], cap[:, :], t0, ALU.mult))
            st.link(dve.scalar_tensor_tensor(base[:, :], dblk[:, :], float(SLOTS), t1, ALU.mult, ALU.add))
            st.link(dve.tensor_scalar(dst_f, flat_dst, float(MID), None, ALU.subtract))
            for q in range(2):
                st.link(dve.memset(pay[q][:, :, :], 0.0))
            dve.wait_ge(s_vec, 32)

            os_ = mark25[:, :, NB:2 * NB]
            sel = work_ps[:, 0:1024].rearrange("p (h c) -> p h c", c=512)[:, :, 0:G // 2 * NB]

            def mark_group(g):
                cols = bass.ds(G * g, G)
                dve.wait_ge(s_sel, g + 1)
                nos = no25[:, :].unsqueeze(1).to_broadcast([P, G, NB])
                dve.tensor_tensor(mark25[:, :, 0:NB], nos, dblk[:, cols].unsqueeze(2).to_broadcast([P, G, NB]), ALU.is_equal)
                dve.tensor_tensor(os_, nos, sblk[:, cols].unsqueeze(2).to_broadcast([P, G, NB]), ALU.is_equal).then_inc(s_mark, 1)

            def count_upto(g):
                dve.wait_ge(s_hist, 2 * g + 2)
                dve.tensor_tensor_scan(upto[:, :, :].rearrange("d s c -> d (s c)"), keep[:, :, :].rearrange("d s c -> d (s c)"),
                                       hist[:, :, :].rearrange("d s c -> d (s c)"), 0.0, ALU.mult, ALU.add).then_inc(s_scan, 1)
                dve.wait_ge(s_scan, g + 1)
                dve.tensor_scalar(upto16[:, :, :].rearrange("d c s -> d s c"), upto[:, :, 0:G], 2000.0, None, ALU.min).then_inc(s_upto, 1)
                dve.tensor_copy(hist[:, :, 0:1], upto[:, :, G:G + 1]).then_inc(s_carry, 1)

            def place(g, q, i2):
                cols = bass.ds(G * g, G)

                def dep(ins, k):
                    ins.then_inc(s_place, 1)
                    dve.wait_ge(s_place, PL * g + (k + 1))

                dve.wait_ge(s_sel, g + 2)
                dve.wait_ge(s_rin, G * g + (G + 4))
                r, m, hi, t, f = (rank[:, k, :] for k in range(5))
                for h in range(2):
                    half = rsel[:, h * (G // 2):(h + 1) * (G // 2), :]
                    dep(dve.tensor_tensor(half, sel[:, h, :].rearrange("p (c s) -> p c s", s=NB),
                                          mark25[:, h * (G // 2):(h + 1) * (G // 2), NB:2 * NB], ALU.mult), h)
                dep(dve.tensor_reduce(r, rsel[:, :, :], AX.X, ALU.add), 2)
                dep(dve.tensor_tensor(r, r, rank_in[:, :], ALU.add), 3)
                dep(dve.tensor_tensor(m, r, cap[:, cols], ALU.is_lt), 4)
                dep(dve.tensor_tensor(placed[:, :], placed[:, :], m, ALU.add), 5)
                dep(dve.tensor_scalar(hi, r, float(P), None, ALU.is_ge), 6)
                dep(dve.tensor_scalar(t, r, 2.0 * P, None, ALU.is_ge), 7)
                dep(dve.tensor_tensor(hi, hi, t, ALU.add), 8)
                dep(dve.scalar_tensor_tensor(t, r, float(CH), base[:, cols], ALU.mult, ALU.add), 9)
                dep(dve.scalar_tensor_tensor(t, hi, 1.0 - CH * P, t, ALU.mult, ALU.add), 10)
                dep(dve.tensor_tensor(f, t, dump[:, :], ALU.subtract), 11)
                dep(dve.tensor_tensor(f, f, m, ALU.mult), 12)
                if i2 is not None:
                    dve.wait_ge(s_placed[q], i2)
                dep(dve.tensor_tensor(pos[q][:, :], f, dump[:, :], ALU.add), 13)
                dep(dve.tensor_scalar(dump[:, :], dump[:, :], float(G), None, ALU.add), 14)
                dve.wait_ge(s_ef[q], 8 * g + (16 - 8 * q))
                dve.tensor_copy(pay[q][:, :, 0:ED], efeat[q][:, :, :]).then_inc(s_efused, 1)
                dep(dve.tensor_copy(pay[q][:, :, ED], slo[:, cols]), 15)
                dep(dve.tensor_copy(pay[q][:, :, ED + 1], dlo1[:, cols]), 16)
                dve.tensor_copy(pay[q][:, :, ED + 2], wgt[:, g, :]).then_inc(s_pos, 1)

            PL = 17

            def tiles(m, step, ks):
                for k in ks:
                    if k == 0:
                        dve.wait_ge(s_acc, step + (m * STEPS + 1))
                    dve.wait_ge(s_w[k], 16 * step + 16 * (m * STEPS + 1))
                    dve.wait_ge(s_wused, RING * step + (m * TILES + k + 1))
                    dve.tensor_tensor_reduce(out=junk[k % 2][:, 0:H], in0=w_tile[k][:, :], in1=vec[m][:, :],
                                             scale=1.0, scalar=0.0, op0=ALU.mult, op1=ALU.add,
                                             accum_out=acc[:, k:k + 1]).then_inc(s_wused, 1)
                    if k == RING - 1:
                        dve.wait_ge(s_wused, RING * step + (m * TILES + RING + 2))
                        dve.tensor_copy(gates[:, bass.ds(RING * step + m * TILES, RING)], acc[:, :]).then_inc(s_acc, 1)

            dve.sem_inc(s_sel, 1)
            dve.sem_inc(s_pos, 1)
            dve.sem_inc(s_carry, 1)
            dve.sem_inc(s_curT, 1)

            def sort_and_multiply(m, i, peeled):
                for q in range(2):
                    step = 2 * i + q
                    g = 2 * i + (m * STEPS + q)
                    mark_group(g)
                    tiles(m, step, (0, 1))
                    count_upto(g)
                    tiles(m, step, (2, 3))
                    place(g, q, None if peeled else 16 * G * i + 16 * G * (m * STEPS // 2))
                    tiles(m, step, (4, 5))

            sort_and_multiply(0, 0, True)
            with dve.Fori(1, STEPS // 2) as i:
                sort_and_multiply(0, i, False)
            with dve.Fori(0, STEPS // 2) as i:
                sort_and_multiply(1, i, False)
            for g in range(2 * STEPS, NG):
                mark_group(g)
                count_upto(g)
                place(g, g % 2, 16 * G * (g // 2))
            dve.wait_ge(s_acc, 2 * STEPS + 1)
            dve.memset(rT[D:D + 1, :], 1.0).then_inc(s_const, 1)
            dve.wait_ge(s_const, 7)
            dve.sem_inc(s_cell, 1)
            st.link(dve.tensor_reduce(count[:, :], placed[:, :], AX.X, ALU.add))
            dve.sem_inc(s_cnt, 1)
            dve.wait_ge(s_tot, 1)
            dve.tensor_scalar(flag[:, :], work_ps[0:1, 1024:1025], float(E), None, ALU.is_equal).then_inc(s_flag, 1)
            st.link(dve.memset(spread[:, :, :, :], 0.0))
            for k in range(2):
                st.link(dve.tensor_copy(spread[:, k, :, k], ident[0:GT, 0:GT]))
            tg = work_ps[0:GT, 0:6 * P].rearrange("t (m g p) -> t m g p", m=2, g=3)
            dve.wait_ge(s_cellT, 1)
            dve.wait_ge(s_small, 16 * N_SMALL)
            gi = cell[:, 0:3, :]
            gh = cell[:, 3:6, :]
            st.link(dve.tensor_tensor(gi, tg[:, 0, :, :], bias_g[:, 0, :, :], ALU.add))
            st.link(dve.tensor_tensor(gh, tg[:, 1, :, :], bias_g[:, 1, :, :], ALU.add))
            dve.tensor_tensor(cell[:, 0:2, :], cell[:, 0:2, :], cell[:, 3:5, :], ALU.add).then_inc(s_cd, 1)
            dve.wait_ge(s_ca, 1)
            st.link(dve.tensor_tensor(cell[:, 5, :], cell[:, 0, :], cell[:, 5, :], ALU.mult))
            dve.tensor_tensor(cell[:, 2, :], cell[:, 2, :], cell[:, 5, :], ALU.add).then_inc(s_cd, 1)
            dve.wait_ge(s_ca, 2)
            st.link(dve.tensor_scalar(cell[:, 3, :], cell[:, 1, :], -1.0, 1.0, ALU.mult, ALU.add))
            st.link(dve.tensor_tensor(cell[:, 3, :], cell[:, 3, :], cell[:, 2, :], ALU.mult))
            st.link(dve.tensor_tensor(cell[:, 4, :], cell[:, 1, :], gc_g[:, :], ALU.mult))
            dve.tensor_tensor(newRT[:, :], cell[:, 3, :], cell[:, 4, :], ALU.add).then_inc(s_cd, 1)
            dve.wait_ge(s_nw, 1)
            dve.tensor_copy(new_w[:, :], work_ps[0:D, 0:D]).then_inc(s_cd, 1)
            dve.wait_ge(s_nw, 2)
            dve.tensor_copy(w1T[:, :], work_ps[0:D, D:2 * D]).then_inc(s_cd, 1)
            dve.tensor_copy(w2T[0:D, :], work_ps[0:D, 2 * D:3 * D]).then_inc(s_cd, 1)
            dve.wait_ge(s_x, 16)
            dve.wait_ge(s_flag, 1)
            fits = dve.value_load(flag[0:1, 0:1], min_val=0, max_val=1)
            n0 = st.n
            with dve.If(fits == 1):
                fast_dve(dve, st)
            st.n = n0
            with dve.Else():
                general_dve(dve, st)

        def node_act(act):
            tp, std = [0], [0]

            def copy_hT():
                for c in range(NC7):
                    w = min(NT, N - c * NT)
                    tp[0] += 1
                    act.wait_ge(s_tp, tp[0])
                    act.activation(hT[:, c * NT:c * NT + w], work_ps[0:D, 512 * (c % 2):512 * (c % 2) + w], ACT.Copy).then_inc(s_ev, 1)

            def relu_rT(col):
                for c in range(NC7):
                    w = min(NT, N - c * NT)
                    tp[0] += 1
                    act.wait_ge(s_tp, tp[0])
                    act.activation(rT[0:D, c * NT:c * NT + w], work_ps[0:D, 1024 + 512 * (c % 2):1024 + 512 * (c % 2) + w],
                                   ACT.Relu, bias=b1[:, col:col + 1]).then_inc(s_ev, 1)

            def deviation():
                std[0] += 1
                act.wait_ge(s_var, std[0])
                act.activation(stat[:, 3, :], stat[:, 2, :], ACT.Sqrt).then_inc(s_std, 1)

            return copy_hT, relu_rT, deviation

        def fast_act(act):
            copy_hT, relu_rT, deviation = node_act(act)
            act.wait_ge(s_cell, 1)
            with act.Fori(0, NB) as d:
                act.wait_ge(s_curtp, d + 2)
                act.activation(curT[:, d, :], work_ps[0:CH, 1024:1024 + P], ACT.Copy).then_inc(s_curT, 1)

            def take_messages(layer):
                with act.Fori(0, NB) as d:
                    if layer == 3:
                        copy_slots(d, 0)
                    for n, (k, c0, c1) in enumerate(GROUPS):
                        w = c1 - c0
                        m = NGR * NB * layer + n
                        if layer == 3 and n + 1 < NGR:
                            copy_slots(d, n + 1)
                        act.wait_ge(s_gps, NGR * d + (m + 1))
                        act.wait_ge(s_sct, NGR * d + (m + NGR - (1 if n else 0)))
                        at = 1024 * (n % 2)
                        if layer < 2:
                            act.activation(msg[n % 2][:, :, 0:3 * D],
                                           agg_ps[:, at:at + 256 * W].rearrange("p (j c) -> p j c", c=256)[:, :, 0:3 * D], ACT.Copy).then_inc(s_msg, 1)
                        elif layer == 2:
                            act.activation(msg32[n % 2][:, 0:w * D], agg_ps[:, at:at + w * D], ACT.Copy).then_inc(s_msg, 1)
                        else:
                            act.activation(msg[n % 2][:, 0:w, 0:D], agg_ps[:, at:at + w * D].rearrange("p (j f) -> p j f", f=D), ACT.Relu).then_inc(s_hi, 1)

            def copy_slots(d, n):
                k, c0, c1 = GROUPS[n]
                act.wait_ge(s_stp, NGR * d + (n + 1))
                w = W * ROW
                act.activation(slotT[n % 2][0:w, :], work_ps[0:w, 512 * (1 + n % 2):512 * (1 + n % 2) + P], ACT.Copy).then_inc(s_sT, 1)

            take_messages(0)
            copy_hT()
            relu_rT(0)
            deviation()
            take_messages(1)
            copy_hT()
            deviation()
            take_messages(2)
            deviation()
            take_messages(3)
            copy_hT()
            relu_rT(1)
            deviation()
            deviation()

        def general_act(act):
            copy_hT, relu_rT, deviation = node_act(act)
            copy_hT()
            relu_rT(0)
            deviation()
            copy_hT()
            deviation()
            deviation()
            with act.Fori(0, NG) as g:
                act.wait_ge(s_eaW, g + 1)
                for h, (k0, k1) in enumerate(HALVES):
                    act.wait_ge(s_gtp, 2 * g + (h + 1))
                    act.activation(eaT[:, k0:k1, :], work_ps[:, 1536:1536 + P * (k1 - k0)].rearrange("p (k e) -> p k e", e=P),
                                   ACT.Copy).then_inc(s_eaT, 1)
            copy_hT()
            relu_rT(1)
            deviation()
            deviation()

        @block.scalar
        def _(act):
            act.wait_ge(s_blank, 1)
            ninth = CH * ROW // 9
            for d in range(NB):
                act.dma_start(block_slots[d].rearrange("p (a w) -> p a w", w=ninth),
                              blank[:, :].unsqueeze(1).to_broadcast([P, 9, ninth])).then_inc(s_init, 16)

            def load_features(g, q):
                act.wait_ge(s_efused, g + 1)
                act.dma_start(efeat[q][:, :, :].rearrange("p j c -> p (j c)"), ea_rows[g]).then_inc(s_ef[q], 16)

            for q in range(2):
                load_features(q, q)
            act.wait_ge(s_const, 6)

            def sort_group(g, loads):
                q = loads[1]
                act.wait_ge(s_mtp, g + 1)
                act.wait_ge(s_sel, g + 1)
                act.activation(markT[:, :, :].rearrange("k j e -> k (j e)"), agg_ps[0:2 * NB, 0:G * P // 2].bitcast(fp16), ACT.Copy).then_inc(s_mT, 1)
                act.wait_ge(s_hps, g + 1)
                act.wait_ge(s_carry, g + 1)
                for h in range(2):
                    act.activation(hist[:, :, 1 + h * (G // 2):1 + (h + 1) * (G // 2)].rearrange("d s c -> d c s"),
                                   work_ps[0:NB, 512 * h:512 * h + G // 2 * NB].rearrange("d (c s) -> d c s", s=NB), ACT.Copy).then_inc(s_hist, 1)
                act.wait_ge(s_pos, g + 1)
                for j in range(G):
                    if j % 4 == 0:
                        act.wait_ge(s_same, (G // 4) * g + (j // 4 + 1))
                    act.wait_ge(s_rin, G * g + (j + 1))
                    act.activation(rjunk[:, j % 4, :], same_ps(j), ACT.Relu, bias=minus2[:, :],
                                   accum_out=rank_in[:, j:j + 1]).then_inc(s_rin, 1)
                if loads[0] is not None:
                    load_features(loads[0], q)

            with act.Fori(0, NG // 2 - 2) as i:
                for q in range(2):
                    sort_group(2 * i + q, (2 * i + q + 2, q))
            sort_group(NG - 4, (NG - 2, 0))
            sort_group(NG - 3, (None, 1))
            full = (NG - 1) * P * G
            act.wait_ge(s_efused, NG)
            act.dma_start(efeat[1][TP:TP + 1, :, :].rearrange("p j c -> p (j c)")[:, 0:TR * ED],
                          row(edge_attr_32[full + TP * G:E, :].rearrange("e c -> (e c)"))).then_inc(s_eftail, 16)
            act.wait_ge(s_eftail, 16)
            act.dma_start(efeat[1][0:TP, :, :].rearrange("p j c -> p (j c)"),
                          edge_attr_32[full:full + TP * G, :].rearrange("(p j) c -> p (j c)", j=G)).then_inc(s_ef[1], 16)
            sort_group(NG - 2, (None, 0))
            sort_group(NG - 1, (None, 1))
            act.wait_ge(s_cd, 1)
            act.activation(cell[:, 0:2, :], cell[:, 0:2, :], ACT.Sigmoid).then_inc(s_ca, 1)
            act.wait_ge(s_cd, 2)
            act.activation(cell[:, 2, :], cell[:, 2, :], ACT.Tanh).then_inc(s_ca, 1)
            act.wait_ge(s_flag, 1)
            fits = act.value_load(flag[0:1, 0:1], min_val=0, max_val=1)
            with act.If(fits == 1):
                fast_act(act)
            with act.Else():
                general_act(act)

        def node_pe(pe):
            def transposed(evs):
                for c in range(NC7):
                    if c >= 2:
                        pe.wait_ge(s_ev, evs + c - 1)
                    for b in range(4 * c, min(4 * c + 4, NB)):
                        last = pe.transpose(work_ps[0:D, 512 * (c % 2) + BN * (b % 4):512 * (c % 2) + BN * (b % 4 + 1)],
                                            hb[:, b, :], ident[0:BN, 0:BN])
                    last.then_inc(s_tp, 1)

            def two_products(evs, w_first, w_second):
                for c in range(NC7):
                    w = min(NT, N - c * NT)
                    pe.wait_ge(s_ev, evs + max(c + 1, NC7 + c - 1 if c >= 2 else 0))
                    pe.matmul(work_ps[0:D, 1024 + 512 * (c % 2):1024 + 512 * (c % 2) + w], w_first, hT[:, c * NT:c * NT + w],
                              start=True, stop=True).then_inc(s_tp, 1)
                pe.wait_ge(s_ev, evs + 2 * NC7)
                for b in range(NB):
                    last = pe.matmul(agg_ps[0:BN, b * D:(b + 1) * D], rT[:, b * BN:(b + 1) * BN], w_second, start=True, stop=True)
                last.then_inc(s_pe, 1)

            def one_product(evs):
                pe.wait_ge(s_ev, evs + NC7)
                for b in range(NB):
                    last = pe.matmul(agg_ps[0:BN, b * D:(b + 1) * D], hT[:, b * BN:(b + 1) * BN], new_w[:, :], start=True, stop=True)
                last.then_inc(s_pe, 1)

            return transposed, two_products, one_product

        def fast_pe(pe):
            transposed, two_products, one_product = node_pe(pe)
            with pe.Fori(0, NB) as d:
                pe.wait_ge(s_cur, d + 1)
                pe.wait_ge(s_curT, d + 1)
                pe.sem_inc(s_pe_pass, 1)
                pe.transpose(work_ps[0:CH, 1024:1024 + P], cur[:, 0, :], ident[:, :]).then_inc(s_curtp, 1)

            def transpose_slots(d, n):
                k, c0, c1 = GROUPS[n]
                if n == 0 or GROUPS[n - 1][0] != k:
                    pe.wait_ge(s_slot[k], 16 * d + 16)
                w = W * ROW
                pe.transpose(work_ps[0:w, 512 * (1 + n % 2):512 * (1 + n % 2) + P],
                             slot_row[:, c0:c1, :].rearrange("p c w -> p (c w)"), ident[:, :]).then_inc(s_stp, 1)

            def gather(layer, d, n):
                k, c0, c1 = GROUPS[n]
                if n == 0 or GROUPS[n - 1][0] != k:
                    pe.wait_ge(s_sec, 6 * d + (6 * NB * layer + 2 * k + 1))
                pe.wait_ge(s_msg, NGR * d + (NGR * NB * layer + n + (2 if n == 0 else 1)))
                at = 1024 * (n % 2)
                if layer == 3:
                    pe.wait_ge(s_sT, NGR * d + (n + 1))
                    w = c1 - c0
                    pe.matmul(agg_ps[:, at:at + w * D], slotT[n % 2][0:W * ROW, :],
                              we3[:, :, :].rearrange("p a f -> p (a f)"), start=True, stop=False, skip_group_check=True)
                for c in range(c0, c1):
                    mark = src_mark[0:BN, c * P:(c + 1) * P]
                    b = d + source_of(c)
                    j = c - c0
                    if layer < 2:
                        to = at + 256 * j
                        last = pe.matmul(agg_ps[:, to:to + 3 * D], mark, x_part[:, b, :], start=True, stop=True)
                    else:
                        for part_no in range(3):
                            last = pe.matmul(agg_ps[:, at + j * D:at + (j + 1) * D], mark, x_part[:, b, part_no * D:(part_no + 1) * D],
                                             start=(part_no == 0 and layer == 2), stop=(part_no == 2), skip_group_check=True)
                last.then_inc(s_gps, 1)

            def scatter(layer, d, n):
                k, c0, c1 = GROUPS[n]
                if n == 0:
                    pe.wait_ge(s_blk, d + (NB * layer + 1))
                if n == 0 or GROUPS[n - 1][0] != k:
                    pe.wait_ge(s_sec, 6 * d + (6 * NB * layer + 2 * k + 2))
                pe.wait_ge(s_msg, NGR * d + (NGR * NB * layer + n + 3))
                for c in range(c0, c1):
                    first, final = c == 0, c == CH - 1
                    if layer == 2:
                        last = pe.matmul(work_ps[0:D, 0:BN], msg32[n % 2][:, (c - c0) * D:(c - c0 + 1) * D], dst_mark32[:, c, :], start=first, stop=final)
                    else:
                        last = pe.matmul(work_ps[0:BN, 0:MS - 1], dst_mark[:, c, :], msg[n % 2][:, c - c0, 0:MS - 1], start=first, stop=final)
                last.then_inc(s_sct, 1)

            def aggregate(layer):
                pe.wait_ge(s_xp, layer + 1)
                with pe.Fori(0, NB) as d:
                    if layer == 3:
                        transpose_slots(d, 0)
                    for n in range(NGR):
                        if layer == 3 and n + 1 < NGR:
                            transpose_slots(d, n + 1)
                        gather(layer, d, n)
                        if n:
                            scatter(layer, d, n - 1)
                    scatter(layer, d, NGR - 1)

            aggregate(0)
            pe.wait_ge(s_h, 1)
            transposed(0)
            two_products(0, w1T[:, :], w2T[:, :])
            aggregate(1)
            pe.wait_ge(s_h, 2)
            transposed(2 * NC7)
            one_product(2 * NC7)
            aggregate(2)
            pe.wait_ge(s_h, 3)
            for b in range(NB):
                last = pe.transpose(agg_ps[0:BN, b * D:(b + 1) * D], hT[:, b * BN:(b + 1) * BN], ident[0:D, 0:D])
            last.then_inc(s_back, 1)
            aggregate(3)
            pe.wait_ge(s_h, 4)
            transposed(3 * NC7)
            two_products(3 * NC7, w1c[:, :], w2c[:, :])

        def general_pe(pe):
            transposed, two_products, one_product = node_pe(pe)
            pe.wait_ge(s_const, 8)

            def aggregate(layer):
                if layer:
                    pe.wait_ge(s_aggfree, layer)
                for k in range(4):
                    pe.matmul(agg_ps[:, 512 * k:512 * (k + 1)], zeros[:, 0:P], zeros[:, :], start=True, stop=False, skip_group_check=True)
                first = layer * NG

                def edge_products(g, q):
                    pe.wait_ge(s_ea[q], 16 * g[0] + 16)
                    for h, (k0, k1) in enumerate(HALVES):
                        pe.wait_ge(s_eaT, 2 * g[1] + (h + 1))
                        for k in range(k0, k1):
                            last = pe.transpose(work_ps[:, 1536 + P * (k - k0):1536 + P * (k - k0 + 1)], ea[q][:, k * P:(k + 1) * P], ident[:, :])
                        last.then_inc(s_gtp, 1)

                with pe.Fori(0, NG // 2) as i:
                    for q in range(2):
                        if layer == 3:
                            edge_products((i, 2 * i + q), q)
                            pe.wait_ge(s_eaWfree, 2 * i + (q + 1))
                            pe.wait_ge(s_eaT, 4 * i + (2 * q + 3))
                            for k in range(G // 4):
                                last = pe.matmul(work_ps[:, 256 * k:256 * (k + 1)], eaT[:, k, :],
                                                 we4[:, :, :].rearrange("p a f -> p (a f)"), start=True, stop=True)
                            last.then_inc(s_eaW, 1)
                            pe.wait_ge(s_eaW, 2 * i + (q + 2))
                            pe.sem_inc(s_eafree, 1)
                        with pe.Fori(0, G // 2) as c:
                            for u in range(2):
                                pe.wait_ge(s_hot, 2 * G * i + 2 * c + ((first + q) * G + u + 1))
                                for b in range(NB):
                                    mark = hot[u][:, b * BN:(b + 1) * BN]
                                    for k in range(3):
                                        last = pe.matmul(agg_ps[0:BN, b * D:(b + 1) * D], mark, part[:, 2 * c + (q * G + u), k, :],
                                                         start=False, stop=False, skip_group_check=True)
                                    if layer == 0:
                                        last = pe.matmul(agg_ps[0:BN, NB * D + b:NB * D + b + 1], mark, ones[:, :],
                                                         start=False, stop=False, skip_group_check=True)
                                last.then_inc(s_hfree, 1)
                        pe.wait_ge(s_hfree, 2 * G * i + ((first + q + 1) * G + 2))
                        pe.sem_inc(s_pfree, 1)
                pe.wait_ge(s_hfree, (layer + 1) * NG * G + 2)
                pe.sem_inc(s_agg, 1)

            aggregate(0)
            pe.wait_ge(s_h, 1)
            transposed(0)
            two_products(0, w1T[:, :], w2T[:, :])
            aggregate(1)
            pe.wait_ge(s_h, 2)
            transposed(2 * NC7)
            one_product(2 * NC7)
            aggregate(2)
            aggregate(3)
            pe.wait_ge(s_h, 4)
            transposed(3 * NC7)
            two_products(3 * NC7, w1c[:, :], w2c[:, :])

        @block.tensor
        def _(pe):
            pe.wait_ge(s_const, 6)
            tps = agg_ps[0:2 * NB, 0:G * P // 2].bitcast(fp16)

            def sort_group(g, first):
                pe.wait_ge(s_mark, g + 1)
                if not first:
                    pe.wait_ge(s_mT, g)
                pe.sem_inc(s_pe_pass, 1)
                for j in range(G):
                    last = pe.transpose(tps[:, j * P:(j + 1) * P], mark25[:, j, :], ident16[:, :])
                last.then_inc(s_mtp, 1)
                pe.wait_ge(s_pos, g + 1)
                for j in range(G):
                    last = pe.matmul(work_ps[0:NB, 512 * (j // 12) + NB * (j % 12):512 * (j // 12) + NB * (j % 12 + 1)],
                                     mark25[:, j, 0:NB], mark25[:, j, NB:2 * NB], start=True, stop=True)
                last.then_inc(s_hps, 1)
                pe.wait_ge(s_mT, g + 1)
                for b in range(G // 4):
                    if b >= 2:
                        pe.wait_ge(s_rin, G * g + (4 * (b - 1) + 4))
                    else:
                        pe.wait_ge(s_rin, G * g + 4)
                    bank = work_ps[:, 1024 + 512 * (b % 2):1024 + 512 * (b % 2) + 512]
                    pe.matmul(bank, ident16[:, :], before[:, :].unsqueeze(1).to_broadcast([P, 4, P]), start=True, stop=False)
                    for j in range(4):
                        last = pe.matmul(bank[:, j * P:(j + 1) * P], markT[:, 4 * b + j, :], markT[:, 4 * b + j, :], start=False, stop=(j == 3))
                    last.then_inc(s_same, 1)
                pe.wait_ge(s_upto, g + 1)
                pe.wait_ge(s_hist, 2 * g + 2)
                for j in range(G):
                    last = pe.matmul(work_ps[:, 512 * (j // 12) + NB * (j % 12):512 * (j // 12) + NB * (j % 12 + 1)],
                                     markT[0:NB, j, :], upto16[:, j, :], start=True, stop=True)
                last.then_inc(s_sel, 1)

            sort_group(0, True)
            with pe.Fori(1, NG) as g:
                sort_group(g, False)
            pe.wait_ge(s_cnt, 1)
            pe.matmul(work_ps[0:1, 1024:1025], count[:, :], ones32[:, :], start=True, stop=True).then_inc(s_tot, 1)
            pe.wait_ge(s_cell, 1)
            for k in range(6):
                last = pe.transpose(work_ps[0:GT, k * P:(k + 1) * P], gates[:, k * GT:(k + 1) * GT], ident[:, :])
            last.then_inc(s_cellT, 1)
            pe.wait_ge(s_cd, 3)
            for k in range(2):
                last = pe.matmul(work_ps[0:D, 0:D], spread[:, k, :, :].rearrange("t a k -> t (a k)"),
                                 newRT[:, k * D:(k + 1) * D], start=(k == 0), stop=(k == 1))
            last.then_inc(s_nw, 1)
            pe.wait_ge(s_cd, 4)
            pe.wait_ge(s_small, 16 * N_SMALL)
            for k in range(2):
                last = pe.transpose(work_ps[0:D, (k + 1) * D:(k + 2) * D], w_in[:, k, :], ident[0:D, 0:D])
            last.then_inc(s_nw, 1)
            pe.wait_ge(s_cd, 6)
            pe.wait_ge(s_flag, 1)
            fits = pe.value_load(flag[0:1, 0:1], min_val=0, max_val=1)
            with pe.If(fits == 1):
                fast_pe(pe)
            with pe.Else():
                general_pe(pe)


_INS = ['x', 'src', 'dst', 'edge_attr_32', 'edge_weight', 'L0_gnn_W1', 'L0_gnn_b1', 'L0_gnn_W2', 'L0_gnn_b2',
        'L1_gnn_gc_weights', 'L1_gnn_prev_weights', 'L1_gnn_w_ih', 'L1_gnn_w_hh', 'L1_gnn_b_ih', 'L1_gnn_b_hh',
        'L3_gnn_We', 'L3_gnn_be', 'L3_gnn_W1', 'L3_gnn_b1', 'L3_gnn_W2', 'L3_gnn_b2', 'L3_gnn_eps_gin',
        'L3_gnn_gamma', 'L3_gnn_beta']


def kernel(**inputs):
    import numpy as _np
    import concourse.bacc as _bacc
    from concourse import mybir as _mybir
    from concourse.bass_utils import run_bass_kernel_spmd as _run

    nc = _bacc.Bacc("TRN2", target_bir_lowering=False, num_devices=1)
    arrays, args = {}, []
    for name in _INS:
        a = _np.ascontiguousarray(inputs[name])
        if a.ndim == 0:
            a = a.reshape(1)
        arrays[f"in_{name}_dram"] = a
        args.append(nc.dram_tensor(f"in_{name}_dram", a.shape, _mybir.dt.from_np(a.dtype), kind="ExternalInput").ap())
    res = nc.dram_tensor("out_0_dram", (N, D), fp32, kind="ExternalOutput").ap()
    gnn_kernel(nc, *args, res)
    r = _run(nc, [arrays], core_ids=[0])
    return r.results[0]["out_0_dram"]
```

```python
import numpy as np
import concourse.bass as bass
from concourse import mybir
from contextlib import ExitStack

fp32 = mybir.dt.float32
bf16 = mybir.dt.bfloat16
fp16 = mybir.dt.float16
i32 = mybir.dt.int32
ALU = mybir.AluOpType
ACT = mybir.ActivationFunctionType
AX = mybir.AxisListType

P = 128
N = 3125
D = 64
ED = 32
E = 103125
NB = 25
BN = N // NB
G = 24
NG = -(-E // (P * G))
COLS = NG * G
TAIL = E - (NG - 1) * P * G
TP, TR = TAIL // G, TAIL % G
H = D * D
TILES = 3 * H // P
GT = H // P
RING = 6
STEPS = TILES // RING
MID = (N - 1) // 2
LN_EPS = 1e-5
SLOPE = 0.2
HALVES = ((0, 4), (4, G // 4))
NT = 500
NC7 = -(-N // NT)

CH = 2 * NB + 1
SLOTS = CH * P
DUMP = NB * SLOTS
ROW = ED + 4
MAGIC = 1.5 * 2.0 ** 23
SECTIONS = ((0, 18), (18, 36), (36, CH))
WS = 18

MS = 3 * D + 2
W = 6
TW = 3
BUFS = 3
LAG = 4
GROUPS = [(k, c, min(c + W, c1)) for k, (c0, c1) in enumerate(SECTIONS) for c in range(c0, c1, W)]
NGR = len(GROUPS)
ENDS = [sum(g[0] <= k for g in GROUPS) for k in range(3)]


def source_of(c):
    return 0 if c < 3 else (c - 1) // 2


QUADS = [(a, min(a + 4, NB)) for a in range(0, NB, 4)]
NQ = len(QUADS)
QCH = [(2 * a + 1 if a else 0, 2 * b + 1) for a, b in QUADS]
QSEC = [[c1 <= e for _, e in SECTIONS].index(True) for _, c1 in QCH]
QLAST = [max(q for q in range(NQ) if QCH[q][0] < e) for _, e in SECTIONS]
ABUF = 4


class Step:

    def __init__(self, engine, sem):
        self.engine, self.sem, self.n = engine, sem, 0

    def link(self, ins):
        self.n += 1
        ins.then_inc(self.sem, 1)
        self.engine.wait_ge(self.sem, self.n)


def gnn_kernel(nc, x, src, dst, edge_attr_32, edge_weight, L0_gnn_W1, L0_gnn_b1, L0_gnn_W2, L0_gnn_b2,
               L1_gnn_gc_weights, L1_gnn_prev_weights, L1_gnn_w_ih, L1_gnn_w_hh, L1_gnn_b_ih, L1_gnn_b_hh,
               L3_gnn_We, L3_gnn_be, L3_gnn_W1, L3_gnn_b1, L3_gnn_W2, L3_gnn_b2, L3_gnn_eps_gin,
               L3_gnn_gamma, L3_gnn_beta, out):
    ctx = ExitStack()
    with ctx:
        def sb(name, shape, dt=fp32):
            return ctx.enter_context(nc.sbuf_tensor(name, shape, dt))

        def sem(name):
            return ctx.enter_context(nc.semaphore(name))

        def row(v):
            return v.rearrange("(a n) -> a n", a=1)

        tables = [nc.dram_tensor(f"node_table{k}", (N, D), fp32).ap() for k in range(3)]

        slots = nc.dram_tensor("edge_slots", (DUMP + P * COLS, ROW), fp32).ap()
        slot_src = nc.dram_tensor("slot_src", (NB, SLOTS), fp16).ap()
        adjacency = nc.dram_tensor("adjacency", (NB, BN, NB * BN), fp16).ap()

        arena = sb("arena", [P, (RING + 3) * H])
        taken = [0]

        def carve(rows, words):
            at = taken[0]
            taken[0] += words
            assert taken[0] <= (RING + 3) * H, taken
            return arena[0:rows, at:at + words]

        w_tile = [carve(P, H) for k in range(RING)]
        vec = [carve(P, H) for k in range(2)]
        junk = [carve(P, H // 2).bitcast(bf16) for k in range(2)]
        taken[0] = 0
        hT = carve(D, N)
        bias_g, cell, gc_g, newRT = (arena[0:GT, at:at + n] for at, n in ((0, 6 * P), (6 * P, 6 * P), (12 * P, P), (13 * P, P)))
        bias_g = bias_g.rearrange("t (m g p) -> t m g p", m=2, g=3)
        cell = cell.rearrange("t (m p) -> t m p", p=P)
        slotT = [arena[:, k * 2 * P:(k + 1) * 2 * P] for k in range(2)]
        spread = arena[0:GT, 14 * P:15 * P].rearrange("t (k a m) -> t k a m", k=2, m=2)
        w_in = arena[0:D, 15 * P:16 * P].rearrange("n (k m) -> n k m", k=2)
        rT = carve(D + 1, N)
        hb = carve(BN, NB * D).rearrange("p (b f) -> p b f", f=D)
        sq = carve(BN, NB * D).rearrange("p (b f) -> p b f", f=D)
        X = carve(BN, NB * D).rearrange("p (b f) -> p b f", f=D)
        layers_at = taken[0]
        gat = [carve(P, G * D).rearrange("p (j f) -> p j f", f=D) for k in range(2)]
        part = carve(P, 2 * G * 3 * D // 2).bitcast(bf16).rearrange("p (c k f) -> p c k f", k=3, f=D)
        hot = [carve(P, (N + 1) // 2).bitcast(bf16)[:, 0:N] for k in range(2)]
        node_no = carve(P, (N + 1) // 2).bitcast(fp16)[:, 0:N]
        ea = [carve(P, G * ED) for k in range(2)]
        zeros = carve(P, 256).bitcast(bf16)
        eaT = carve(P, G // 4 * P).rearrange("p (k e) -> p k e", e=P)
        taken[0] = layers_at
        x_part = carve(BN, NB * MS).bitcast(bf16).rearrange("p (b c) -> p b c", c=MS)
        src_mark = carve(P, SLOTS // 2).bitcast(bf16)
        src_row = carve(P, SLOTS // 2).bitcast(fp16)
        adj = [t[0:BN, k * (NB * BN + 1):k * (NB * BN + 1) + NB * BN].rearrange("p (b n) -> p b n", n=BN)
               for t in (src_row, src_mark.bitcast(fp16)) for k in range(2)]
        marks_at = taken[0]
        dst_mark = carve(P, SLOTS // 2).bitcast(bf16)[:, 0:CH * BN]
        taken[0] += NB * P // 2
        curT = arena[0:CH, marks_at + SLOTS // 2:taken[0]].bitcast(fp16)[:, 0:NB * P].rearrange("c (b p) -> c b p", p=P)
        rowB_at = taken[0]
        MW = W * 3 * D // 2
        msg_at = [carve(P, MW) for k in range(4)] + [arena[:, N + k * MW:N + (k + 1) * MW] for k in range(NGR - 4)]
        msg = [t.bitcast(bf16).rearrange("p (j c) -> p j c", c=3 * D) for t in msg_at]
        msg32 = [carve(P, W * D) for k in range(3)] + [arena[:, 4 * P + k * W * D:4 * P + (k + 1) * W * D] for k in range(NGR - 3)]
        slot_rowB = arena[:, rowB_at:rowB_at + CH * ROW].rearrange("p (c w) -> p c w", w=ROW)
        slot_row = carve(P, CH * ROW).rearrange("p (c w) -> p c w", w=ROW)
        slot_dst = carve(P, (NB * CH + 1) // 2).bitcast(fp16)
        slot_w = carve(P, NB * CH)
        src16 = carve(P, CH // 2 + 1).bitcast(fp16)[:, 0:CH]
        number = carve(P, BN * WS // 2).bitcast(fp16).rearrange("p (n c) -> p n c", c=WS)

        def marks(t, k):
            c0, c1 = SECTIONS[k]
            return t[:, c0 * BN:c1 * BN].rearrange("p (n c) -> p n c", c=c1 - c0)

        def mark_of(t, c):
            k = [c < e for _, e in SECTIONS].index(True)
            return marks(t, k)[:, :, c - SECTIONS[k][0]]

        acc = sb("acc", [P, RING])
        gates = sb("gates", [P, 2 * TILES])
        src_i = sb("src_i", [P, NG, G], i32)
        dst_i = sb("dst_i", [P, NG, G], i32)
        dst_f = dst_i[:, :, :].rearrange("p g j -> p (g j)").bitcast(fp32)
        wgt = sb("wgt", [P, NG, G])
        ident = sb("ident", [P, P])
        ident16 = sb("ident16", [P, P], fp16)
        before = sb("before", [P, P], fp16)
        idx = [sb(f"idx{k}", [P, G], i32) for k in range(2)]
        ones = sb("ones", [P, 1], bf16)
        ones32 = sb("ones32", [P, 1])
        we4 = sb("we4", [P, 4, D])
        we3 = sb("we3", [TW * ROW, TW, D])
        no25 = sb("no25", [P, NB], fp16)
        dblk = sb("dblk", [P, COLS], fp16)
        sblk = sb("sblk", [P, COLS], fp16)
        slo = sb("slo", [P, COLS], fp16)
        dlo1 = sb("dlo1", [P, COLS], fp16)
        cap = sb("cap", [P, COLS], fp16)
        base = sb("base", [P, COLS])
        efeat = [sb(f"efeat{k}", [P, G, ED]) for k in range(2)]
        pay = [sb(f"pay{k}", [P, G, ROW]) for k in range(2)]
        mark25 = sb("mark25", [P, G, 2 * NB], fp16)
        markT = sb("markT", [2 * NB, G, P], fp16)
        hist = sb("hist", [NB, NB, G + 1])
        keep = sb("keep", [NB, NB, G + 1])
        upto = sb("upto", [NB, NB, G + 1])
        upto16 = sb("upto16", [NB, G, NB], fp16)
        rjunk = sb("rjunk", [P, 4, P], bf16)
        dump = sb("dump", [P, G])
        minus2 = sb("minus2", [P, 1])
        rank_in = sb("rank_in", [P, G])
        rsel = sb("rsel", [P, G, NB])
        rank = sb("rank", [P, 5, G])
        pos = [sb(f"pos{k}", [P, G], i32) for k in range(2)]
        placed = sb("placed", [P, G])
        count = sb("count", [P, 1])
        flag = sb("flag", [1, 1], i32)
        node_f = sb("node_f", [P, 1])
        cur = sb("cur", [P, CH])
        blank = sb("blank", [P, CH * ROW // 9])

        stat = sb("stat", [BN, 4, NB])
        rdeg = sb("rdeg", [BN, NB])
        w1T = sb("w1T", [D, D])
        w2T = sb("w2T", [D + 1, D])
        w1c = sb("w1c", [D, D])
        w2c = sb("w2c", [D + 1, D])
        b1 = sb("b1", [D, 2])
        be_b = sb("be_b", [P, D])
        gam_b = sb("gam_b", [P, D])
        bet_b = sb("bet_b", [P, D])
        eps_b = sb("eps_b", [P, 1])
        new_w = sb("new_w", [D, D])

        agg_ps = ctx.enter_context(nc.psum_tensor("agg_ps", [P, 2048], fp32))
        work_ps = ctx.enter_context(nc.psum_tensor("work_ps", [P, 2048], fp32))
        agg = agg_ps[0:BN, 0:NB * D].rearrange("p (b f) -> p b f", f=D)
        deg = agg_ps[0:BN, NB * D:NB * D + NB]

        s_edges = sem("edges_loaded")
        s_pads = sem("pads_set")
        s_small = sem("weights_loaded")
        s_x = sem("x_loaded")
        s_vec = sem("cell_vectors_loaded")
        s_w = [sem(f"w_tile_loaded{k}") for k in range(RING)]
        s_wused = sem("w_tile_used")
        s_acc = sem("acc_copied")
        s_iota = sem("pool_constants")
        s_dve = sem("dve_steps")
        s_const = sem("dve_constants")
        s_idx = sem("idx_ready")
        s_gat = [sem(f"gathered{k}") for k in range(2)]
        s_gfree = sem("gat_free")
        s_part = sem("part_ready")
        s_pfree = sem("part_free")
        s_hot = sem("hot_ready")
        s_hfree = sem("hot_free")
        s_ea = [sem(f"ea_loaded{k}") for k in range(2)]
        s_eafree = sem("ea_free")
        s_tail = sem("ea_tail_row_loaded")
        s_tp = sem("eaT_transposed")
        s_eaT = sem("eaT_ready")
        s_eaW = sem("eaW_ready")
        s_eaWfree = sem("eaW_free")
        s_agg = sem("agg_done")
        s_pe = sem("pe_node_steps")
        s_ev = sem("act_node_steps")
        s_h = sem("h_ready")
        s_aggfree = sem("agg_free")
        s_var = sem("variance_ready")
        s_std = sem("std_ready")
        s_xnew = sem("x_new")
        s_tab = sem("table_stored")
        s_res = sem("out_stored")
        s_cell = sem("cell_gates_ready")
        s_cellT = sem("cell_gates_transposed")
        s_ca = sem("cell_act")
        s_cd = sem("cell_dve")
        s_nw = sem("new_w_ready")

        s_pool_pass = sem("pool_wait_passed")
        s_pe_pass = sem("pe_wait_passed")
        s_gtp = sem("ea_transposed")
        s_blank = sem("blank_set")
        s_init = sem("slots_blanked")
        s_ef = [sem(f"efeat_loaded{k}") for k in range(2)]
        s_eftail = sem("efeat_tail_row_loaded")
        s_efused = sem("efeat_used")
        s_mark = sem("mark25_ready")
        s_mtp = sem("mark25_transposed")
        s_mT = sem("markT_ready")
        s_hps = sem("histogram_in_psum")
        s_hist = sem("histogram_ready")
        s_upto = sem("upto_ready")
        s_same = sem("same_key_in_psum")
        s_rin = sem("rank_in_column_ready")
        s_sel = sem("upto_of_block_in_psum")
        s_pos = sem("pos_ready")
        s_placed = [sem(f"edges_placed{k}") for k in range(2)]
        s_cnt = sem("count_ready")
        s_tot = sem("total_in_psum")
        s_flag = sem("flag_ready")
        s_srow = [sem(f"slot_row_loaded{k}") for k in range(2)]
        s_cur = sem("cur_ready")
        s_curtp = sem("cur_transposed")
        s_curT = sem("curT_ready")
        s_ssrc = sem("slot_src_stored")
        s_row = [sem(f"src_row_loaded{k}") for k in range(3)]
        s_slot = [sem(f"slot_section_loaded{k}") for k in range(3)]
        s_mark0 = sem("marks_of_layer0_ready")
        s_built = sem("quad_in_psum")
        s_adj = sem("quad_in_adj")
        s_prod = sem("block_products_done")
        s_astore = [sem(f"adjacency_stored{k}") for k in range(2)]
        s_aload = [sem(f"adjacency_loaded{k}") for k in range(ABUF)]
        s_sec = sem("section_marked")
        s_xp = sem("x_parts_ready")
        s_gps = sem("messages_in_psum")
        s_hi = sem("high_part_ready")
        s_mid = sem("middle_part_ready")
        s_msg = sem("messages_ready")
        s_sct = sem("group_scattered")
        s_blk = sem("block_taken")
        s_stp = sem("slots_transposed")
        s_sT = sem("slotT_ready")
        s_weighed = sem("weighed_message_ready")

        w_rows = [w.rearrange("(t p) k -> t p k", p=P) for w in (L1_gnn_w_ih, L1_gnn_w_hh)]
        ea_rows = edge_attr_32[0:(NG - 1) * P * G, :].rearrange("(g p j) c -> g p (j c)", p=P, j=G)
        N_SMALL = 19 + TW
        block_slots = slots[0:DUMP, :].rearrange("(b p c) w -> b p (c w)", p=P, c=CH)

        def same_ps(j):
            return work_ps[:, 1024 + P * (j % 8):1024 + P * (j % 8 + 1)]

        s_scan, s_carry, s_place, s_split = (sem(k) for k in ("scan_done", "carry_set", "place_steps", "less_high_ready"))

        def views(n):
            w = GROUPS[n][2] - GROUPS[n][1]
            return w, msg32[n][:, 0:w * D].rearrange("p (j f) -> p j f", f=D), msg[n]

        block = ctx.enter_context(nc.Block())

        def fast_sp(sp):
            rows = [slot_row, slot_rowB]

            def load_block(d, q):
                sp.dma_start(rows[q][:, :, :].rearrange("p c w -> p (c w)"), block_slots[d]).then_inc(s_srow[q], 16)

            for q in range(2):
                sp.wait_ge(s_placed[q], 16 * G * (NG // 2))
            for q in range(2):
                load_block(q, q)

            def store_block(d, q):
                sp.wait_ge(s_adj, NQ * d + 2 * NQ)
                sp.dma_start(adjacency[d], adj[q][:, :, :].rearrange("p b n -> p (b n)")).then_inc(s_astore[q], 16)

            with sp.Fori(0, NB // 2 - 1) as i:
                for q in range(2):
                    sp.wait_ge(s_cur, 2 * i + q + 1)
                    load_block(2 * i + q + 2, q)
                    store_block(2 * i + q, q)
            sp.wait_ge(s_cur, NB - 2)
            load_block(NB - 1, 0)
            for d in range(NB - 3, NB):
                store_block(d, d % 2)
            sp.wait_ge(s_curT, NB + 1)
            sp.dma_start(slot_src.rearrange("b (c p) -> c b p", p=P), curT[:, :, :]).then_inc(s_ssrc, 16)
            sp.wait_ge(s_prod, NB + 2)
            sp.wait_ge(s_astore[0], 16 * (NB // 2 + 2))
            sp.wait_ge(s_astore[1], 16 * (NB // 2 + 1))

            def load_adj(d, k):
                sp.dma_start(adj[k][:, :, :].rearrange("p b n -> p (b n)"), adjacency[d]).then_inc(s_aload[k], 16)

            for k in range(ABUF):
                load_adj(k, k)
            with sp.Fori(1, NB // ABUF) as i:
                for k in range(ABUF):
                    sp.wait_ge(s_prod, ABUF * i + (NB - ABUF + k + 3))
                    load_adj(ABUF * i + k, k)
            for d in range(NB // ABUF * ABUF, NB):
                sp.wait_ge(s_prod, d + NB - ABUF + 3)
                load_adj(d, d % ABUF)
            sp.wait_ge(s_prod, 2 * NB + 2)
            sp.wait_ge(s_ssrc, 16)

            def load_sections(layer, d, waits):
                for k, (c0, c1) in enumerate(SECTIONS):
                    if waits:
                        sp.wait_ge(s_sec, 6 * d + (6 * (NB * (layer - 2) - 1) + 2 * k + 1))
                    sp.dma_start(src_row[:, c0 * P:c1 * P],
                                 slot_src[d, c0 * P:c1 * P].partition_broadcast(P)).then_inc(s_row[k], 16)
                    if layer == 3:
                        if waits != 2:
                            sp.wait_ge(s_stp, NGR * d + (ENDS[k] - NGR))
                        sp.dma_start(slot_row[:, c0:c1, :].rearrange("p c w -> p (c w)"),
                                     block_slots[d][:, c0 * ROW:c1 * ROW]).then_inc(s_slot[k], 16)

            load_sections(2, 0, 0)
            with sp.Fori(1, NB) as d:
                load_sections(2, d, 1)
            load_sections(3, 0, 2)
            with sp.Fori(1, NB) as d:
                load_sections(3, d, 1)
            sp.wait_ge(s_xnew, 4)

        def general_sp(sp):
            full = (NG - 1) * P * G
            for layer in range(3):
                sp.wait_ge(s_xnew, layer + 1)
                made = hb if layer == 2 else X
                sp.dma_start(tables[layer].rearrange("(b p) f -> p b f", p=BN), made[:, :, :]).then_inc(s_tab, 16)
            with sp.Fori(0, NG // 2 - 1) as i:
                for q in range(2):
                    sp.wait_ge(s_eafree, 2 * i + q + 1)
                    sp.dma_start(ea[q][:, :], ea_rows[2 * i + q]).then_inc(s_ea[q], 16)
            sp.wait_ge(s_eafree, NG - 1)
            sp.dma_start(ea[0][:, :], ea_rows[NG - 2]).then_inc(s_ea[0], 16)
            sp.wait_ge(s_eafree, NG)
            sp.dma_start(ea[1][TP:TP + 1, 0:TR * ED], row(edge_attr_32[full + TP * G:E, :].rearrange("e c -> (e c)"))).then_inc(s_tail, 16)
            sp.wait_ge(s_tail, 16)
            sp.dma_start(ea[1][0:TP, :], edge_attr_32[full:full + TP * G, :].rearrange("(p j) c -> p (j c)", j=G)).then_inc(s_ea[1], 16)
            sp.wait_ge(s_xnew, 4)
            sp.wait_ge(s_tab, 48)

        @block.sync
        def _(sp):
            sp.wait_ge(s_pads, 3)
            full = (NG - 1) * P * G
            for v, t in ((src, src_i), (dst, dst_i), (edge_weight, wgt)):
                sp.dma_start(t[:, 0:NG - 1, :], v[0:full].rearrange("(g p j) -> p g j", p=P, j=G)).then_inc(s_edges, 16)
                sp.dma_start(t[0:TP, NG - 1, :], v[full:full + TP * G].rearrange("(p j) -> p j", j=G)).then_inc(s_edges, 16)
                sp.dma_start(t[TP:TP + 1, NG - 1, 0:TR], row(v[full + TP * G:E])).then_inc(s_edges, 16)
            for k, v in enumerate((L1_gnn_prev_weights, L1_gnn_gc_weights)):
                sp.dma_start(vec[k][:, :], v.rearrange("a c -> (a c)").partition_broadcast(P)).then_inc(s_vec, 16)
            sp.wait_ge(s_init, 16 * NB)
            for k in range(RING):
                sp.dma_start(w_tile[k][:, :], w_rows[0][k]).then_inc(s_w[k], 16)
            n = 0
            small = [
                (w2T[D:D + 1, :], row(L0_gnn_b2)),
                (b1[:, 0:1], L0_gnn_b1.rearrange("(n a) -> n a", a=1)),
                (w1c[:, :], L3_gnn_W1), (w2c[0:D, :], L3_gnn_W2), (w2c[D:D + 1, :], row(L3_gnn_b2)),
                (b1[:, 1:2], L3_gnn_b1.rearrange("(n a) -> n a", a=1)),
                (be_b[:, :], L3_gnn_be.partition_broadcast(P)),
                (gam_b[:, :], L3_gnn_gamma.partition_broadcast(P)),
                (bet_b[:, :], L3_gnn_beta.partition_broadcast(P)),
                (eps_b[:, :], L3_gnn_eps_gin.partition_broadcast(P)),
            ]
            sp.wait_ge(s_const, 3)
            for k in range(4):
                small.append((we4[ED * k:ED * (k + 1), k, :], L3_gnn_We))
            for k in range(TW):
                small.append((we3[ROW * k:ROW * k + ED, k, :], L3_gnn_We))
            for to, of in small:
                n += 1
                sp.dma_start(to, of).then_inc(s_small, 16)
            assert n == N_SMALL - 5
            with sp.Fori(0, STEPS - 1) as i:
                for k in range(RING):
                    sp.wait_ge(s_wused, RING * i + k + 3)
                    sp.dma_start(w_tile[k][:, :], w_rows[0][RING * i + RING + k]).then_inc(s_w[k], 16)
            with sp.Fori(0, STEPS) as i:
                for k in range(RING):
                    sp.wait_ge(s_wused, RING * i + (TILES - RING + k + 3))
                    sp.dma_start(w_tile[k][:, :], w_rows[1][RING * i + k]).then_inc(s_w[k], 16)
            sp.wait_ge(s_cell, 1)
            sp.dma_start(bias_g[:, 0, :, :], L1_gnn_b_ih.rearrange("(g t p) -> t g p", t=GT, p=P)).then_inc(s_small, 16)
            sp.dma_start(bias_g[:, 1, :, :], L1_gnn_b_hh.rearrange("(g t p) -> t g p", t=GT, p=P)).then_inc(s_small, 16)
            sp.dma_start(w_in[:, 0, :], L0_gnn_W1).then_inc(s_small, 16)
            sp.dma_start(w_in[:, 1, :], L0_gnn_W2).then_inc(s_small, 16)
            sp.dma_start(gc_g[:, :], L1_gnn_gc_weights.rearrange("(t a) c -> t (a c)", a=2)).then_inc(s_small, 16)
            sp.dma_start(X[:, :, :], x.rearrange("(b p) f -> p b f", p=BN)).then_inc(s_x, 16)
            sp.wait_ge(s_flag, 1)
            fits = sp.value_load(flag[0:1, 0:1], min_val=0, max_val=1)
            with sp.If(fits == 1):
                fast_sp(sp)
            with sp.Else():
                general_sp(sp)
            sp.dma_start(out.rearrange("(b p) f -> p b f", p=BN), X[:, :, :]).then_inc(s_res, 16)
            sp.wait_ge(s_res, 16)

        def general_pool(pool):
            pool.wait_ge(s_cell, 1)
            pool.iota(node_no[:, :], pattern=[[1, N]], base=-MID, channel_multiplier=0, allow_small_or_imprecise_dtypes=True).then_inc(s_iota, 1)
            for layer in range(4):
                table = x if layer == 0 else tables[layer - 1]
                if layer:
                    pool.wait_ge(s_tab, 16 * layer)
                first = layer * NG
                with pool.Fori(0, NG // 2) as i:
                    for q in range(2):
                        pool.wait_ge(s_gfree, 2 * i + (first + q + 1))
                        pool.tensor_copy(idx[q][:, :], src_i[:, 2 * i + q, :]).then_inc(s_idx, 1)
                        pool.wait_ge(s_pads, 3)
                        pool.wait_ge(s_idx, 2 * i + (first + q + 1))
                        for j in range(G):
                            pool.indirect_dma_start(
                                out=gat[q][:, j, :], out_offset=None, in_=table,
                                in_offset=bass.IndirectOffsetOnAxis(ap=idx[q][:, j:j + 1], axis=0)).then_inc(s_gat[q], 16)

        @block.gpsimd
        def _(pool):
            pool.memset(src_i[:, :, :], 0).then_inc(s_pads, 1)
            pool.memset(dst_i[:, :, :], -N).then_inc(s_pads, 1)
            pool.memset(wgt[:, :, :], 0.0).then_inc(s_pads, 1)
            pool.memset(ident[:, :], 0.0).then_inc(s_iota, 1)
            pool.memset(before[:, :], 1.0).then_inc(s_iota, 1)
            pool.iota(no25[:, :], pattern=[[1, NB]], base=0, channel_multiplier=0, allow_small_or_imprecise_dtypes=True).then_inc(s_iota, 1)
            pool.iota(node_f[:, :], pattern=[[0, 1]], base=0, channel_multiplier=1, allow_small_or_imprecise_dtypes=True).then_inc(s_iota, 1)
            pool.iota(dump[:, :], pattern=[[1, G]], base=DUMP, channel_multiplier=COLS, allow_small_or_imprecise_dtypes=True).then_inc(s_iota, 1)
            pool.wait_ge(s_iota, 5)
            pool.affine_select(out=ident[:, :], in_=ident[:, :], compare_op=ALU.not_equal, fill=1.0,
                               base=0, pattern=[[-1, P]], channel_multiplier=1).then_inc(s_iota, 1)
            pool.affine_select(out=before[:, :], in_=before[:, :], compare_op=ALU.is_gt, fill=0.0,
                               base=0, pattern=[[-1, P]], channel_multiplier=1).then_inc(s_iota, 1)
            pool.wait_ge(s_init, 16 * NB)
            with pool.Fori(0, NG // 2) as i:
                for q in range(2):
                    pool.wait_ge(s_pos, 2 * i + (q + 2))
                    pool.sem_inc(s_pool_pass, 1)
                    for j in range(G):
                        pool.indirect_dma_start(
                            out=slots, out_offset=bass.IndirectOffsetOnAxis(ap=pos[q][:, j:j + 1], axis=0),
                            in_=pay[q][:, j, :], in_offset=None).then_inc(s_placed[q], 16)
            for q in range(2):
                pool.wait_ge(s_placed[q], 16 * G * (NG // 2))
            pool.wait_ge(s_flag, 1)
            fits = pool.value_load(flag[0:1, 0:1], min_val=0, max_val=1)
            with pool.If(fits == 1):
                pool.wait_ge(s_cell, 1)
                pool.iota(number[:, :, :], pattern=[[1, BN], [0, WS]], base=1, channel_multiplier=0, allow_small_or_imprecise_dtypes=True).then_inc(s_iota, 1)
                with pool.Fori(0, 2 * NB) as d:
                    for n in range(NGR):
                        w, m32, mm = views(n)
                        pool.wait_ge(s_mid, NGR * d + (n + 1))
                        pool.tensor_tensor(mm[:, 0:w, 2 * D:3 * D], m32, mm[:, 0:w, D:2 * D], ALU.subtract).then_inc(s_msg, 1)
            with pool.Else():
                general_pool(pool)

        def normaliser(dve, st):
            done = [0]

            def normalise(y, z):
                done[0] += 1
                st.link(dve.tensor_reduce(stat[:, 0, :], y, AX.X, ALU.add))
                st.link(dve.tensor_scalar(stat[:, 1, :], stat[:, 0, :], 1.0 / D, None, ALU.mult))
                st.link(dve.tensor_tensor(y, y, stat[:, 1, :].unsqueeze(2).to_broadcast([BN, NB, D]), ALU.subtract))
                st.link(dve.tensor_tensor(sq[:, :, :], y, y, ALU.mult))
                st.link(dve.tensor_reduce(stat[:, 0, :], sq[:, :, :], AX.X, ALU.add))
                dve.tensor_scalar(stat[:, 2, :], stat[:, 0, :], 1.0 / D, LN_EPS, ALU.mult, ALU.add).then_inc(s_var, 1)
                dve.wait_ge(s_std, done[0])
                st.link(dve.reciprocal(stat[:, 1, :], stat[:, 3, :]))
                return dve.tensor_tensor(z, y, stat[:, 1, :].unsqueeze(2).to_broadcast([BN, NB, D]), ALU.mult)

            return normalise

        Xv, hv, sv = X[:, :, :], hb[:, :, :], sq[:, :, :]
        out2 = agg

        def last_stage(dve, st, normalise):
            dve.wait_ge(s_pe, 3)
            st.link(dve.tensor_scalar(sv, out2, SLOPE, None, ALU.mult))
            st.link(dve.tensor_tensor(hv, out2, sv, ALU.max))
            st.link(normalise(hv, hv))
            st.link(dve.tensor_tensor(hv, hv, gam_b[0:BN, :].unsqueeze(1).to_broadcast([BN, NB, D]), ALU.mult))
            st.link(dve.tensor_tensor(hv, hv, bet_b[0:BN, :].unsqueeze(1).to_broadcast([BN, NB, D]), ALU.add))
            st.link(dve.tensor_tensor(hv, hv, Xv, ALU.add))
            normalise(hv, Xv).then_inc(s_xnew, 1)

        def fast_dve(dve, st):
            normalise = normaliser(dve, st)
            rows = [slot_row, slot_rowB]
            dve.sem_inc(s_msg, NGR)
            dve.sem_inc(s_split, BUFS)
            dve.sem_inc(s_weighed, BUFS)
            dve.sem_inc(s_sct, NGR)
            dve.sem_inc(s_blk, 2)
            dve.sem_inc(s_built, NQ)
            dve.sem_inc(s_adj, NQ)
            dve.sem_inc(s_prod, 2)
            for q in range(2):
                dve.sem_inc(s_astore[q], 16)
            dve.sem_inc(s_curtp, 1)
            st.link(dve.memset(x_part[:, :, 3 * D:MS], 1.0))

            def parts_of(y):
                pt = [x_part[:, 0:NB, k * D:(k + 1) * D] for k in range(3)]
                st.link(dve.tensor_copy(pt[0], y))
                st.link(dve.tensor_tensor(sv, y, pt[0], ALU.subtract))
                st.link(dve.tensor_copy(pt[1], sv))
                st.link(dve.tensor_tensor(sv, sv, pt[1], ALU.subtract))
                st.link(dve.tensor_copy(pt[2], sv))
                dve.tensor_copy(x_part[:, NB:2 * NB, 0:3 * D], x_part[:, 0:NB, 0:3 * D]).then_inc(s_xp, 1)

            def take_slots(d, q, loads):
                dve.wait_ge(s_srow[q], loads)
                at = bass.ds(CH * d, CH)
                dve.tensor_copy(slot_dst[:, at], rows[q][:, :, ED + 1])
                dve.tensor_copy(slot_w[:, at], rows[q][:, :, ED + 2])
                dve.tensor_scalar(src16[:, :], rows[q][:, :, ED], 1.0, None, ALU.add)
                dve.wait_ge(s_curtp, d + 1)
                dve.tensor_copy(cur[:, :], rows[q][:, :, ED]).then_inc(s_cur, 1)
                dve.wait_ge(s_cur, d + 1)
                for k, (c0, c1) in enumerate(SECTIONS):
                    n = c1 - c0
                    dve.wait_ge(s_built, NQ * d + (QLAST[k] + 1))
                    dve.tensor_tensor(marks(dst_mark, k), number[:, :, 0:n],
                                      slot_dst[:, bass.ds(CH * d + c0, n)].unsqueeze(1).to_broadcast([P, BN, n]), ALU.is_equal)
                    dve.tensor_tensor(marks(src_mark, k), number[:, :, 0:n],
                                      src16[:, c0:c1].unsqueeze(1).to_broadcast([P, BN, n]), ALU.is_equal).then_inc(s_mark0, 1)
                dve.wait_ge(s_mark0, 3 * d + 3)

            def take_product(layer, d, q):
                dve.wait_ge(s_prod, d + (NB * layer + 3))
                ps = work_ps[0:BN, 512 * q:512 * q + MS]
                if layer == 0:
                    dve.tensor_copy(rdeg[:, bass.ds(d, 1)], ps[:, 3 * D:3 * D + 1])
                dve.tensor_reduce(hb[:, d, :], ps[:, 0:3 * D].rearrange("p (k f) -> p f k", f=D), AX.X, ALU.add).then_inc(s_blk, 1)

            def mark_src(layer, k, d):
                c0, c1 = SECTIONS[k]
                dve.wait_ge(s_row[k], 16 * d + 16 * (NB * (layer - 2) + 1))
                if layer == 3 or not isinstance(d, int) or d:
                    dve.wait_ge(s_gps, NGR * d + (NGR * (NB * (layer - 2) - 1) + ENDS[k]))
                dve.tensor_scalar(src_mark[:, c0 * P:c1 * P], src_row[:, c0 * P:c1 * P], node_f[:, :], None, ALU.is_equal).then_inc(s_sec, 1)

            def mark_dst(layer, k, d):
                c0, c1 = SECTIONS[k]
                dve.wait_ge(s_sct, NGR * d + (NGR * NB * (layer - 2) + ENDS[k]))
                n = c1 - c0
                dve.tensor_tensor(marks(dst_mark, k), number[:, :, 0:n],
                                  slot_dst[:, bass.ds(CH * d + c0, n)].unsqueeze(1).to_broadcast([P, BN, n]), ALU.is_equal).then_inc(s_sec, 1)

            def weigh(d, n):
                w, m32, mm = views(n)
                ps = agg_ps[:, 512 * (n % BUFS):512 * (n % BUFS) + w * D].rearrange("p (j f) -> p j f", f=D)
                dve.wait_ge(s_gps, NGR * d + (n + 1))
                dve.wait_ge(s_msg, NGR * d + (n + 1))
                dve.tensor_tensor(m32, ps, slot_w[:, bass.ds(CH * d + GROUPS[n][1], w)].unsqueeze(2).to_broadcast([P, w, D]), ALU.mult).then_inc(s_weighed, 1)

            def less_high(layer, d, n):
                w, m32, mm = views(n)
                dve.wait_ge(s_hi, NGR * d + (NGR * NB * (layer - 2) + n + 1))
                if layer == 2:
                    dve.tensor_tensor(m32, m32, mm[:, 0:w, 0:D], ALU.subtract).then_inc(s_split, 1)
                    return
                ps = agg_ps[:, 512 * (n % BUFS):512 * (n % BUFS) + w * D].rearrange("p (j f) -> p j f", f=D)
                dve.wait_ge(s_msg, NGR * d + (NGR * NB + n + 1))
                dve.scalar_tensor_tensor(m32, ps, 0.0, mm[:, 0:w, 0:D], ALU.max, ALU.subtract).then_inc(s_split, 1)

            def take_sum(layer, d):
                dve.wait_ge(s_sct, NGR * d + NGR * (NB * (layer - 2) + 2))
                dve.tensor_reduce(hb[:, d, :], work_ps[0:BN, 0:3 * D].rearrange("p (k f) -> p f k", f=D), AX.X, ALU.add).then_inc(s_blk, 1)

            def mark_both(layer, k, d):
                mark_src(layer, k, d)
                mark_dst(layer, k, d)

            def block_of(layer, d, first, last):
                for n in range(NGR):
                    if layer == 3:
                        less_high(3, d, n)
                    else:
                        weigh(d, n)
                        if n:
                            less_high(2, d, n - 1)
                        elif not first:
                            less_high(2, d - 1, NGR - 1)
                    if n == 0 and not first:
                        mark_dst(layer, 1, d)
                    if n == 1:
                        mark_src(layer, 2, d)
                    if n == LAG and not first:
                        take_sum(layer, d - 1)
                    if n == LAG + 1:
                        mark_dst(layer, 2, d)
                    if not last:
                        if n == 5:
                            mark_src(layer, 0, d + 1)
                        if n == 7:
                            mark_dst(layer, 0, d + 1)
                        if n == 8:
                            mark_src(layer, 1, d + 1)

            def aggregate(layer):
                mark_both(layer, 0, 0)
                mark_both(layer, 1, 0)
                block_of(layer, 0, True, False)
                with dve.Fori(1, NB - 1) as d:
                    block_of(layer, d, False, False)
                block_of(layer, NB - 1, False, True)
                if layer == 2:
                    less_high(2, NB - 1, NGR - 1)
                take_sum(layer, NB - 1)
                dve.wait_ge(s_blk, NB * (layer + 1) + 2)

            parts_of(Xv)
            dve.wait_ge(s_iota, 8)
            take_slots(0, 0, 16)
            take_slots(1, 1, 16)
            with dve.Fori(1, NB // 2) as i:
                for q in range(2):
                    take_product(0, 2 * i + (q - 2), q)
                    take_slots(2 * i + q, q, 16 * i + 16)
            for d in (NB - 3, NB - 2):
                take_product(0, d, d % 2)
            take_slots(NB - 1, 0, 16 * (NB // 2 + 1))
            take_product(0, NB - 1, 0)
            dve.wait_ge(s_blk, NB + 2)
            st.link(dve.tensor_scalar(rdeg[:, :], rdeg[:, :], 1.0, None, ALU.max))
            st.link(dve.reciprocal(rdeg[:, :], rdeg[:, :]))
            dve.tensor_tensor(hv, Xv, hv, ALU.add).then_inc(s_h, 1)
            dve.wait_ge(s_pe, 1)
            st.link(dve.tensor_tensor(hv, Xv, out2, ALU.add))
            normalise(hv, Xv).then_inc(s_xnew, 1)
            dve.wait_ge(s_xnew, 1)
            parts_of(Xv)
            with dve.Fori(0, NB // 2) as i:
                for q in range(2):
                    take_product(1, 2 * i + q, (q + 1) % 2)
            take_product(1, NB - 1, 1)
            dve.wait_ge(s_blk, 2 * NB + 2)
            dve.sem_inc(s_h, 1)
            dve.wait_ge(s_pe, 2)
            st.link(dve.tensor_tensor(hv, out2, rdeg[:, :].unsqueeze(2).to_broadcast([BN, NB, D]), ALU.mult))
            st.link(dve.tensor_tensor(hv, hv, Xv, ALU.add))
            normalise(hv, Xv).then_inc(s_xnew, 1)
            dve.wait_ge(s_xnew, 2)
            parts_of(Xv)
            aggregate(2)
            st.link(dve.tensor_tensor(hv, Xv, hv, ALU.add))
            st.link(normalise(hv, Xv))
            dve.tensor_tensor(hv, Xv, be_b[0:BN, :].unsqueeze(1).to_broadcast([BN, NB, D]), ALU.add).then_inc(s_xnew, 1)
            dve.wait_ge(s_xnew, 3)
            parts_of(hv)
            dve.wait_ge(s_xp, 4)
            aggregate(3)
            st.link(dve.memset(rT[D:D + 1, :], 1.0))
            st.link(dve.tensor_scalar(stat[:, 0, 0:1], eps_b[0:BN, :], 1.0, None, ALU.add))
            dve.scalar_tensor_tensor(hv, Xv, stat[:, 0, 0:1], hv, ALU.mult, ALU.add).then_inc(s_h, 1)
            last_stage(dve, st, normalise)

        def general_dve(dve, st):
            normalise = normaliser(dve, st)
            dve.memset(eaT[:, :, :], 0.0).then_inc(s_eaT, 1)
            dve.memset(zeros[:, :], 0.0).then_inc(s_const, 1)
            dve.sem_inc(s_eaW, 1)
            dve.sem_inc(s_eaWfree, 1)
            for q in range(2):
                dve.memset(ea[q][:, :], 0.0).then_inc(s_eafree, 1)
                dve.memset(gat[q][:, :, :], 0.0).then_inc(s_gfree, 1)
                dve.memset(part[:, q * G:(q + 1) * G, :, :], 0.0).then_inc(s_pfree, 1)
                dve.memset(hot[q][:, :], 0.0).then_inc(s_hfree, 1)
            dve.wait_ge(s_iota, 8)
            dve.wait_ge(s_eafree, 2)

            def aggregate(layer):
                first = layer * NG
                with dve.Fori(0, NG // 2) as i:
                    for q in range(2):
                        n0 = st.n
                        dve.wait_ge(s_gat[q], 16 * G * i + 16 * G * (layer * NG // 2 + 1))
                        dve.wait_ge(s_pfree, 2 * i + (first + q + 1))
                        m = gat[q][:, :, :]
                        per = 4 + (layer == 2) + 2 * (layer == 3)

                        def dep(ins, k):
                            ins.then_inc(s_dve, 1)
                            dve.wait_ge(s_dve, 2 * per * i + (n0 + q * per + k))

                        k = 1
                        if layer == 2:
                            wg = wgt[:, 2 * i + q, :].unsqueeze(2).to_broadcast([P, G, D])
                            dep(dve.tensor_tensor(m, m, wg, ALU.mult), k)
                            k += 1
                        if layer == 3:
                            dve.wait_ge(s_eaW, 2 * i + (q + 2))
                            dep(dve.tensor_tensor(m, m, work_ps[:, 0:G * D].rearrange("p (j f) -> p j f", f=D), ALU.add), k)
                            k += 1
                            ins = dve.tensor_scalar(m, m, 0.0, None, ALU.max)
                            dep(ins, k)
                            dve.sem_inc(s_eaWfree, 1)
                            k += 1
                        pt = part[:, q * G:(q + 1) * G, :, :]
                        dep(dve.tensor_copy(pt[:, :, 0, :], m), k)
                        dep(dve.tensor_tensor(m, m, pt[:, :, 0, :], ALU.subtract), k + 1)
                        dep(dve.tensor_copy(pt[:, :, 1, :], m), k + 2)
                        dep(dve.tensor_tensor(m, m, pt[:, :, 1, :], ALU.subtract), k + 3)
                        dve.tensor_copy(pt[:, :, 2, :], m).then_inc(s_part, 1)
                        dve.wait_ge(s_part, 2 * i + (first + q + 1))
                        dve.sem_inc(s_gfree, 1)
                        for j in range(G):
                            dve.wait_ge(s_hfree, 2 * G * i + ((first + q) * G + j + 1))
                            dve.tensor_scalar(hot[j % 2][:, :], node_no[:, :], dst_f[:, bass.ds(2 * G * i + (q * G + j), 1)],
                                              None, ALU.is_equal).then_inc(s_hot, 1)
                st.n += (NG // 2) * 2 * per

            aggregate(0)
            dve.wait_ge(s_agg, 1)
            st.link(dve.tensor_scalar(rdeg[:, :], deg, 1.0, None, ALU.max))
            st.link(dve.reciprocal(rdeg[:, :], rdeg[:, :]))
            dve.tensor_tensor(hv, Xv, agg, ALU.add).then_inc(s_h, 1)
            dve.wait_ge(s_pe, 1)
            st.link(dve.tensor_tensor(hv, Xv, out2, ALU.add))
            dve.sem_inc(s_aggfree, 1)
            normalise(hv, Xv).then_inc(s_xnew, 1)
            dve.wait_ge(s_xnew, 1)
            aggregate(1)
            dve.wait_ge(s_agg, 2)
            dve.tensor_copy(hv, agg).then_inc(s_h, 1)
            dve.wait_ge(s_pe, 2)
            st.link(dve.tensor_tensor(hv, out2, rdeg[:, :].unsqueeze(2).to_broadcast([BN, NB, D]), ALU.mult))
            dve.sem_inc(s_aggfree, 1)
            st.link(dve.tensor_tensor(hv, hv, Xv, ALU.add))
            dve.wait_ge(s_tab, 16)
            normalise(hv, Xv).then_inc(s_xnew, 1)
            dve.wait_ge(s_xnew, 2)
            aggregate(2)
            dve.wait_ge(s_agg, 3)
            st.link(dve.tensor_tensor(hv, Xv, agg, ALU.add))
            dve.sem_inc(s_aggfree, 1)
            dve.wait_ge(s_tab, 32)
            st.link(normalise(hv, Xv))
            dve.tensor_tensor(hv, Xv, be_b[0:BN, :].unsqueeze(1).to_broadcast([BN, NB, D]), ALU.add).then_inc(s_xnew, 1)
            aggregate(3)
            dve.wait_ge(s_agg, 4)
            dve.wait_ge(s_tab, 48)
            st.link(dve.tensor_scalar(stat[:, 0, 0:1], eps_b[0:BN, :], 1.0, None, ALU.add))
            dve.scalar_tensor_tensor(hv, Xv, stat[:, 0, 0:1], agg, ALU.mult, ALU.add).then_inc(s_h, 1)
            last_stage(dve, st, normalise)

        @block.vector
        def _(dve):
            st = Step(dve, s_dve)
            dve.memset(blank[:, :], 0.0).then_inc(s_blank, 1)
            dve.memset(ones[:, :], 1.0).then_inc(s_const, 1)
            dve.memset(we4[:, :, :], 0.0).then_inc(s_const, 1)
            dve.memset(we3[:, :, :], 0.0).then_inc(s_const, 1)
            dve.memset(minus2[:, :], -2.0).then_inc(s_const, 1)
            dve.memset(ones32[:, :], 1.0).then_inc(s_const, 1)
            for q in range(2):
                dve.memset(efeat[q][:, :, :], 0.0).then_inc(s_efused, 1)
                dve.memset(junk[q][:, :], 0.0).then_inc(s_wused, 1)
            dve.memset(gates[:, :], 0.0).then_inc(s_acc, 1)
            dve.memset(rjunk[:, :, :], 0.0)
            dve.sem_inc(s_rin, 4)
            st.link(dve.memset(placed[:, :], 0.0))
            st.link(dve.memset(keep[:, :, :], 1.0))
            st.link(dve.memset(keep[:, :, 0:1], 0.0))
            st.link(dve.memset(hist[:, :, :], 0.0))
            dve.wait_ge(s_iota, 7)
            dve.tensor_copy(ident16[:, :], ident[:, :]).then_inc(s_const, 1)
            dve.wait_ge(s_const, 6)

            dve.wait_ge(s_edges, 16 * 9)
            flat_src = src_i[:, :, :].rearrange("p g j -> p (g j)")
            flat_dst = dst_i[:, :, :].rearrange("p g j -> p (g j)")
            t0, t1 = base[:, :], pay[0][:, :, :].rearrange("p j w -> p (j w)")[:, 0:COLS]
            for flat, blk, low, plus in ((flat_src, sblk, slo, 0.0), (flat_dst, dblk, dlo1, 1.0)):
                st.link(dve.tensor_scalar(t0, flat, 1.0 / BN, 0.5 / BN - 0.5, ALU.mult, ALU.add))
                st.link(dve.tensor_scalar(t0, t0, MAGIC, MAGIC, ALU.add, ALU.subtract))
                st.link(dve.tensor_copy(blk[:, :], t0))
                st.link(dve.tensor_scalar(t0, t0, -float(BN), plus, ALU.mult, ALU.add))
                st.link(dve.tensor_copy(t1, flat))
                st.link(dve.tensor_tensor(low[:, :], t0, t1, ALU.add))
            st.link(dve.tensor_scalar(cap[:, :], t1, 0.0, None, ALU.is_ge))
            st.link(dve.tensor_tensor(t1, sblk[:, :], dblk[:, :], ALU.subtract))
            st.link(dve.tensor_scalar(t0, t1, 0.0, None, ALU.is_lt))
            st.link(dve.scalar_tensor_tensor(t1, t0, float(NB), t1, ALU.mult, ALU.add))
            st.link(dve.tensor_scalar(t0, t1, 0.0, None, ALU.is_gt))
            st.link(dve.scalar_tensor_tensor(t1, t1, 2.0, t0, ALU.mult, ALU.add))
            st.link(dve.tensor_scalar(t0, t0, -float(P), 3.0 * P, ALU.mult, ALU.add))
            st.link(dve.tensor_tensor(cap[:, :], cap[:, :], t0, ALU.mult))
            st.link(dve.scalar_tensor_tensor(base[:, :], dblk[:, :], float(SLOTS), t1, ALU.mult, ALU.add))
            st.link(dve.tensor_scalar(dst_f, flat_dst, float(MID), None, ALU.subtract))
            for q in range(2):
                st.link(dve.memset(pay[q][:, :, :], 0.0))
            dve.wait_ge(s_vec, 32)

            os_ = mark25[:, :, NB:2 * NB]
            sel = work_ps[:, 0:1024].rearrange("p (h c) -> p h c", c=512)[:, :, 0:G // 2 * NB]

            def mark_group(g):
                cols = bass.ds(G * g, G)
                dve.wait_ge(s_sel, g + 1)
                nos = no25[:, :].unsqueeze(1).to_broadcast([P, G, NB])
                dve.tensor_tensor(mark25[:, :, 0:NB], nos, dblk[:, cols].unsqueeze(2).to_broadcast([P, G, NB]), ALU.is_equal)
                dve.tensor_tensor(os_, nos, sblk[:, cols].unsqueeze(2).to_broadcast([P, G, NB]), ALU.is_equal).then_inc(s_mark, 1)

            def count_upto(g):
                dve.wait_ge(s_hist, 2 * g + 2)
                dve.tensor_tensor_scan(upto[:, :, :].rearrange("d s c -> d (s c)"), keep[:, :, :].rearrange("d s c -> d (s c)"),
                                       hist[:, :, :].rearrange("d s c -> d (s c)"), 0.0, ALU.mult, ALU.add).then_inc(s_scan, 1)
                dve.wait_ge(s_scan, g + 1)
                dve.tensor_scalar(upto16[:, :, :].rearrange("d c s -> d s c"), upto[:, :, 0:G], 2000.0, None, ALU.min).then_inc(s_upto, 1)
                dve.tensor_copy(hist[:, :, 0:1], upto[:, :, G:G + 1]).then_inc(s_carry, 1)

            def place(g, q, i2):
                cols = bass.ds(G * g, G)

                def dep(ins, k):
                    ins.then_inc(s_place, 1)
                    dve.wait_ge(s_place, PL * g + (k + 1))

                dve.wait_ge(s_sel, g + 2)
                dve.wait_ge(s_rin, G * g + (G + 4))
                r, m, hi, t, f = (rank[:, k, :] for k in range(5))
                for h in range(2):
                    half = rsel[:, h * (G // 2):(h + 1) * (G // 2), :]
                    dep(dve.tensor_tensor(half, sel[:, h, :].rearrange("p (c s) -> p c s", s=NB),
                                          mark25[:, h * (G // 2):(h + 1) * (G // 2), NB:2 * NB], ALU.mult), h)
                dep(dve.tensor_reduce(r, rsel[:, :, :], AX.X, ALU.add), 2)
                dep(dve.tensor_tensor(r, r, rank_in[:, :], ALU.add), 3)
                dep(dve.tensor_tensor(m, r, cap[:, cols], ALU.is_lt), 4)
                dep(dve.tensor_tensor(placed[:, :], placed[:, :], m, ALU.add), 5)
                dep(dve.tensor_scalar(hi, r, float(P), None, ALU.is_ge), 6)
                dep(dve.tensor_scalar(t, r, 2.0 * P, None, ALU.is_ge), 7)
                dep(dve.tensor_tensor(hi, hi, t, ALU.add), 8)
                dep(dve.scalar_tensor_tensor(t, r, float(CH), base[:, cols], ALU.mult, ALU.add), 9)
                dep(dve.scalar_tensor_tensor(t, hi, 1.0 - CH * P, t, ALU.mult, ALU.add), 10)
                dep(dve.tensor_tensor(f, t, dump[:, :], ALU.subtract), 11)
                dep(dve.tensor_tensor(f, f, m, ALU.mult), 12)
                if i2 is not None:
                    dve.wait_ge(s_placed[q], i2)
                dep(dve.tensor_tensor(pos[q][:, :], f, dump[:, :], ALU.add), 13)
                dep(dve.tensor_scalar(dump[:, :], dump[:, :], float(G), None, ALU.add), 14)
                dve.wait_ge(s_ef[q], 8 * g + (16 - 8 * q))
                dve.tensor_copy(pay[q][:, :, 0:ED], efeat[q][:, :, :]).then_inc(s_efused, 1)
                dep(dve.tensor_copy(pay[q][:, :, ED], slo[:, cols]), 15)
                dep(dve.tensor_copy(pay[q][:, :, ED + 1], dlo1[:, cols]), 16)
                dve.tensor_copy(pay[q][:, :, ED + 2], wgt[:, g, :]).then_inc(s_pos, 1)

            PL = 17

            def tiles(m, step, ks):
                for k in ks:
                    if k == 0:
                        dve.wait_ge(s_acc, step + (m * STEPS + 1))
                    dve.wait_ge(s_w[k], 16 * step + 16 * (m * STEPS + 1))
                    dve.wait_ge(s_wused, RING * step + (m * TILES + k + 1))
                    dve.tensor_tensor_reduce(out=junk[k % 2][:, 0:H], in0=w_tile[k][:, :], in1=vec[m][:, :],
                                             scale=1.0, scalar=0.0, op0=ALU.mult, op1=ALU.add,
                                             accum_out=acc[:, k:k + 1]).then_inc(s_wused, 1)
                    if k == RING - 1:
                        dve.wait_ge(s_wused, RING * step + (m * TILES + RING + 2))
                        dve.tensor_copy(gates[:, bass.ds(RING * step + m * TILES, RING)], acc[:, :]).then_inc(s_acc, 1)

            dve.sem_inc(s_sel, 1)
            dve.sem_inc(s_pos, 1)
            dve.sem_inc(s_carry, 1)
            dve.sem_inc(s_curT, 1)

            for g in range(2):
                mark_group(g)
                count_upto(g)
                place(g, g, None)

            def sort_and_multiply(m, i, early):
                for q in range(2):
                    step = 2 * i + q
                    g = 2 * i + (m * STEPS + q + 2)
                    mark_group(g)
                    tiles(m, step, range(0, early // 2))
                    count_upto(g)
                    tiles(m, step, range(early // 2, early))
                    place(g, q, 16 * G * i + 16 * G * (m * STEPS // 2 + 1))
                    tiles(m, step, range(early, RING))

            with dve.Fori(0, STEPS // 2) as i:
                sort_and_multiply(0, i, 4)
            with dve.Fori(0, STEPS // 2 - 1) as i:
                sort_and_multiply(1, i, 4)
            sort_and_multiply(1, STEPS // 2 - 1, 2)
            dve.wait_ge(s_acc, 2 * STEPS + 1)
            dve.memset(rT[D:D + 1, :], 1.0).then_inc(s_const, 1)
            dve.wait_ge(s_const, 7)
            dve.sem_inc(s_cell, 1)
            st.link(dve.tensor_reduce(count[:, :], placed[:, :], AX.X, ALU.add))
            dve.sem_inc(s_cnt, 1)
            dve.wait_ge(s_tot, 1)
            dve.tensor_scalar(flag[:, :], work_ps[0:1, 1024:1025], float(E), None, ALU.is_equal).then_inc(s_flag, 1)
            st.link(dve.memset(spread[:, :, :, :], 0.0))
            for k in range(2):
                st.link(dve.tensor_copy(spread[:, k, :, k], ident[0:GT, 0:GT]))
            tg = work_ps[0:GT, 0:6 * P].rearrange("t (m g p) -> t m g p", m=2, g=3)
            dve.wait_ge(s_cellT, 1)
            dve.wait_ge(s_small, 16 * N_SMALL)
            gi = cell[:, 0:3, :]
            gh = cell[:, 3:6, :]
            st.link(dve.tensor_tensor(gi, tg[:, 0, :, :], bias_g[:, 0, :, :], ALU.add))
            st.link(dve.tensor_tensor(gh, tg[:, 1, :, :], bias_g[:, 1, :, :], ALU.add))
            dve.tensor_tensor(cell[:, 0:2, :], cell[:, 0:2, :], cell[:, 3:5, :], ALU.add).then_inc(s_cd, 1)
            dve.wait_ge(s_ca, 1)
            st.link(dve.tensor_tensor(cell[:, 5, :], cell[:, 0, :], cell[:, 5, :], ALU.mult))
            dve.tensor_tensor(cell[:, 2, :], cell[:, 2, :], cell[:, 5, :], ALU.add).then_inc(s_cd, 1)
            dve.wait_ge(s_ca, 2)
            st.link(dve.tensor_scalar(cell[:, 3, :], cell[:, 1, :], -1.0, 1.0, ALU.mult, ALU.add))
            st.link(dve.tensor_tensor(cell[:, 3, :], cell[:, 3, :], cell[:, 2, :], ALU.mult))
            st.link(dve.tensor_tensor(cell[:, 4, :], cell[:, 1, :], gc_g[:, :], ALU.mult))
            dve.tensor_tensor(newRT[:, :], cell[:, 3, :], cell[:, 4, :], ALU.add).then_inc(s_cd, 1)
            dve.wait_ge(s_nw, 1)
            dve.tensor_copy(new_w[:, :], work_ps[0:D, 0:D]).then_inc(s_cd, 1)
            dve.wait_ge(s_nw, 2)
            dve.tensor_copy(w1T[:, :], work_ps[0:D, D:2 * D]).then_inc(s_cd, 1)
            dve.tensor_copy(w2T[0:D, :], work_ps[0:D, 2 * D:3 * D]).then_inc(s_cd, 1)
            dve.wait_ge(s_x, 16)
            dve.wait_ge(s_flag, 1)
            fits = dve.value_load(flag[0:1, 0:1], min_val=0, max_val=1)
            n0 = st.n
            with dve.If(fits == 1):
                fast_dve(dve, st)
            st.n = n0
            with dve.Else():
                general_dve(dve, st)

        def node_act(act):
            tp, std = [0], [0]

            def copy_hT():
                for c in range(NC7):
                    w = min(NT, N - c * NT)
                    tp[0] += 1
                    act.wait_ge(s_tp, tp[0])
                    act.activation(hT[:, c * NT:c * NT + w], work_ps[0:D, 512 * (c % 2):512 * (c % 2) + w], ACT.Copy).then_inc(s_ev, 1)

            def relu_rT(col):
                for c in range(NC7):
                    w = min(NT, N - c * NT)
                    tp[0] += 1
                    act.wait_ge(s_tp, tp[0])
                    act.activation(rT[0:D, c * NT:c * NT + w], work_ps[0:D, 1024 + 512 * (c % 2):1024 + 512 * (c % 2) + w],
                                   ACT.Relu, bias=b1[:, col:col + 1]).then_inc(s_ev, 1)

            def deviation():
                std[0] += 1
                act.wait_ge(s_var, std[0])
                act.activation(stat[:, 3, :], stat[:, 2, :], ACT.Sqrt).then_inc(s_std, 1)

            return copy_hT, relu_rT, deviation

        def fast_act(act):
            copy_hT, relu_rT, deviation = node_act(act)
            act.wait_ge(s_cell, 1)

            def copy_quads(d, q):
                act.wait_ge(s_prod, d + 1)
                for n, (a, b) in enumerate(QUADS):
                    act.wait_ge(s_built, NQ * d + (n + 1 + NQ))
                    if n == 0:
                        act.wait_ge(s_astore[q], 8 * d + (16 - 8 * q))
                    act.activation(adj[q][:, a:b, :].rearrange("p b n -> p (b n)"),
                                   agg_ps[0:BN, 512 * (n % 4):512 * (n % 4) + (b - a) * BN], ACT.Copy).then_inc(s_adj, 1)
                    if n == 3:
                        act.wait_ge(s_curtp, d + 2)
                        act.activation(curT[:, d, :], work_ps[0:CH, 1024:1024 + P], ACT.Copy).then_inc(s_curT, 1)

            def take_messages(layer):
                def block_of(d, first):
                    if layer == 3:
                        copy_slots(d, 0)
                    for n, (k, c0, c1) in enumerate(GROUPS):
                        w = c1 - c0
                        m = NGR * NB * (layer - 2) + n
                        if layer == 3 and n + 1 < NGR:
                            copy_slots(d, n + 1)
                        if layer == 2:
                            act.wait_ge(s_weighed, NGR * d + (n + 1 + BUFS))
                            act.wait_ge(s_sct, NGR * d + (m + 1))
                            act.activation(views(n)[2][:, 0:w, 0:D], views(n)[1], ACT.Copy).then_inc(s_hi, 1)
                        else:
                            act.wait_ge(s_gps, NGR * d + (m + 1))
                            act.wait_ge(s_sct, NGR * d + (m + 1))
                            ps = agg_ps[:, 512 * (n % BUFS):512 * (n % BUFS) + w * D]
                            act.activation(msg[n][:, 0:w, 0:D], ps.rearrange("p (j f) -> p j f", f=D), ACT.Relu).then_inc(s_hi, 1)
                        if n:
                            middle_part(layer, d, n - 1)
                        elif not first:
                            middle_part(layer, d - 1, NGR - 1)

                block_of(0, True)
                with act.Fori(1, NB) as d:
                    block_of(d, False)
                middle_part(layer, NB - 1, NGR - 1)

            def middle_part(layer, d, n):
                act.wait_ge(s_split, NGR * d + (NGR * NB * (layer - 2) + n + 1 + BUFS))
                w = GROUPS[n][2] - GROUPS[n][1]
                act.activation(msg[n][:, 0:w, D:2 * D], msg32[n][:, 0:w * D].rearrange("p (j f) -> p j f", f=D), ACT.Copy).then_inc(s_mid, 1)

            def copy_slots(d, n):
                k, c0, c1 = GROUPS[n]
                act.wait_ge(s_stp, NGR * d + (n + 1))
                w = (c1 - c0) // TW * P
                act.activation(slotT[n % 2][0:TW * ROW, 0:w], work_ps[0:TW * ROW, 512 * (1 + n % 2):512 * (1 + n % 2) + w], ACT.Copy).then_inc(s_sT, 1)

            with act.Fori(0, NB // 2) as i:
                for q in range(2):
                    copy_quads(2 * i + q, q)
            copy_quads(NB - 1, 0)
            copy_hT()
            relu_rT(0)
            deviation()
            copy_hT()
            deviation()
            take_messages(2)
            deviation()
            take_messages(3)
            copy_hT()
            relu_rT(1)
            deviation()
            deviation()

        def general_act(act):
            copy_hT, relu_rT, deviation = node_act(act)
            copy_hT()
            relu_rT(0)
            deviation()
            copy_hT()
            deviation()
            deviation()
            with act.Fori(0, NG) as g:
                act.wait_ge(s_eaW, g + 1)
                for h, (k0, k1) in enumerate(HALVES):
                    act.wait_ge(s_gtp, 2 * g + (h + 1))
                    act.activation(eaT[:, k0:k1, :], work_ps[:, 1536:1536 + P * (k1 - k0)].rearrange("p (k e) -> p k e", e=P),
                                   ACT.Copy).then_inc(s_eaT, 1)
            copy_hT()
            relu_rT(1)
            deviation()
            deviation()

        @block.scalar
        def _(act):
            act.wait_ge(s_blank, 1)
            ninth = CH * ROW // 9
            for d in range(NB):
                act.dma_start(block_slots[d].rearrange("p (a w) -> p a w", w=ninth),
                              blank[:, :].unsqueeze(1).to_broadcast([P, 9, ninth])).then_inc(s_init, 16)

            def load_features(g, q):
                act.wait_ge(s_efused, g + 1)
                act.dma_start(efeat[q][:, :, :].rearrange("p j c -> p (j c)"), ea_rows[g]).then_inc(s_ef[q], 16)

            for q in range(2):
                load_features(q, q)
            act.wait_ge(s_const, 6)

            def sort_group(g, loads):
                q = loads[1]
                act.wait_ge(s_mtp, g + 1)
                act.wait_ge(s_sel, g + 1)
                act.activation(markT[:, :, :].rearrange("k j e -> k (j e)"), agg_ps[0:2 * NB, 0:G * P // 2].bitcast(fp16), ACT.Copy).then_inc(s_mT, 1)
                act.wait_ge(s_hps, g + 1)
                act.wait_ge(s_carry, g + 1)
                for h in range(2):
                    act.activation(hist[:, :, 1 + h * (G // 2):1 + (h + 1) * (G // 2)].rearrange("d s c -> d c s"),
                                   work_ps[0:NB, 512 * h:512 * h + G // 2 * NB].rearrange("d (c s) -> d c s", s=NB), ACT.Copy).then_inc(s_hist, 1)
                act.wait_ge(s_pos, g + 1)
                for j in range(G):
                    if j % 4 == 0:
                        act.wait_ge(s_same, (G // 4) * g + (j // 4 + 1))
                    act.wait_ge(s_rin, G * g + (j + 1))
                    act.activation(rjunk[:, j % 4, :], same_ps(j), ACT.Relu, bias=minus2[:, :],
                                   accum_out=rank_in[:, j:j + 1]).then_inc(s_rin, 1)
                if loads[0] is not None:
                    load_features(loads[0], q)

            with act.Fori(0, NG // 2 - 2) as i:
                for q in range(2):
                    sort_group(2 * i + q, (2 * i + q + 2, q))
            sort_group(NG - 4, (NG - 2, 0))
            sort_group(NG - 3, (None, 1))
            full = (NG - 1) * P * G
            act.wait_ge(s_efused, NG)
            act.dma_start(efeat[1][TP:TP + 1, :, :].rearrange("p j c -> p (j c)")[:, 0:TR * ED],
                          row(edge_attr_32[full + TP * G:E, :].rearrange("e c -> (e c)"))).then_inc(s_eftail, 16)
            act.wait_ge(s_eftail, 16)
            act.dma_start(efeat[1][0:TP, :, :].rearrange("p j c -> p (j c)"),
                          edge_attr_32[full:full + TP * G, :].rearrange("(p j) c -> p (j c)", j=G)).then_inc(s_ef[1], 16)
            sort_group(NG - 2, (None, 0))
            sort_group(NG - 1, (None, 1))
            act.wait_ge(s_cd, 1)
            act.activation(cell[:, 0:2, :], cell[:, 0:2, :], ACT.Sigmoid).then_inc(s_ca, 1)
            act.wait_ge(s_cd, 2)
            act.activation(cell[:, 2, :], cell[:, 2, :], ACT.Tanh).then_inc(s_ca, 1)
            act.wait_ge(s_flag, 1)
            fits = act.value_load(flag[0:1, 0:1], min_val=0, max_val=1)
            with act.If(fits == 1):
                fast_act(act)
            with act.Else():
                general_act(act)

        def node_pe(pe):
            def transposed(evs):
                for c in range(NC7):
                    if c >= 2:
                        pe.wait_ge(s_ev, evs + c - 1)
                    for b in range(4 * c, min(4 * c + 4, NB)):
                        last = pe.transpose(work_ps[0:D, 512 * (c % 2) + BN * (b % 4):512 * (c % 2) + BN * (b % 4 + 1)],
                                            hb[:, b, :], ident[0:BN, 0:BN])
                    last.then_inc(s_tp, 1)

            def two_products(evs, w_first, w_second):
                for c in range(NC7):
                    w = min(NT, N - c * NT)
                    pe.wait_ge(s_ev, evs + max(c + 1, NC7 + c - 1 if c >= 2 else 0))
                    pe.matmul(work_ps[0:D, 1024 + 512 * (c % 2):1024 + 512 * (c % 2) + w], w_first, hT[:, c * NT:c * NT + w],
                              start=True, stop=True).then_inc(s_tp, 1)
                pe.wait_ge(s_ev, evs + 2 * NC7)
                for b in range(NB):
                    last = pe.matmul(agg_ps[0:BN, b * D:(b + 1) * D], rT[:, b * BN:(b + 1) * BN], w_second, start=True, stop=True)
                last.then_inc(s_pe, 1)

            def one_product(evs):
                pe.wait_ge(s_ev, evs + NC7)
                for b in range(NB):
                    last = pe.matmul(agg_ps[0:BN, b * D:(b + 1) * D], hT[:, b * BN:(b + 1) * BN], new_w[:, :], start=True, stop=True)
                last.then_inc(s_pe, 1)

            return transposed, two_products, one_product

        def fast_pe(pe):
            transposed, two_products, one_product = node_pe(pe)

            def build(d, n):
                if n == 0 or QSEC[n - 1] != QSEC[n]:
                    pe.wait_ge(s_mark0, 3 * d + (QSEC[n] + 1))
                last_in_bank = [m for m in range(NQ) if m % 4 == n % 4][-1]
                pe.wait_ge(s_adj, NQ * d + (n - 3 + NQ if n >= 4 else last_in_bank + 1))
                (a, b), (c0, c1) = QUADS[n], QCH[n]
                for c in range(c0, c1):
                    s = source_of(c)
                    first = c == 0 or source_of(c - 1) != s
                    final = c == CH - 1 or source_of(c + 1) != s
                    at = 512 * (n % 4) + BN * (s - a)
                    last = pe.matmul(agg_ps[0:BN, at:at + BN], mark_of(src_mark, c), mark_of(dst_mark, c), start=first, stop=final)
                last.then_inc(s_built, 1)

            def products(layer, d, n, buf, q):
                if layer == 0:
                    pe.wait_ge(s_adj, NQ * d + (n + 1 + NQ))
                if n == 0:
                    pe.wait_ge(s_blk, d + (NB * layer + 1))
                for s in range(*QUADS[n]):
                    last = pe.matmul(work_ps[0:BN, 512 * q:512 * q + MS - 1], adj[buf][:, s, :], x_part[:, d + s, 0:MS - 1],
                                     start=(s == 0), stop=(s == NB - 1))
                if n == NQ - 1:
                    last.then_inc(s_prod, 1)

            def block_of_layer0(d, q):
                for n in range(NQ):
                    build(d, n)
                    if n == 1:
                        pe.wait_ge(s_curT, d + 1)
                        pe.sem_inc(s_pe_pass, 1)
                        pe.transpose(work_ps[0:CH, 1024:1024 + P], cur[:, :], ident[:, :]).then_inc(s_curtp, 1)
                    if n >= 2:
                        products(0, d, n - 2, q, q)
                for n in (NQ - 2, NQ - 1):
                    products(0, d, n, q, q)

            def transpose_slots(d, n):
                k, c0, c1 = GROUPS[n]
                if n == 0 or GROUPS[n - 1][0] != k:
                    pe.wait_ge(s_slot[k], 16 * d + 16)
                for h in range((c1 - c0) // TW):
                    at = 512 * (1 + n % 2) + P * h
                    last = pe.transpose(work_ps[0:TW * ROW, at:at + P],
                                        slot_row[:, c0 + TW * h:c0 + TW * (h + 1), :].rearrange("p c w -> p (c w)"), ident[:, :])
                last.then_inc(s_stp, 1)

            def gather(layer, d, n):
                k, c0, c1 = GROUPS[n]
                if n == 0 or GROUPS[n - 1][0] != k:
                    pe.wait_ge(s_sec, 6 * d + (6 * NB * (layer - 2) + 2 * k + 1))
                if layer == 2:
                    pe.wait_ge(s_weighed, NGR * d + (n + 1))
                else:
                    pe.wait_ge(s_split, NGR * d + (NGR * NB + n + 1))
                at = 512 * (n % BUFS)
                if layer == 3:
                    pe.wait_ge(s_sT, NGR * d + (n + 1))
                for c in range(c0, c1):
                    mark = src_mark[0:BN, c * P:(c + 1) * P]
                    b = d + source_of(c)
                    j = c - c0
                    if layer == 3 and j % TW == 0:
                        h = j // TW
                        pe.matmul(agg_ps[:, at + TW * D * h:at + TW * D * (h + 1)], slotT[n % 2][0:TW * ROW, P * h:P * (h + 1)],
                                  we3[:, :, :].rearrange("p a f -> p (a f)"), start=True, stop=False, skip_group_check=True)
                    for part_no in range(3):
                        last = pe.matmul(agg_ps[:, at + j * D:at + (j + 1) * D], mark, x_part[:, b, part_no * D:(part_no + 1) * D],
                                         start=(part_no == 0 and layer == 2), stop=(part_no == 2), skip_group_check=True)
                last.then_inc(s_gps, 1)

            def scatter(layer, d, n):
                k, c0, c1 = GROUPS[n]
                if n == 0:
                    pe.wait_ge(s_blk, d + (NB * layer + 2))
                if n == 0 or GROUPS[n - 1][0] != k:
                    pe.wait_ge(s_sec, 6 * d + (6 * NB * (layer - 2) + 2 * k + 2))
                pe.wait_ge(s_msg, NGR * d + (NGR * NB * (layer - 2) + n + 1 + NGR))
                for c in range(c0, c1):
                    first, final = c == 0, c == CH - 1
                    last = pe.matmul(work_ps[0:BN, 0:3 * D], mark_of(dst_mark, c), msg[n][:, c - c0, :], start=first, stop=final)
                last.then_inc(s_sct, 1)

            def aggregate(layer):
                pe.wait_ge(s_xp, layer + 1)

                def block_of(d, first):
                    if layer == 3:
                        transpose_slots(d, 0)
                    for n in range(NGR):
                        if layer == 3 and n + 1 < NGR:
                            transpose_slots(d, n + 1)
                        gather(layer, d, n)
                        if n >= LAG:
                            scatter(layer, d, n - LAG)
                        elif not first:
                            scatter(layer, d - 1, n + NGR - LAG)

                block_of(0, True)
                with pe.Fori(1, NB) as d:
                    block_of(d, False)
                for n in range(NGR - LAG, NGR):
                    scatter(layer, NB - 1, n)

            pe.wait_ge(s_xp, 1)
            with pe.Fori(0, NB // 2) as i:
                for q in range(2):
                    block_of_layer0(2 * i + q, q)
            block_of_layer0(NB - 1, 0)
            pe.wait_ge(s_h, 1)
            transposed(0)
            two_products(0, w1T[:, :], w2T[:, :])
            pe.wait_ge(s_xp, 2)
            with pe.Fori(0, NB // ABUF) as i:
                for k in range(ABUF):
                    pe.wait_ge(s_aload[k], 16 * i + 16)
                    for n in range(NQ):
                        products(1, ABUF * i + k, n, k, (k + 1) % 2)
            for d in range(NB // ABUF * ABUF, NB):
                pe.wait_ge(s_aload[d % ABUF], 16 * (d // ABUF + 1))
                for n in range(NQ):
                    products(1, d, n, d % ABUF, (d + 1) % 2)
            pe.wait_ge(s_h, 2)
            transposed(2 * NC7)
            one_product(2 * NC7)
            aggregate(2)
            aggregate(3)
            pe.wait_ge(s_h, 3)
            transposed(3 * NC7)
            two_products(3 * NC7, w1c[:, :], w2c[:, :])

        def general_pe(pe):
            transposed, two_products, one_product = node_pe(pe)
            pe.wait_ge(s_const, 8)

            def aggregate(layer):
                if layer:
                    pe.wait_ge(s_aggfree, layer)
                for k in range(4):
                    pe.matmul(agg_ps[:, 512 * k:512 * (k + 1)], zeros[:, 0:P], zeros[:, :], start=True, stop=False, skip_group_check=True)
                first = layer * NG

                def edge_products(g, q):
                    pe.wait_ge(s_ea[q], 16 * g[0] + 16)
                    for h, (k0, k1) in enumerate(HALVES):
                        pe.wait_ge(s_eaT, 2 * g[1] + (h + 1))
                        for k in range(k0, k1):
                            last = pe.transpose(work_ps[:, 1536 + P * (k - k0):1536 + P * (k - k0 + 1)], ea[q][:, k * P:(k + 1) * P], ident[:, :])
                        last.then_inc(s_gtp, 1)

                with pe.Fori(0, NG // 2) as i:
                    for q in range(2):
                        if layer == 3:
                            edge_products((i, 2 * i + q), q)
                            pe.wait_ge(s_eaWfree, 2 * i + (q + 1))
                            pe.wait_ge(s_eaT, 4 * i + (2 * q + 3))
                            for k in range(G // 4):
                                last = pe.matmul(work_ps[:, 256 * k:256 * (k + 1)], eaT[:, k, :],
                                                 we4[:, :, :].rearrange("p a f -> p (a f)"), start=True, stop=True)
                            last.then_inc(s_eaW, 1)
                            pe.wait_ge(s_eaW, 2 * i + (q + 2))
                            pe.sem_inc(s_eafree, 1)
                        with pe.Fori(0, G // 2) as c:
                            for u in range(2):
                                pe.wait_ge(s_hot, 2 * G * i + 2 * c + ((first + q) * G + u + 1))
                                for b in range(NB):
                                    mark = hot[u][:, b * BN:(b + 1) * BN]
                                    for k in range(3):
                                        last = pe.matmul(agg_ps[0:BN, b * D:(b + 1) * D], mark, part[:, 2 * c + (q * G + u), k, :],
                                                         start=False, stop=False, skip_group_check=True)
                                    if layer == 0:
                                        last = pe.matmul(agg_ps[0:BN, NB * D + b:NB * D + b + 1], mark, ones[:, :],
                                                         start=False, stop=False, skip_group_check=True)
                                last.then_inc(s_hfree, 1)
                        pe.wait_ge(s_hfree, 2 * G * i + ((first + q + 1) * G + 2))
                        pe.sem_inc(s_pfree, 1)
                pe.wait_ge(s_hfree, (layer + 1) * NG * G + 2)
                pe.sem_inc(s_agg, 1)

            aggregate(0)
            pe.wait_ge(s_h, 1)
            transposed(0)
            two_products(0, w1T[:, :], w2T[:, :])
            aggregate(1)
            pe.wait_ge(s_h, 2)
            transposed(2 * NC7)
            one_product(2 * NC7)
            aggregate(2)
            aggregate(3)
            pe.wait_ge(s_h, 3)
            transposed(3 * NC7)
            two_products(3 * NC7, w1c[:, :], w2c[:, :])

        @block.tensor
        def _(pe):
            pe.wait_ge(s_const, 6)
            tps = agg_ps[0:2 * NB, 0:G * P // 2].bitcast(fp16)

            def sort_group(g, first):
                pe.wait_ge(s_mark, g + 1)
                if not first:
                    pe.wait_ge(s_mT, g)
                pe.sem_inc(s_pe_pass, 1)
                for j in range(G):
                    last = pe.transpose(tps[:, j * P:(j + 1) * P], mark25[:, j, :], ident16[:, :])
                last.then_inc(s_mtp, 1)
                pe.wait_ge(s_pos, g + 1)
                for j in range(G):
                    last = pe.matmul(work_ps[0:NB, 512 * (j // 12) + NB * (j % 12):512 * (j // 12) + NB * (j % 12 + 1)],
                                     mark25[:, j, 0:NB], mark25[:, j, NB:2 * NB], start=True, stop=True)
                last.then_inc(s_hps, 1)
                pe.wait_ge(s_mT, g + 1)
                for b in range(G // 4):
                    if b >= 2:
                        pe.wait_ge(s_rin, G * g + (4 * (b - 1) + 4))
                    else:
                        pe.wait_ge(s_rin, G * g + 4)
                    bank = work_ps[:, 1024 + 512 * (b % 2):1024 + 512 * (b % 2) + 512]
                    pe.matmul(bank, ident16[:, :], before[:, :].unsqueeze(1).to_broadcast([P, 4, P]), start=True, stop=False)
                    for j in range(4):
                        last = pe.matmul(bank[:, j * P:(j + 1) * P], markT[:, 4 * b + j, :], markT[:, 4 * b + j, :], start=False, stop=(j == 3))
                    last.then_inc(s_same, 1)
                pe.wait_ge(s_upto, g + 1)
                pe.wait_ge(s_hist, 2 * g + 2)
                for j in range(G):
                    last = pe.matmul(work_ps[:, 512 * (j // 12) + NB * (j % 12):512 * (j // 12) + NB * (j % 12 + 1)],
                                     markT[0:NB, j, :], upto16[:, j, :], start=True, stop=True)
                last.then_inc(s_sel, 1)

            sort_group(0, True)
            with pe.Fori(1, NG) as g:
                sort_group(g, False)
            pe.wait_ge(s_cnt, 1)
            pe.matmul(work_ps[0:1, 1024:1025], count[:, :], ones32[:, :], start=True, stop=True).then_inc(s_tot, 1)
            pe.wait_ge(s_cell, 1)
            for k in range(6):
                last = pe.transpose(work_ps[0:GT, k * P:(k + 1) * P], gates[:, k * GT:(k + 1) * GT], ident[:, :])
            last.then_inc(s_cellT, 1)
            pe.wait_ge(s_cd, 3)
            for k in range(2):
                last = pe.matmul(work_ps[0:D, 0:D], spread[:, k, :, :].rearrange("t a k -> t (a k)"),
                                 newRT[:, k * D:(k + 1) * D], start=(k == 0), stop=(k == 1))
            last.then_inc(s_nw, 1)
            pe.wait_ge(s_cd, 4)
            pe.wait_ge(s_small, 16 * N_SMALL)
            for k in range(2):
                last = pe.transpose(work_ps[0:D, (k + 1) * D:(k + 2) * D], w_in[:, k, :], ident[0:D, 0:D])
            last.then_inc(s_nw, 1)
            pe.wait_ge(s_cd, 6)
            pe.wait_ge(s_flag, 1)
            fits = pe.value_load(flag[0:1, 0:1], min_val=0, max_val=1)
            with pe.If(fits == 1):
                fast_pe(pe)
            with pe.Else():
                general_pe(pe)


_INS = ['x', 'src', 'dst', 'edge_attr_32', 'edge_weight', 'L0_gnn_W1', 'L0_gnn_b1', 'L0_gnn_W2', 'L0_gnn_b2',
        'L1_gnn_gc_weights', 'L1_gnn_prev_weights', 'L1_gnn_w_ih', 'L1_gnn_w_hh', 'L1_gnn_b_ih', 'L1_gnn_b_hh',
        'L3_gnn_We', 'L3_gnn_be', 'L3_gnn_W1', 'L3_gnn_b1', 'L3_gnn_W2', 'L3_gnn_b2', 'L3_gnn_eps_gin',
        'L3_gnn_gamma', 'L3_gnn_beta']


def kernel(**inputs):
    import numpy as _np
    import concourse.bacc as _bacc
    from concourse import mybir as _mybir
    from concourse.bass_utils import run_bass_kernel_spmd as _run

    nc = _bacc.Bacc("TRN2", target_bir_lowering=False, num_devices=1)
    arrays, args = {}, []
    for name in _INS:
        a = _np.ascontiguousarray(inputs[name])
        if a.ndim == 0:
            a = a.reshape(1)
        arrays[f"in_{name}_dram"] = a
        args.append(nc.dram_tensor(f"in_{name}_dram", a.shape, _mybir.dt.from_np(a.dtype), kind="ExternalInput").ap())
    res = nc.dram_tensor("out_0_dram", (N, D), fp32, kind="ExternalOutput").ap()
    gnn_kernel(nc, *args, res)
    r = _run(nc, [arrays], core_ids=[0])
    return r.results[0]["out_0_dram"]
```
